# Optimizing a Trainium2 kernel written in Bass

```python
import numpy as np
import jax
import jax.numpy as jnp

def _softmax(x, axis=-1):
    return jax.nn.softmax(x, axis=axis)

def _gelu(x):
    return jax.nn.gelu(x, approximate=True)

def _silu(x):
    return jax.nn.silu(x)

def _sigmoid(x):
    return jax.nn.sigmoid(x)

def _layernorm(x, axis=-1, eps=1e-05):
    m = jnp.mean(x, axis=axis, keepdims=True)
    v = jnp.var(x, axis=axis, keepdims=True)
    return (x - m) / jnp.sqrt(v + eps)

def _scatter_add(tgt, idx, src, axis=0):
    return tgt.at[idx].add(src)

def _segment_sum(src, seg, n):
    return jax.ops.segment_sum(src, seg, n)
kernel_name = 'mk_gnn_preln_d4_gnn_r64_d5b215'

def setup_inputs(seed: int=0):
    np.random.seed(seed)
    _w = jnp.asarray

    def _rec_inputs():
        import jax
        import jax.numpy as jnp
        _gk = jax.random.key(seed)
        x = -0.0005121 + 1.001 * jax.random.normal(jax.random.fold_in(_gk, 1), (100000, 64), jnp.float32)
        src = jax.random.randint(jax.random.fold_in(_gk, 2), (50000,), 0, 100000, jnp.int32)
        dst = jnp.minimum((100000 * jax.random.uniform(jax.random.fold_in(_gk, 3), (50000,)) ** 2.0).astype(jnp.int32), 99999)
        _o = jnp.argsort(dst, stable=True)
        src = src[_o]
        dst = dst[_o]
        edge_attr_32 = -8.62073e-06 + 0.999901 * jax.random.normal(jax.random.fold_in(_gk, 11), (50000, 32), jnp.float32)
        edge_weight = jax.random.uniform(jax.random.fold_in(_gk, 13), (50000,), jnp.float32, 0.0, 0.999998)
        return (x, src, dst, edge_attr_32, edge_weight)
    x, src, dst, edge_attr_32, edge_weight = _rec_inputs()

    def _L0_gnn_setup():
        import jax, jax.numpy as jnp
        import numpy as np
        N = 50000
        E = 12500
        F_IN = 64
        F_OUT = 64
        K = 3
        HEADS = 4
        LN_EPS = 1e-05
        SM_EPS = 1e-16
        NEG_ACT = 0.01
        NEG_GAT = 0.2

        def _leaky(x, slope):
            return jnp.where(x >= 0, x, slope * x)

        def _forward(x, edge_index, edge_attr, ln_gamma, ln_beta, cheb_w, cheb_b, gat_w, att_src, att_dst, gat_b):
            n = x.shape[0]
            src, dst = (edge_index[0], edge_index[1])
            mu = jnp.mean(x, axis=-1, keepdims=True)
            var = jnp.mean(jnp.square(x - mu), axis=-1, keepdims=True)
            x = (x - mu) * jax.lax.rsqrt(var + LN_EPS) * ln_gamma + ln_beta
            deg = jax.ops.segment_sum(edge_attr, src, num_segments=n)
            dinv = jnp.where(deg > 0, 1.0 / jnp.sqrt(jnp.where(deg > 0, deg, 1.0)), 0.0)
            w = -(dinv[src] * edge_attr * dinv[dst])

            def prop(h):
                return jax.ops.segment_sum(w[:, None] * h[src], dst, num_segments=n)
            Tx0 = x
            out = Tx0 @ cheb_w[0]
            Tx1 = prop(Tx0)
            out = out + Tx1 @ cheb_w[1]
            for k in range(2, cheb_w.shape[0]):
                Tx2 = 2.0 * prop(Tx1) - Tx0
                out = out + Tx2 @ cheb_w[k]
                Tx0, Tx1 = (Tx1, Tx2)
            h = _leaky(out + cheb_b, NEG_ACT)
            H, C = att_src.shape
            xh = (h @ gat_w).reshape(n, H, C)
            a_src = jnp.sum(xh * att_src, axis=-1)
            a_dst = jnp.sum(xh * att_dst, axis=-1)
            loop = jnp.arange(n, dtype=src.dtype)
            s2 = jnp.concatenate([src, loop])
            d2 = jnp.concatenate([dst, loop])
            e = _leaky(a_src[s2] + a_dst[d2], NEG_GAT)
            emax = jax.ops.segment_max(e, d2, num_segments=n)
            ex = jnp.exp(e - emax[d2])
            denom = jax.ops.segment_sum(ex, d2, num_segments=n) + SM_EPS
            alpha = ex / denom[d2]
            o = jax.ops.segment_sum(xh[s2] * alpha[:, :, None], d2, num_segments=n)
            o = jnp.mean(o, axis=1) + gat_b
            return _leaky(o, NEG_ACT)
        key = jax.random.key(seed)
        ks = jax.random.split(key, 10)
        s = 1.0 / np.sqrt(F_IN)
        return {'x': jax.random.normal(ks[0], (N, F_IN), dtype=jnp.float32), 'edge_index': jax.random.randint(ks[1], (2, E), 0, N, dtype=jnp.int32), 'edge_attr': jax.random.uniform(ks[2], (E,), dtype=jnp.float32), 'ln_gamma': jnp.ones((F_IN,), jnp.float32), 'ln_beta': jnp.zeros((F_IN,), jnp.float32), 'cheb_w': jax.random.normal(ks[3], (K, F_IN, F_OUT), jnp.float32) * s, 'cheb_b': jax.random.normal(ks[4], (F_OUT,), jnp.float32) * 0.01, 'gat_w': jax.random.normal(ks[5], (F_OUT, HEADS * F_OUT), jnp.float32) * s, 'att_src': jax.random.normal(ks[6], (HEADS, F_OUT), jnp.float32) * s, 'att_dst': jax.random.normal(ks[7], (HEADS, F_OUT), jnp.float32) * s, 'gat_b': jax.random.normal(ks[8], (F_OUT,), jnp.float32) * 0.01}
    _L0_gnn_all = _L0_gnn_setup()
    _L0_gnn_in = {k: v for k, v in _L0_gnn_all.items() if k in ('ln_gamma', 'ln_beta', 'cheb_w', 'cheb_b', 'gat_w', 'att_src', 'att_dst', 'gat_b')}
    del _L0_gnn_all

    def _L1_gnn_setup():
        import jax, jax.numpy as jnp
        import numpy as np
        N_NODES = 100000
        N_EDGES = 15625
        NODE_DIM = 64
        EDGE_DIM = 32
        EPS = 1e-05
        SLOPE = 0.1

        def _mlp2(v, W1, b1, W2, b2):
            h = jax.nn.leaky_relu(v @ W1 + b1, negative_slope=SLOPE)
            return h @ W2 + b2
        key = jax.random.key(seed)
        ks = jax.random.split(key, 8)
        s = 0.05
        return {'x': jax.random.normal(ks[0], (N_NODES, NODE_DIM), dtype=jnp.float32), 'edge_attr': jax.random.normal(ks[1], (N_EDGES, EDGE_DIM), dtype=jnp.float32), 'W1n': jax.random.normal(ks[2], (NODE_DIM, 2 * NODE_DIM), dtype=jnp.float32) * s, 'b1n': jnp.zeros((2 * NODE_DIM,), dtype=jnp.float32), 'W2n': jax.random.normal(ks[3], (2 * NODE_DIM, NODE_DIM), dtype=jnp.float32) * s, 'b2n': jnp.zeros((NODE_DIM,), dtype=jnp.float32), 'W1e': jax.random.normal(ks[4], (EDGE_DIM, NODE_DIM), dtype=jnp.float32) * s, 'b1e': jnp.zeros((NODE_DIM,), dtype=jnp.float32), 'W2e': jax.random.normal(ks[5], (NODE_DIM, NODE_DIM), dtype=jnp.float32) * s, 'b2e': jnp.zeros((NODE_DIM,), dtype=jnp.float32), 'res_w': jnp.ones((1,), dtype=jnp.float32), 'dp_scale': jnp.ones((1,), dtype=jnp.float32), 'gamma': jnp.ones((NODE_DIM,), dtype=jnp.float32), 'beta': jnp.zeros((NODE_DIM,), dtype=jnp.float32), 'edge_index': jax.random.randint(ks[6], (2, N_EDGES), 0, N_NODES, dtype=jnp.int64) if jax.config.jax_enable_x64 else jax.random.randint(ks[6], (2, N_EDGES), 0, N_NODES, dtype=jnp.int32)}
    _L1_gnn_all = _L1_gnn_setup()
    _L1_gnn_in = {k: v for k, v in _L1_gnn_all.items() if k in ('W1n', 'b1n', 'W2n', 'b2n', 'W1e', 'b1e', 'W2e', 'b2e', 'res_w', 'dp_scale', 'gamma', 'beta')}
    del _L1_gnn_all

    def _L2_gnn_setup():
        import jax, jax.numpy as jnp
        import numpy as np
        N_NODES = 50000
        N_EDGES = 12500
        D_FEAT = 64
        key = jax.random.key(seed)
        k_x, k_e, k_w = jax.random.split(key, 3)
        x = jax.random.normal(k_x, (N_NODES, D_FEAT), dtype=jnp.float32)
        edge_index = jax.random.randint(k_e, (2, N_EDGES), 0, N_NODES, dtype=jnp.int64)
        W = jax.random.normal(k_w, (D_FEAT, D_FEAT), dtype=jnp.float32) / np.sqrt(D_FEAT)
        b = jnp.zeros((D_FEAT,), dtype=jnp.float32)
        return {'x': x, 'edge_index': edge_index, 'W': W, 'b': b}
    _L2_gnn_all = _L2_gnn_setup()
    _L2_gnn_in = {k: v for k, v in _L2_gnn_all.items() if k in ('W', 'b')}
    del _L2_gnn_all

    def _L3_gnn_setup():
        import jax, jax.numpy as jnp
        import numpy as np
        NEG_SLOPE = 0.3
        BN_EPS = 1e-05
        key = jax.random.key(seed)
        k1, k2, k3, k4 = jax.random.split(key, 4)
        N, E, IN_DIM, OUT_DIM = (50000, 12500, 64, 64)
        feature = jax.random.normal(k1, (N, IN_DIM), dtype=jnp.float32)
        edge_index = jax.random.randint(k2, (2, E), 0, N, dtype=jnp.int64)
        lim = 1.0 / np.sqrt(2 * IN_DIM)
        W = jax.random.uniform(k3, (OUT_DIM, 2 * IN_DIM), minval=-lim, maxval=lim, dtype=jnp.float32)
        b = jax.random.uniform(k4, (OUT_DIM,), minval=-lim, maxval=lim, dtype=jnp.float32)
        gamma = jnp.ones((OUT_DIM,), dtype=jnp.float32)
        beta = jnp.zeros((OUT_DIM,), dtype=jnp.float32)
        return {'feature': feature, 'edge_index': edge_index, 'W': W, 'b': b, 'gamma': gamma, 'beta': beta}
    _L3_gnn_all = _L3_gnn_setup()
    _L3_gnn_in = {k: v for k, v in _L3_gnn_all.items() if k in ('W', 'b', 'gamma', 'beta')}
    del _L3_gnn_all
    return {'x': x, 'src': src, 'dst': dst, 'edge_attr_32': edge_attr_32, 'edge_weight': edge_weight, 'L0_gnn_ln_gamma': _L0_gnn_in['ln_gamma'], 'L0_gnn_ln_beta': _L0_gnn_in['ln_beta'], 'L0_gnn_cheb_w': _L0_gnn_in['cheb_w'], 'L0_gnn_cheb_b': _L0_gnn_in['cheb_b'], 'L0_gnn_gat_w': _L0_gnn_in['gat_w'], 'L0_gnn_att_src': _L0_gnn_in['att_src'], 'L0_gnn_att_dst': _L0_gnn_in['att_dst'], 'L0_gnn_gat_b': _L0_gnn_in['gat_b'], 'L1_gnn_W1n': _L1_gnn_in['W1n'], 'L1_gnn_b1n': _L1_gnn_in['b1n'], 'L1_gnn_W2n': _L1_gnn_in['W2n'], 'L1_gnn_b2n': _L1_gnn_in['b2n'], 'L1_gnn_W1e': _L1_gnn_in['W1e'], 'L1_gnn_b1e': _L1_gnn_in['b1e'], 'L1_gnn_W2e': _L1_gnn_in['W2e'], 'L1_gnn_b2e': _L1_gnn_in['b2e'], 'L1_gnn_res_w': _L1_gnn_in['res_w'], 'L1_gnn_dp_scale': _L1_gnn_in['dp_scale'], 'L1_gnn_gamma': _L1_gnn_in['gamma'], 'L1_gnn_beta': _L1_gnn_in['beta'], 'L2_gnn_W': _L2_gnn_in['W'], 'L2_gnn_b': _L2_gnn_in['b'], 'L3_gnn_W': _L3_gnn_in['W'], 'L3_gnn_b': _L3_gnn_in['b'], 'L3_gnn_gamma': _L3_gnn_in['gamma'], 'L3_gnn_beta': _L3_gnn_in['beta']}

def reference(x, src, dst, edge_attr_32, edge_weight, L0_gnn_ln_gamma, L0_gnn_ln_beta, L0_gnn_cheb_w, L0_gnn_cheb_b, L0_gnn_gat_w, L0_gnn_att_src, L0_gnn_att_dst, L0_gnn_gat_b, L1_gnn_W1n, L1_gnn_b1n, L1_gnn_W2n, L1_gnn_b2n, L1_gnn_W1e, L1_gnn_b1e, L1_gnn_W2e, L1_gnn_b2e, L1_gnn_res_w, L1_gnn_dp_scale, L1_gnn_gamma, L1_gnn_beta, L2_gnn_W, L2_gnn_b, L3_gnn_W, L3_gnn_b, L3_gnn_gamma, L3_gnn_beta):
    import jax
    import jax.numpy as jnp

    def _L0_gnn_ref(x, edge_index, edge_attr, ln_gamma, ln_beta, cheb_w, cheb_b, gat_w, att_src, att_dst, gat_b):
        import jax, jax.numpy as jnp
        import numpy as np
        N = 50000
        E = 12500
        F_IN = 64
        F_OUT = 64
        K = 3
        HEADS = 4
        LN_EPS = 1e-05
        SM_EPS = 1e-16
        NEG_ACT = 0.01
        NEG_GAT = 0.2

        def _leaky(x, slope):
            return jnp.where(x >= 0, x, slope * x)

        def _forward(x, edge_index, edge_attr, ln_gamma, ln_beta, cheb_w, cheb_b, gat_w, att_src, att_dst, gat_b):
            n = x.shape[0]
            src, dst = (edge_index[0], edge_index[1])
            mu = jnp.mean(x, axis=-1, keepdims=True)
            var = jnp.mean(jnp.square(x - mu), axis=-1, keepdims=True)
            x = (x - mu) * jax.lax.rsqrt(var + LN_EPS) * ln_gamma + ln_beta
            deg = jax.ops.segment_sum(edge_attr, src, num_segments=n)
            dinv = jnp.where(deg > 0, 1.0 / jnp.sqrt(jnp.where(deg > 0, deg, 1.0)), 0.0)
            w = -(dinv[src] * edge_attr * dinv[dst])

            def prop(h):
                return jax.ops.segment_sum(w[:, None] * h[src], dst, num_segments=n)
            Tx0 = x
            out = Tx0 @ cheb_w[0]
            Tx1 = prop(Tx0)
            out = out + Tx1 @ cheb_w[1]
            for k in range(2, cheb_w.shape[0]):
                Tx2 = 2.0 * prop(Tx1) - Tx0
                out = out + Tx2 @ cheb_w[k]
                Tx0, Tx1 = (Tx1, Tx2)
            h = _leaky(out + cheb_b, NEG_ACT)
            H, C = att_src.shape
            xh = (h @ gat_w).reshape(n, H, C)
            a_src = jnp.sum(xh * att_src, axis=-1)
            a_dst = jnp.sum(xh * att_dst, axis=-1)
            loop = jnp.arange(n, dtype=src.dtype)
            s2 = jnp.concatenate([src, loop])
            d2 = jnp.concatenate([dst, loop])
            e = _leaky(a_src[s2] + a_dst[d2], NEG_GAT)
            emax = jax.ops.segment_max(e, d2, num_segments=n)
            ex = jnp.exp(e - emax[d2])
            denom = jax.ops.segment_sum(ex, d2, num_segments=n) + SM_EPS
            alpha = ex / denom[d2]
            o = jax.ops.segment_sum(xh[s2] * alpha[:, :, None], d2, num_segments=n)
            o = jnp.mean(o, axis=1) + gat_b
            return _leaky(o, NEG_ACT)
        return _forward(x, edge_index, edge_attr, ln_gamma, ln_beta, cheb_w, cheb_b, gat_w, att_src, att_dst, gat_b)

    def _L1_gnn_ref(x, edge_attr, W1n, b1n, W2n, b2n, W1e, b1e, W2e, b2e, res_w, dp_scale, gamma, beta, edge_index):
        import jax, jax.numpy as jnp
        import numpy as np
        N_NODES = 100000
        N_EDGES = 15625
        NODE_DIM = 64
        EDGE_DIM = 32
        EPS = 1e-05
        SLOPE = 0.1

        def _mlp2(v, W1, b1, W2, b2):
            h = jax.nn.leaky_relu(v @ W1 + b1, negative_slope=SLOPE)
            return h @ W2 + b2
        num_nodes = x.shape[0]
        x_t = _mlp2(x, W1n, b1n, W2n, b2n)
        e_t = _mlp2(edge_attr, W1e, b1e, W2e, b2e)
        src, dst = (edge_index[0], edge_index[1])
        msgs = x_t[src] * e_t * dp_scale
        aggregated = jax.ops.segment_sum(msgs, dst, num_segments=num_nodes)
        out = x + aggregated * res_w
        mu = jnp.mean(out, axis=-1, keepdims=True)
        var = jnp.mean(jnp.square(out - mu), axis=-1, keepdims=True)
        return (out - mu) * jax.lax.rsqrt(var + EPS) * gamma + beta

    def _L2_gnn_ref(x, edge_index, W, b):
        import jax, jax.numpy as jnp
        import numpy as np
        N_NODES = 50000
        N_EDGES = 12500
        D_FEAT = 64
        src = edge_index[0]
        dst = edge_index[1]
        n_nodes = x.shape[0]
        x_j = x[src]
        msg = jax.nn.relu(jnp.einsum('ed,df->ef', x_j, W) + b)
        out = jax.ops.segment_sum(msg, dst, num_segments=n_nodes)
        return out

    def _L3_gnn_ref(feature, edge_index, W, b, gamma, beta):
        import jax, jax.numpy as jnp
        import numpy as np
        NEG_SLOPE = 0.3
        BN_EPS = 1e-05
        N = feature.shape[0]
        src, dst = (edge_index[0], edge_index[1])
        x_i = feature[dst]
        x_j = feature[src]
        msg_in = jnp.concatenate([x_i, x_j - x_i], axis=-1)
        h = msg_in @ W.T + b
        mean = jnp.mean(h, axis=0)
        var = jnp.var(h, axis=0)
        h = (h - mean) * jax.lax.rsqrt(var + BN_EPS) * gamma + beta
        h = jnp.where(h >= 0, h, NEG_SLOPE * h)
        summed = jax.ops.segment_sum(h, dst, num_segments=N)
        counts = jax.ops.segment_sum(jnp.ones((h.shape[0],), h.dtype), dst, num_segments=N)
        return summed / jnp.maximum(counts, 1.0)[:, None]
    edge_index = jnp.stack([src, dst])
    h = jnp.maximum(_layernorm(x, axis=-1), 0.0)
    x = x + _L0_gnn_ref(h, edge_index, edge_weight, L0_gnn_ln_gamma, L0_gnn_ln_beta, L0_gnn_cheb_w, L0_gnn_cheb_b, L0_gnn_gat_w, L0_gnn_att_src, L0_gnn_att_dst, L0_gnn_gat_b)
    h = jnp.maximum(_layernorm(x, axis=-1), 0.0)
    x = x + _L1_gnn_ref(h, edge_attr_32, L1_gnn_W1n, L1_gnn_b1n, L1_gnn_W2n, L1_gnn_b2n, L1_gnn_W1e, L1_gnn_b1e, L1_gnn_W2e, L1_gnn_b2e, L1_gnn_res_w, L1_gnn_dp_scale, L1_gnn_gamma, L1_gnn_beta, edge_index)
    h = jnp.maximum(_layernorm(x, axis=-1), 0.0)
    x = x + _L2_gnn_ref(h, edge_index, L2_gnn_W, L2_gnn_b)
    h = jnp.maximum(_layernorm(x, axis=-1), 0.0)
    x = x + _L3_gnn_ref(h, edge_index, L3_gnn_W, L3_gnn_b, L3_gnn_gamma, L3_gnn_beta)
    return x

_drawn_inputs = setup_inputs


def setup_inputs(seed=0):
    import zlib

    import numpy as np

    out = dict(_drawn_inputs(seed))
    spreads = {'L0_gnn_ln_gamma': (1.0, 0.2),
     'L0_gnn_ln_beta': (0.0, 0.1),
     'L1_gnn_b1n': (0.0, 0.8),
     'L1_gnn_b2n': (0.0, 0.606),
     'L1_gnn_b1e': (0.0, 2.0),
     'L1_gnn_b2e': (0.0, 2.0),
     'L1_gnn_gamma': (1.0, 0.2),
     'L1_gnn_beta': (0.0, 0.1),
     'L2_gnn_b': (0.0, 0.1),
     'L3_gnn_gamma': (1.0, 0.2),
     'L3_gnn_beta': (0.0, 0.527)}
    factors = {'edge_attr_32': 8.0,
     'L0_gnn_cheb_b': 26.231,
     'L0_gnn_gat_b': 8.0,
     'L1_gnn_W1n': 7.737,
     'L1_gnn_W2n': 5.048,
     'L1_gnn_W1e': 8.0,
     'L1_gnn_W2e': 6.384,
     'L3_gnn_b': 64.0}
    for name, (base, spread) in spreads.items():
        noise = np.random.default_rng([zlib.crc32(name.encode()), seed]).standard_normal(out[name].shape)
        drawn = base * np.exp(spread * noise) if base else spread * noise
        out[name] = jnp.asarray(drawn.astype(out[name].dtype))
    for name, factor in factors.items():
        out[name] = (out[name] * factor).astype(out[name].dtype)
    return out
```

```python
from contextlib import ExitStack
import concourse.bass as bass
from concourse import mybir

ALU = mybir.AluOpType
ACT = mybir.ActivationFunctionType
F32 = mybir.dt.float32
I32 = mybir.dt.int32
BF16 = mybir.dt.bfloat16
F16 = mybir.dt.float16
U8 = mybir.dt.uint8
AX_X = mybir.AxisListType.X

P = 128
C = 64
S = 8
G_ROWS = P * S
HALF = G_ROWS // 2
EDGES, NODES = 50000, 100000
GROUPS = -(-EDGES // G_ROWS)
EP = GROUPS * G_ROWS
NODE_GROUPS = -(-NODES // G_ROWS)
NP_ = NODE_GROUPS * G_ROWS
TILES = GROUPS * S
HEADS = 4
EDIM = 32
LO_BITS = 10
LO = 1 << LO_BITS
HI = NP_ // LO
NOWHERE = 1.0e6
FAR = 1.0e30
EPS = 1e-5
PARTS = 5
CHUNK = EP // P
EXCHANGES = (4, 4, 4, 4, 4)
BN_STEPS = 10
PREP_STEPS = 24
ODD_EVEN = (16 * ((GROUPS + 1) // 2), 16 * (GROUPS // 2))
IMM = dict(bounds_check=EP - 1, oob_is_err=False)


def paired_loop(eng, n, first, second=None):
    def two(f, i, par):
        f(i, par, i * 2 + par)

    def step(i):
        two(first, i, 1)
        if second:
            two(second, i, 0)
        two(first, i + 1, 0)
        if second:
            two(second, i, 1)

    two(first, 0, 0)
    pairs = (n - 1) // 2
    with eng.Fori(0, pairs) as i:
        step(i)
    if n % 2 == 0:
        two(first, pairs, 1)
    if second:
        two(second, pairs, 0)
        if n % 2 == 0:
            two(second, pairs, 1)


def hold(eng, sem, value):
    eng.wait_ge(sem, value)
    eng.sem_inc(HELD[0], 1)


HELD = [None]


class Norm:

    def __init__(self, sem, name, per):
        self.per = per
        self.step = sem(name + "_dve_step")
        self.centred = sem(name + "_centred")
        self.squared = sem(name + "_squared")
        self.varied = sem(name + "_variance")
        self.rooted = sem(name + "_rooted")

    def dve(self, nc, dve, g, k, x, b):
        n = g * self.per + k
        nc.vector.reduce_sum(b.mean, x, AX_X).then_inc(self.step, 1)
        dve.wait_ge(self.step, n * 4 + 1)
        nc.vector.tensor_scalar(b.mean, b.mean, -1.0 / C, None, ALU.mult).then_inc(self.step, 1)
        dve.wait_ge(self.step, n * 4 + 2)
        nc.vector.tensor_tensor(b.xc, x, spread(b.mean), ALU.add).then_inc(self.centred, 1)
        dve.wait_ge(self.squared, n + 1)
        nc.vector.reduce_sum(b.var, b.sq, AX_X).then_inc(self.step, 1)
        dve.wait_ge(self.step, n * 4 + 3)
        nc.vector.tensor_scalar(b.var, b.var, 1.0 / C, EPS, ALU.mult, ALU.add).then_inc(self.varied, 1)
        dve.wait_ge(self.rooted, n + 1)
        nc.vector.reciprocal(b.rstd, b.sd).then_inc(self.step, 1)
        dve.wait_ge(self.step, n * 4 + 4)

    def act(self, nc, act, g, k, b):
        n = g * self.per + k
        act.wait_ge(self.centred, n + 1)
        nc.scalar.activation(b.sq, b.xc, ACT.Square).then_inc(self.squared, 1)
        act.wait_ge(self.varied, n + 1)
        nc.scalar.activation(b.sd, b.var, ACT.Sqrt).then_inc(self.rooted, 1)


def norm_bufs(t, name):
    b = Bufs()
    b.xc, b.sq = t(name + "_xc", [P, S, C])[:], t(name + "_sq", [P, S, C])[:]
    b.mean, b.var, b.sd, b.rstd = (t(name + "_" + n, [P, S])[:] for n in ("mean", "var", "sd", "rstd"))
    return b


def group_rows(a):
    return a.rearrange("(g p s) c -> g p s c", p=P, s=S)


def group_cols(a):
    return a.rearrange("f (g e) -> g f e", e=G_ROWS)


def slot_cols(n):
    at = (n % 2) * HALF + (n // 2) * P
    return slice(at, at + P)


def transpose_rows(nc, out, rows, W):
    for n in range(S):
        last = nc.tensor.transpose(out[0:C, slot_cols(n)], rows[:, n], W.ident[:])
    return last


def transpose_pairs(nc, out, rows, W):
    flat = rows.rearrange("p s c -> p (s c)")
    for n in range(S // 2):
        last = nc.tensor.transpose(out[:, P * n:P * n + P], flat[:, P * n:P * n + P], W.ident[:])
    return last


def transpose_back(nc, out, columns, W):
    for n in range(S):
        last = nc.tensor.transpose(out[:, C * n:C * n + C], columns[:, slot_cols(n)], W.ident[0:C, 0:C])
    return last


def halves(nc, out, weights, paired):
    for h in (0, 1):
        last = nc.tensor.matmul(out[:, HALF * h:HALF * h + HALF], weights[:, h], paired, start=True, stop=True)
    return last


def leaky_parts(nc, out, x, slope, bias=None, rest=None):
    b = dict(bias=bias) if bias is not None else {}
    r = dict(bias=rest) if rest is not None else {}
    nc.scalar.activation(out[0], x, ACT.Identity, scale=slope, **b)
    return nc.scalar.activation(out[1], x, ACT.Relu, scale=1.0 - slope, **r)


def sum_transposed(nc, out, parts, W, n):
    k = parts[0].shape[0]
    for q in range(n):
        at = slice(P * q, P * q + P) if n < S else slot_cols(q)
        for j in (0, 1):
            last = nc.tensor.matmul(out[:, k * q:k * q + k], parts[j][:, at], W.ident[0:k, 0:k],
                                    start=j == 0, stop=j == 1)
    return last


def as_rows(x):
    return x.rearrange("p (s c) -> p s c", c=C)


def spread(v):
    return v.unsqueeze(2).to_broadcast([P, S, C])


def along(v):
    return v.unsqueeze(1).to_broadcast([P, S, C])


class Bufs:
    pass


def build(nc, A, out):
    ctx = ExitStack()
    with ctx:
        def sb(name, shape, dt=F32):
            return ctx.enter_context(nc.sbuf_tensor(name, shape, dt))

        def sem(name):
            return ctx.enter_context(nc.semaphore(name))

        def dram(name, shape, dt=F32):
            return nc.dram_tensor(name, shape, dt, kind=KIND).ap()

        KIND = "Internal"
        ps = ctx.enter_context(nc.psum_tensor("ps", [P, 4096], F32))
        bank = lambda n, k=1: ps[:, 512 * n:512 * (n + k)]

        D = Bufs()
        (D.xs, D.xd, D.t0s, D.h_lone, D.x1_lone, D.x2_lone, D.tx1, D.hd, D.hs, D.x1d, D.x2d, D.x3d) = (
            dram("d_" + name, (EP, C)) for name in
            ("xs", "xd", "t0s", "h_lone", "x1_lone", "x2_lone", "tx1", "hd", "hs", "x1d", "x2d", "x3d"))
        D.table = dram("d_table", (NP_, 2))
        D.ls = dram("d_ls", (GROUPS, P, S), I32)
        D.final_idx = dram("d_final_idx", (GROUPS, P, S), I32)
        D.et = dram("d_et", (C, EP))
        D.pd = dram("d_pd", (C, EP))
        D.hh = dram("d_hh", (C, EP))
        D.att_s = dram("d_att_s", (HEADS, EP))
        D.att_d = dram("d_att_d", (2 * HEADS, EP))
        D.alpha = dram("d_alpha", (2 * HEADS, EP))
        grp = lambda a: a.rearrange("(g p s) c -> g p s c", p=P, s=S)
        cols = lambda a: a.rearrange("f (g e) -> g f e", e=G_ROWS)

        W = Bufs()
        W.ident = sb("ident", [P, P])
        W.w02 = sb("w02", [P, P])
        W.w02_half = sb("w02_half", [P, 2, C])
        W.w1 = sb("w1", [C, C])
        W.w2x2 = sb("w2x2", [C, C])
        W.gmean = sb("gmean", [P, P])
        W.gatw = sb("gatw", [P, 2, C])
        W.att = sb("att", [C, 2, HEADS])
        W.att_half = sb("att_half", [P, 2, HEADS])
        W.w1n = sb("w1n", [P, 2, P])
        W.w2n = sb("w2n", [P, C])
        W.w1e = sb("w1e", [EDIM, C])
        W.w2e = sb("w2e", [C, C])
        W.l2w = sb("l2w", [P, 2, C])
        W.l3b = sb("l3b", [P, 2, C])
        W.l3ab = sb("l3ab", [P, 2, C])
        W.vecs = sb("vecs", [P, 16])
        VEC = ("cheb_b", "gat_b", "b1n", "b1e", "ln_gamma", "ln_beta", "b2n", "b2e", "dp", "res", "l2b",
               "l3b", "bn_gamma", "bn_beta")
        W.slanted = sb("slanted", [P, 2, 4])
        col = {n: W.vecs[:, i:i + 1] for i, n in enumerate(VEC)}
        for i, n in enumerate(VEC[:4]):
            col[n + "_slope"], col[n + "_rest"] = W.slanted[:, 0, i:i + 1], W.slanted[:, 1, i:i + 1]
        W.rows = sb("rowvecs", [P, 4, C])
        srcE = sb("srcE", [P, GROUPS, S], I32)
        dstE = sb("dstE", [P, GROUPS, S], I32)
        lastE = sb("lastE", [P, GROUPS, S])
        ewE = sb("ewE", [P, GROUPS, S])
        wE = sb("wE", [P, GROUPS, S])
        same = sb("same", [C, EP + 1], U8)

        with ExitStack() as loc:
            t = lambda n, sh, dt=F32: loc.enter_context(nc.sbuf_tensor(n, sh, dt))
            loaded, stepped, consts, masks_in0, masks_in1, masks_used = map(sem, (
                "weights_loaded", "prep_step", "pool_consts", "masks_loaded0", "masks_loaded1", "masks_used"))
            gw2 = t("gw2", [P, HEADS, C])
            chw = t("chw", [P, 3, C])
            attb = t("attb", [C, 2, HEADS, C])
            prod = t("attprod", [C, 2, HEADS, C])
            dnE = t("dnE", [P, GROUPS, S], I32)
            idx0 = t("finidx", [P, GROUPS, S])
            idx0i = t("finidxi", [P, GROUPS, S], I32)
            l3a = t("l3a", [P, C])
            pairrow = t("pairrow", [C, 2, 2, G_ROWS], I32)
            linear = A["dst_line"]
            n_loads = [0]
            fin_st = sem("final_idx_stored")
            with nc.Block() as block:
                @block.sync
                def _(sp):
                    def ld(o, i):
                        n_loads[0] += 1
                        sp.dma_start(o, i).then_inc(loaded, 16)
                    sp.wait_ge(consts, 1)
                    for h in (0, 1):
                        lanes = slice(C * h, C * h + C)
                        ld(gw2[lanes], A["L0_gnn_gat_w"].rearrange("k (h f) -> k h f", h=HEADS))
                        ld(chw[lanes], A["L0_gnn_cheb_w"].rearrange("k i o -> i k o"))
                        ld(W.w1n[lanes, h, :], A["L1_gnn_W1n"])
                        ld(W.l2w[lanes, h, :], A["L2_gnn_W"])
                        ld(W.l3b[lanes, h, :], A["l3_wt"][C:2 * C, :])
                        ld(l3a[lanes], A["l3_wt"][0:C, :])
                        for n, name in (("ln_gamma", "L0_gnn_ln_gamma"), ("ln_beta", "L0_gnn_ln_beta"),
                                        ("cheb_b", "L0_gnn_cheb_b"), ("gat_b", "L0_gnn_gat_b"),
                                        ("b2n", "L1_gnn_b2n"), ("b1e", "L1_gnn_b1e"), ("b2e", "L1_gnn_b2e"),
                                        ("l2b", "L2_gnn_b"), ("l3b", "L3_gnn_b"),
                                        ("bn_gamma", "L3_gnn_gamma"), ("bn_beta", "L3_gnn_beta")):
                            ld(col[n][lanes], A[name].rearrange("(c a) -> c a", a=1))
                    ld(col["b1n"], A["L1_gnn_b1n"].rearrange("(c a) -> c a", a=1))
                    ld(col["dp"], A["L1_gnn_dp_scale"].rearrange("(c a) -> c a", a=1).to_broadcast([P, 1]))
                    ld(col["res"], A["L1_gnn_res_w"].rearrange("(c a) -> c a", a=1).to_broadcast([P, 1]))
                    ld(W.w1[:], A["L0_gnn_cheb_w"][1])
                    ld(W.w2x2[:], A["L0_gnn_cheb_w"][2])
                    for q in (0, 1):
                        ld(W.gatw[C * q:C * q + C], A["L0_gnn_gat_w"].rearrange("k (a b f) -> b k a f", a=2, b=2)[q])
                    for q, name in enumerate(("L0_gnn_att_src", "L0_gnn_att_dst")):
                        ld(attb[:, q], A[name].unsqueeze(0).to_broadcast([C, HEADS, C]))
                    ld(W.w2n[:], A["L1_gnn_W2n"])
                    ld(W.w1e[:], A["L1_gnn_W1e"])
                    ld(W.w2e[:], A["L1_gnn_W2e"])
                    for q, name in enumerate(("L0_gnn_ln_gamma", "L0_gnn_ln_beta", "L1_gnn_gamma", "L1_gnn_beta")):
                        ld(W.rows[:, q], A[name].unsqueeze(0).to_broadcast([P, C]))
                    ld(srcE[:], A["src_rows"].rearrange("g p s -> p g s"))
                    ld(dstE[:], A["dst_rows"].rearrange("g p s -> p g s"))
                    ld(dnE[:], A["next_rows"].rearrange("g p s -> p g s"))
                    ld(ewE[:], A["ew_rows"].rearrange("g p s -> p g s"))

                    def load(i, par, g):
                        sp.wait_ge(masks_used, g + 1)
                        for q in (0, 1):
                            at = g * G_ROWS + (1 - q)
                            sp.dma_start(pairrow[:, par, q], linear[:, bass.ds(at, G_ROWS)].to_broadcast([C, G_ROWS])
                                         ).then_inc((masks_in0, masks_in1)[par], 16)
                    paired_loop(sp, GROUPS, load)
                    sp.wait_ge(stepped, PREP_STEPS)
                    sp.dma_start(D.final_idx.rearrange("g p s -> p g s"), idx0i[:]).then_inc(fin_st, 16)
                    sp.wait_ge(fin_st, 16)

                @block.gpsimd
                def _(pool):
                    for x in (W.w02, W.w02_half, W.gmean, W.w1n, W.l2w, W.l3b, W.l3ab, W.att_half, W.vecs):
                        last = nc.gpsimd.memset(x[:], 0.0)
                    last.then_inc(consts, 1)
                    nc.gpsimd.memset(W.ident[:], 0.0).then_inc(consts, 1)
                    pool.wait_ge(consts, 2)
                    nc.gpsimd.affine_select(out=W.ident[:], in_=W.ident[:], compare_op=ALU.not_equal, fill=1.0,
                                            base=0, pattern=[[-1, P]], channel_multiplier=1).then_inc(consts, 1)

                @block.vector
                def _(dve):
                    dve.sem_inc(masks_used, 2)
                    n = [0]

                    def done(ins):
                        n[0] += 1
                        ins.then_inc(stepped, 1)

                    def wait():
                        dve.wait_ge(stepped, n[0])
                    dve.wait_ge(loaded, 16 * n_loads[0])
                    dve.wait_ge(consts, 1)
                    for h in (0, 1):
                        lanes, out_cols = slice(C * h, C * h + C), slice(C * h, C * h + C)
                        done(nc.vector.tensor_tensor(W.w02[lanes, out_cols], chw[lanes, 0], chw[lanes, 2], ALU.subtract))
                        done(nc.vector.tensor_tensor(W.w02_half[lanes, h], chw[lanes, 0], chw[lanes, 2], ALU.subtract))
                        done(nc.vector.tensor_tensor(W.l3ab[lanes, h], l3a[lanes], W.l3b[lanes, h], ALU.subtract))
                        done(nc.vector.reduce_sum(W.gmean[lanes, out_cols], gw2[lanes].rearrange("k h f -> k f h"), AX_X))
                    for at, slope in ((0, 0.01), (2, 0.1)):
                        for k, f in enumerate((slope, 1.0 - slope)):
                            done(nc.vector.tensor_scalar(W.slanted[:, k, at:at + 2], W.vecs[:, at:at + 2], f, None, ALU.mult))
                    wait()
                    done(nc.vector.tensor_scalar(W.gmean[:], W.gmean[:], 1.0 / HEADS, None, ALU.mult))
                    done(nc.vector.tensor_scalar(W.gatw[:], W.gatw[:], 1.0 / HEADS, None, ALU.mult))
                    done(nc.vector.tensor_scalar(W.w2x2[:], W.w2x2[:], 2.0, None, ALU.mult))
                    for q in (0, 1):
                        done(nc.vector.tensor_tensor(prod[:, q], gw2[0:C], attb[:, q], ALU.mult))
                    wait()
                    for q in (0, 1):
                        done(nc.vector.reduce_sum(W.att[:, q], prod[:, q], AX_X))
                    wait()
                    done(nc.vector.tensor_copy(W.att_half[0:C, 0], W.att[:, 0]))
                    done(nc.vector.tensor_copy(W.att_half[C:P, 1], W.att[:, 0]))
                    done(nc.vector.tensor_tensor(lastE[:], dstE[:], dnE[:], ALU.not_equal))
                    wait()
                    done(nc.vector.tensor_scalar(idx0[:], lastE[:], -NOWHERE, NOWHERE, ALU.mult, ALU.add))
                    wait()
                    done(nc.vector.tensor_tensor(idx0i[:], idx0[:], dstE[:], ALU.add))
                    wait()
                    assert n[0] == PREP_STEPS, n[0]
                    nc.vector.memset(same[:, EP:EP + 1], 0)

                    def mask(i, par, g):
                        dve.wait_ge((masks_in0, masks_in1)[par], i * 32 + 32)
                        nc.vector.tensor_tensor(same[:, bass.ds(g * G_ROWS, G_ROWS)], pairrow[:, par, 0],
                                                pairrow[:, par, 1], ALU.is_equal).then_inc(masks_used, 1)
                    paired_loop(dve, GROUPS, mask)
        def phase(part, *args):
            own = []

            def new(name):
                own.append(nc.alloc_semaphore(name=name))
                return own[-1]
            HELD[0] = new("held_" + part.__name__)
            part(nc, A, new, *args)
            nc.clear_and_free_semaphores(own)
            nc.all_engine_barrier()

        W.col, W.ewE, W.wE, W.same = col, ewE, wE, same
        phase(degrees, W, D, bank, srcE, dstE, lastE, ewE)
        phase(lone_states, W, D, bank, out)
        phase(first_propagation, W, D, bank)
        phase(second_propagation, W, D, bank)
        phase(attention_sources, W, D, bank)
        phase(edge_terms, W, D, bank)
        phase(attention_weights, W, D, bank)
        phase(attention_sums, W, D, bank)
        phase(gated_messages, W, D, bank)
        phase(relu_messages, W, D, bank)
        stats = sb("bn_stats", [C, 2 * GROUPS * 6])
        phase(edge_convolution, W, D, bank, stats)
        phase(finish_rows, W, D, bank, out, stats)


def degrees(nc, A, sem, W, D, bank, srcE, dstE, lastE, ewE):
    ctx = ExitStack()
    with ctx:
        t = lambda n, sh, dt=F32: ctx.enter_context(nc.sbuf_tensor(n, sh, dt))
        hiS, loS, hiD, loD = (t(n, [P, GROUPS, S]) for n in ("hiS", "loS", "hiD", "loD"))
        posI, tmpI = t("posI", [P, GROUPS, S], I32), t("tmpI", [P, GROUPS, S], I32)
        posF, rem = t("posF", [P, GROUPS, S]), t("rem", [P, GROUPS, S])
        part = t("part", [P, GROUPS, S])
        vals = t("vals", [P, GROUPS, S, PARTS], BF16)
        iota_i = t("iota_i", [P, LO], I32)
        iota_hi = t("iota_hi", [P, P], BF16)
        iota_lo = t("iota_lo", [P, LO], F16)
        hot_w = t("hot_w", [P, 2, 3, P], BF16)
        hot_p = t("hot_p", [P, 2, 2, P], BF16)
        hot_lo = t("hot_lo", [P, 2, 2, LO], BF16)
        zero = t("zero_bf", [P, P], BF16)
        deg = t("deg", [P, LO])
        msk = t("degmask", [P, LO])
        tab = t("tab", [P, LO, 2])
        rows = t("gathered", [P, 2, S, C])
        near = [t(f"near{k}", [P, 2, S], I32) for k in (0, 1)]
        (pool_ready, dstep, guarded, hots, products, rooted, table_st, g_in0, g_in1, st0, st1) = map(sem, (
            "iotas", "degree_step", "degree_guarded", "onehots_built", "products_done", "degree_rooted", "table_stored",
            "rows_gathered0", "rows_gathered1", "rows_stored0", "rows_stored1"))
        gin, st = (g_in0, g_in1), (st0, st1)
        id_in = (sem("indices_loaded0"), sem("indices_loaded1"))
        grp = lambda a: a.rearrange("(g p s) c -> g p s c", p=P, s=S)
        N_STEPS = []
        with nc.Block() as block:
            @block.gpsimd
            def _(pool):
                nc.gpsimd.iota(posI[:], pattern=[[G_ROWS, GROUPS], [1, S]], base=1, channel_multiplier=S)
                nc.gpsimd.iota(iota_i[:], pattern=[[1, LO]], base=0, channel_multiplier=0)
                nc.gpsimd.memset(zero[:], 0.0).then_inc(pool_ready, 1)
                for k, ids in enumerate((near[0], near[1])):
                    def gather(i, par, g):
                        hold(pool, id_in[par], i * 16 + k * ODD_EVEN[par] + 16)
                        hold(pool, st[par], i * 16 + k * ODD_EVEN[par] + 16)
                        for q in range(S):
                            pool.indirect_dma_start(
                                out=rows[:, par, q], out_offset=None, in_=A["x"],
                                in_offset=bass.IndirectOffsetOnAxis(ap=ids[:, par, q:q + 1], axis=0),
                                bounds_check=NP_ - 1, oob_is_err=False).then_inc(gin[par], 16)
                    paired_loop(pool, GROUPS, gather)

            @block.vector
            def _(dve):
                n = [0]

                def done(ins):
                    n[0] += 1
                    ins.then_inc(dstep, 1)

                def wait():
                    dve.wait_ge(dstep, n[0])
                dve.wait_ge(pool_ready, 1)
                done(nc.vector.tensor_copy(iota_hi[:], iota_i[:, 0:P]))
                done(nc.vector.tensor_copy(iota_lo[:], iota_i[:]))
                for ids, hi, lo in ((srcE, hiS, loS), (dstE, hiD, loD)):
                    done(nc.vector.tensor_scalar(tmpI[:], ids[:], LO_BITS, None, ALU.logical_shift_right))
                    wait()
                    done(nc.vector.tensor_copy(hi[:], tmpI[:]))
                    wait()
                    done(nc.vector.tensor_scalar(tmpI[:], ids[:], LO - 1, None, ALU.bitwise_and))
                    wait()
                    done(nc.vector.tensor_copy(lo[:], tmpI[:]))
                    wait()
                done(nc.vector.tensor_copy(rem[:], ewE[:]))
                for k in range(3):
                    wait()
                    done(nc.vector.tensor_copy(vals[:, :, :, k], rem[:]))
                    wait()
                    if k < 2:
                        done(nc.vector.tensor_copy(part[:], vals[:, :, :, k]))
                        wait()
                        done(nc.vector.tensor_tensor(rem[:], rem[:], part[:], ALU.subtract))
                for k, (bits) in enumerate((0xFF00, 0xFF)):
                    done(nc.vector.tensor_scalar(tmpI[:], posI[:], bits, None, ALU.bitwise_and))
                    wait()
                    done(nc.vector.tensor_copy(posF[:], tmpI[:]))
                    wait()
                    done(nc.vector.tensor_tensor(vals[:, :, :, 3 + k], posF[:], lastE[:], ALU.mult))
                wait()
                hs, ls, hd, ld = (x[:].rearrange("p g s -> p (g s)") for x in (hiS, loS, hiD, loD))
                v = vals[:].rearrange("p g s k -> p (g s) k")
                wide = lambda x, k: x.unsqueeze(1).to_broadcast([P, k, P])
                dve.sem_inc(products, 2)

                def hot(i, par, tile):
                    dve.wait_ge(products, tile + 1)
                    one = bass.ds(tile, 1)
                    vt = v[:, one, :].rearrange("p a k -> p (a k)")
                    nc.vector.scalar_tensor_tensor(
                        out=hot_w[:, par], in0=wide(iota_hi[:], 3), scalar=hs[:, one],
                        in1=vt[:, 0:3].unsqueeze(2).to_broadcast([P, 3, P]), op0=ALU.is_equal, op1=ALU.mult)
                    nc.vector.scalar_tensor_tensor(
                        out=hot_p[:, par], in0=wide(iota_hi[:], 2), scalar=hd[:, one],
                        in1=vt[:, 3:5].unsqueeze(2).to_broadcast([P, 2, P]), op0=ALU.is_equal, op1=ALU.mult)
                    nc.vector.tensor_scalar(hot_lo[:, par, 0], iota_lo[:], ls[:, one], None, ALU.is_equal)
                    nc.vector.tensor_scalar(hot_lo[:, par, 1], iota_lo[:], ld[:, one], None,
                                            ALU.is_equal).then_inc(hots, 1)
                paired_loop(dve, TILES, hot)
                dve.wait_ge(products, TILES + 3)
                done(nc.vector.tensor_scalar(msk[:], bank(0, 2), 0.0, None, ALU.is_gt))
                done(nc.vector.tensor_scalar(deg[:], bank(0, 2), 0.0, None, ALU.is_le))
                wait()
                done(nc.vector.tensor_tensor(tab[:, :, 0], msk[:], bank(0, 2), ALU.mult))
                wait()
                nc.vector.tensor_tensor(deg[:], deg[:], tab[:, :, 0], ALU.add).then_inc(guarded, 1)
                dve.wait_ge(rooted, 1)
                done(nc.vector.reciprocal(deg[:], tab[:, :, 1]))
                wait()
                done(nc.vector.tensor_tensor(tab[:, :, 0], deg[:], msk[:], ALU.mult))
                wait()
                done(nc.vector.tensor_scalar(msk[:], bank(2, 2), 0.0, NOWHERE, ALU.is_le, ALU.mult))
                wait()
                done(nc.vector.scalar_tensor_tensor(out=deg[:], in0=bank(2, 2), scalar=-1.0, in1=msk[:],
                                                    op0=ALU.add, op1=ALU.add))
                wait()
                done(nc.vector.tensor_copy(tab[:, :, 1].bitcast(I32), deg[:]))
                N_STEPS.append(n[0])

            @block.tensor
            def _(pe):
                pe.wait_ge(pool_ready, 1)
                for b in range(4):
                    nc.tensor.matmul(bank(b), zero[0:1, :], zero[0:1, 0:1].to_broadcast([1, 512]), start=True, stop=False)

                def product(i, par, tile):
                    hold(pe, hots, tile + 1)
                    for k in range(3):
                        for h in (0, 1):
                            last = nc.tensor.matmul(bank(h), hot_w[:, par, k], hot_lo[:, par, 0, 512 * h:512 * h + 512],
                                                    start=False, stop=False)
                    for k in range(2):
                        for h in (0, 1):
                            last = nc.tensor.matmul(bank(2 + h), hot_p[:, par, k],
                                                    hot_lo[:, par, 1, 512 * h:512 * h + 512], start=False, stop=False)
                    last.then_inc(products, 1)
                paired_loop(pe, TILES, product)
                for b in range(4):
                    last = nc.tensor.matmul(bank(b), zero[0:1, :], zero[0:1, 0:1].to_broadcast([1, 512]), start=False, stop=True)
                last.then_inc(products, 1)

            @block.scalar
            def _(act):
                act.wait_ge(guarded, 1)
                nc.scalar.activation(tab[:, :, 1], deg[:], ACT.Sqrt).then_inc(rooted, 1)

            @block.sync
            def _(sp):
                for par in (0, 1):
                    sp.sem_inc(st[par], 16)
                for k, (ids, dest) in enumerate((("src_rows", D.xs), ("dst_rows", D.xd))):
                    def load(i, par, g):
                        sp.wait_ge(st[par], i * 16 + k * ODD_EVEN[par] + 16)
                        sp.dma_start(near[k][:, par], A[ids][g]).then_inc(id_in[par], 16)

                    def store(i, par, g):
                        sp.wait_ge(gin[par], (i * 16 + k * ODD_EVEN[par] + 16) * S)
                        sp.dma_start(grp(dest)[g], rows[:, par]).then_inc(st[par], 16)
                    paired_loop(sp, GROUPS, load, store)
                for par in (0, 1):
                    sp.wait_ge(st[par], 2 * ODD_EVEN[par] + 16)
                sp.wait_ge(dstep, N_STEPS[0])
                sp.dma_start(D.table.rearrange("(h l) c -> h l c", l=LO), tab[0:HI]).then_inc(table_st, 16)
                sp.wait_ge(table_st, 16)



def lone_states(nc, A, sem, W, D, bank, out):
    ctx = ExitStack()
    with ctx:
        t = lambda n, sh, dt=F32: ctx.enter_context(nc.sbuf_tensor(n, sh, dt))
        col = W.col
        x, t0, hb, x1, x2 = (t("lone_" + n, [P, 2, S, C]) for n in ("x", "t0", "hb", "x1", "x2"))
        h0, h1, x1b = (t("lone_" + n, [P, S, C]) for n in ("h0", "h1", "x1b"))
        t0f = t("lone_t0f", [P, HALF])
        hf, uf = ([t(f"lone_{n}{k}", [P, HALF])[:] for k in (0, 1)] for n in ("hf", "uf"))
        na, nb = norm_bufs(t, "lone_a"), norm_bufs(t, "lone_b")
        norm_a, norm_b = Norm(sem, "lone_a", 2), Norm(sem, "lone_b", 2)
        names = ("x_in0", "x_in1", "h0_done", "t0_done", "transposed", "affine_done", "base_done", "h_done",
                 "mean_done", "u_done", "back_done", "x1_done", "h1_done", "y_step", "x2_done", "stored0", "stored1")
        m = {n: sem("lone_" + n) for n in names}
        x_in, stored = (m["x_in0"], m["x_in1"]), (m["stored0"], m["stored1"])
        runs = ((0, NODE_GROUPS, A["x"], 1, 0), (NODE_GROUPS, GROUPS, D.xs, 4, NODE_GROUPS // 2))
        assert NODE_GROUPS % 2 == 0
        with nc.Block() as block:
            @block.sync
            def _(sp):
                for par in (0, 1):
                    sp.sem_inc(stored[par], 16)
                for g0, count, source, n_st, st0 in runs:
                    def load(i, par, g):
                        sp.wait_ge(m["x2_done"], g + g0 + 1)
                        sp.dma_start(x[:, par], group_rows(source)[g]).then_inc(x_in[par], 16)

                    def store(i, par, g):
                        sp.wait_ge(m["x2_done"], g + g0 + 3)
                        if n_st == 1:
                            sp.dma_start(group_rows(out)[g], x2[:, par]).then_inc(stored[par], 16)
                        else:
                            for d, b in ((D.t0s, t0), (D.h_lone, hb), (D.x1_lone, x1), (D.x2_lone, x2)):
                                sp.dma_start(group_rows(d)[g], b[:, par]).then_inc(stored[par], 16)
                    paired_loop(sp, count, load, store)
                for par in (0, 1):
                    sp.wait_ge(stored[par], 16 + 16 * (NODE_GROUPS // 2) + 4 * ODD_EVEN[par])

            @block.vector
            def _(dve):
                dve.sem_inc(m["x2_done"], 2)
                for g0, count, source, n_st, st0 in runs:
                    def first(i, par, g):
                        n = g + g0
                        dve.wait_ge(x_in[par], (i + g0 // 2) * 16 + 16)
                        dve.wait_ge(stored[par], i * 16 * n_st + 16 * st0 + 16)
                        norm_a.dve(nc, dve, n, 0, x[:, par], na)
                        nc.vector.scalar_tensor_tensor(out=h0[:], in0=na.xc[:], scalar=0.0, in1=spread(na.rstd[:]),
                                                       op0=ALU.max, op1=ALU.mult).then_inc(m["h0_done"], 1)
                        dve.wait_ge(m["h0_done"], n + 1)
                        norm_a.dve(nc, dve, n, 1, h0[:], na)
                        nc.vector.tensor_tensor(t0[:, par], na.xc[:], spread(na.rstd[:]), ALU.mult
                                                ).then_inc(m["t0_done"], 1)

                    def second(i, par, g):
                        n = g + g0
                        dve.wait_ge(m["back_done"], n + 1)
                        if n_st > 1:
                            nc.vector.tensor_copy(hb[:, par], as_rows(bank(5 + par)))
                        nc.vector.tensor_tensor(x1[:, par], x[:, par], as_rows(bank(1 + 3 * par)), ALU.add
                                                ).then_inc(m["x1_done"], 1)
                        dve.wait_ge(m["x1_done"], n + 1)
                        norm_b.dve(nc, dve, n, 0, x1[:, par], nb)
                        nc.vector.scalar_tensor_tensor(out=h1[:], in0=nb.xc[:], scalar=0.0, in1=spread(nb.rstd[:]),
                                                       op0=ALU.max, op1=ALU.mult).then_inc(m["h1_done"], 1)
                        dve.wait_ge(m["h1_done"], n + 1)
                        norm_b.dve(nc, dve, n, 1, h1[:], nb)
                        affine_residual(nc, dve, n, m["y_step"], nb, W, h1, x1b, x1[:, par], x2[:, par]
                                        ).then_inc(m["x2_done"], 1)
                    paired_loop(dve, count, first, second)

            @block.tensor
            def _(pe):
                for g0, count, source, n_st, st0 in runs:
                    def work(i, par, g):
                        n = g + g0
                        hold(pe, m["t0_done"], n + 1)
                        transpose_pairs(nc, bank(0), t0[:, par], W).then_inc(m["transposed"], 1)
                        hold(pe, m["affine_done"], n + 1)
                        nc.tensor.matmul(bank(2), W.w02[:], t0f[:], start=True, stop=True).then_inc(m["base_done"], 1)
                        hold(pe, m["h_done"], n + 1)
                        for k in (0, 1):
                            last = nc.tensor.matmul(bank(3), W.gmean[:], hf[k], start=k == 0, stop=k == 1)
                        last.then_inc(m["mean_done"], 1)
                        if n_st > 1:
                            sum_transposed(nc, bank(5 + par), hf, W, S // 2)
                        hold(pe, m["u_done"], n + 1)
                        sum_transposed(nc, bank(1 + 3 * par), uf, W, S // 2).then_inc(m["back_done"], 1)
                    paired_loop(pe, count, work)

            @block.scalar
            def _(act):
                for g0, count, source, n_st, st0 in runs:
                    def first(i, par, g):
                        n = g + g0
                        norm_a.act(nc, act, n, 0, na)
                        norm_a.act(nc, act, n, 1, na)
                        act.wait_ge(m["transposed"], n + 1)
                        nc.scalar.activation(t0f[:], bank(0), ACT.Identity, bias=col["ln_beta"],
                                             scale=col["ln_gamma"]).then_inc(m["affine_done"], 1)
                        act.wait_ge(m["base_done"], n + 1)
                        leaky_parts(nc, hf, bank(2), 0.01, col["cheb_b_slope"], col["cheb_b_rest"]
                                    ).then_inc(m["h_done"], 1)
                        act.wait_ge(m["mean_done"], n + 1)
                        leaky_parts(nc, uf, bank(3), 0.01, col["gat_b_slope"], col["gat_b_rest"]
                                    ).then_inc(m["u_done"], 1)

                    def second(i, par, g):
                        norm_b.act(nc, act, g + g0, 0, nb)
                        norm_b.act(nc, act, g + g0, 1, nb)
                    paired_loop(act, count, first, second)


def affine_residual(nc, dve, n, step, b, W, y, xb, x, out):
    nc.vector.tensor_tensor(y[:], b.xc[:], spread(b.rstd[:]), ALU.mult).then_inc(step, 1)
    nc.vector.tensor_tensor(xb[:], x, along(W.rows[:, 3]), ALU.add).then_inc(step, 1)
    dve.wait_ge(step, n * 3 + 2)
    nc.vector.tensor_tensor(y[:], y[:], along(W.rows[:, 2]), ALU.mult).then_inc(step, 1)
    dve.wait_ge(step, n * 3 + 3)
    return nc.vector.tensor_tensor(out, y[:], xb[:], ALU.add)


def gather_rows(nc, pool, source, ids, out, landed, limit):
    for q in range(S):
        nc.gpsimd.indirect_dma_start(
            out=out[:, q], out_offset=None, in_=source,
            in_offset=bass.IndirectOffsetOnAxis(ap=ids[:, q:q + 1], axis=0),
            bounds_check=limit, oob_is_err=False).then_inc(landed, 16)


def first_propagation(nc, A, sem, W, D, bank):
    ctx = ExitStack()
    with ctx:
        t = lambda n, sh, dt=F32: ctx.enter_context(nc.sbuf_tensor(n, sh, dt))
        col = W.col
        near = t("p1_near", [P, 2, 2, S], I32)
        tabs = t("p1_tab", [P, 2, 2, S, 2])
        wt = t("p1_wt", [P, S])
        lsi = t("p1_ls", [P, 2, S], I32)
        t0, xd, msg, td, g1 = (t("p1_" + n, [P, 2, S, C]) for n in ("t0", "xd", "msg", "td", "g1"))
        h0, ma = t("p1_h0", [P, S, C]), t("p1_ma", [P, S, C])
        tf = t("p1_tf", [P, 2, HALF])
        sums, pd = t("p1_sums", [C, 2, G_ROWS]), t("p1_pd", [C, 2, G_ROWS])
        na = norm_bufs(t, "p1_n")
        norm = Norm(sem, "p1_n", 2)
        names = ("in0", "in1", "tab0", "tab1", "w_step", "m_step", "msg_done", "h0_done", "td_done", "msg_t", "td_t", "tf_done",
                 "sums_done", "pd_mm", "back", "evacuated", "ls_st0", "ls_st1", "st0", "st1", "carry")
        m = {n: sem("p1_" + n) for n in names}
        two = lambda n: (m[n + "0"], m[n + "1"])
        inn, tabl, ls_st, st = two("in"), two("tab"), two("ls_st"), two("st")
        with nc.Block() as block:
            @block.sync
            def _(sp):
                for par in (0, 1):
                    sp.sem_inc(ls_st[par], 16)
                    sp.sem_inc(st[par], 32)

                def load(i, par, g):
                    sp.wait_ge(m["td_done"], g + 1)
                    sp.dma_start(near[:, par, 0], A["src_rows"][g]).then_inc(inn[par], 16)
                    sp.dma_start(near[:, par, 1], A["dst_rows"][g]).then_inc(inn[par], 16)
                    sp.dma_start(t0[:, par], group_rows(D.t0s)[g]).then_inc(inn[par], 16)
                    sp.dma_start(xd[:, par], group_rows(D.xd)[g]).then_inc(inn[par], 16)

                def store(i, par, g):
                    sp.wait_ge(m["td_done"], g + 3)
                    sp.dma_start(D.ls[g], lsi[:, par]).then_inc(ls_st[par], 16)
                    sp.wait_ge(m["evacuated"], g * 2 + 4)
                    sp.dma_start(group_cols(D.pd)[g], pd[:, par]).then_inc(st[par], 16)
                    sp.dma_start(group_rows(D.tx1)[g], g1[:, par]).then_inc(st[par], 16)
                paired_loop(sp, GROUPS, load, store)
                for par in (0, 1):
                    sp.wait_ge(ls_st[par], ODD_EVEN[par] + 16)
                    sp.wait_ge(st[par], 2 * ODD_EVEN[par] + 32)

            @block.gpsimd
            def _(pool):
                def gather(i, par, g):
                    hold(pool, inn[par], i * 64 + 64)
                    hold(pool, m["td_done"], g + 1)
                    for k in (0, 1):
                        gather_rows(nc, pool, D.table, near[:, par, k], tabs[:, par, k], tabl[par], NP_ - 1)
                paired_loop(pool, GROUPS, gather)

            @block.vector
            def _(dve):
                dve.sem_inc(m["td_done"], 2)
                nc.vector.memset(sums[:, 1, G_ROWS - 1:G_ROWS], 0.0).then_inc(m["carry"], 1)

                def first(i, par, g):
                    dve.wait_ge(inn[par], i * 64 + 64)
                    dve.wait_ge(tabl[par], i * 256 + 256)
                    dve.wait_ge(ls_st[par], i * 16 + 16)
                    w = W.wE[:, bass.ds(g, 1)].rearrange("p a s -> p (a s)")
                    ew = W.ewE[:, bass.ds(g, 1)].rearrange("p a s -> p (a s)")
                    nc.vector.scalar_tensor_tensor(out=wt[:], in0=tabs[:, par, 0, :, 0], scalar=-1.0,
                                                   in1=tabs[:, par, 1, :, 0], op0=ALU.mult, op1=ALU.mult
                                                   ).then_inc(m["w_step"], 1)
                    nc.vector.tensor_copy(lsi[:, par], tabs[:, par, 0, :, 1].bitcast(I32))
                    nc.vector.tensor_tensor(ma[:], t0[:, par], along(W.rows[:, 0]), ALU.mult).then_inc(m["m_step"], 1)
                    dve.wait_ge(m["w_step"], g * 2 + 1)
                    nc.vector.tensor_tensor(w, wt[:], ew, ALU.mult).then_inc(m["w_step"], 1)
                    dve.wait_ge(m["m_step"], g * 2 + 1)
                    nc.vector.tensor_tensor(ma[:], ma[:], along(W.rows[:, 1]), ALU.add).then_inc(m["m_step"], 1)
                    dve.wait_ge(m["m_step"], g * 2 + 2)
                    nc.vector.tensor_tensor(msg[:, par], ma[:], spread(w), ALU.mult).then_inc(m["msg_done"], 1)
                    norm.dve(nc, dve, g, 0, xd[:, par], na)
                    nc.vector.scalar_tensor_tensor(out=h0[:], in0=na.xc[:], scalar=0.0, in1=spread(na.rstd[:]),
                                                   op0=ALU.max, op1=ALU.mult).then_inc(m["h0_done"], 1)
                    dve.wait_ge(m["h0_done"], g + 1)
                    norm.dve(nc, dve, g, 1, h0[:], na)
                    nc.vector.tensor_tensor(td[:, par], na.xc[:], spread(na.rstd[:]), ALU.mult
                                            ).then_inc(m["td_done"], 1)

                def second(i, par, g):
                    dve.wait_ge(m["msg_t"], g + 1)
                    dve.wait_ge(m["carry"], g + 1)
                    run_sums(nc, W, g, par, bank(4 + 2 * par, 2)[0:C], sums, m)
                paired_loop(dve, GROUPS, first, second)

            @block.tensor
            def _(pe):
                def first(i, par, g):
                    hold(pe, m["msg_done"], g + 1)
                    transpose_rows(nc, bank(4 + 2 * par, 2), msg[:, par], W).then_inc(m["msg_t"], 1)
                    hold(pe, m["td_done"], g + 3)
                    transpose_pairs(nc, bank(0), td[:, par], W).then_inc(m["td_t"], 1)

                def second(i, par, g):
                    hold(pe, m["tf_done"], g + 1)
                    hold(pe, m["carry"], g + 2)
                    hold(pe, m["evacuated"], g * 2 + 2)
                    for h in (0, 1):
                        part = slice(HALF * h, HALF * h + HALF)
                        nc.tensor.matmul(bank(2, 2)[0:C, part], W.w02_half[:, h], tf[:, par], start=True, stop=False)
                        last = nc.tensor.matmul(bank(2, 2)[0:C, part], W.w1[:], sums[:, par, part], start=False, stop=True)
                    last.then_inc(m["pd_mm"], 1)
                    transpose_back(nc, bank(1), sums[:, par], W).then_inc(m["back"], 1)
                paired_loop(pe, GROUPS, first, second)

            @block.scalar
            def _(act):
                act.sem_inc(m["evacuated"], 2)

                def first(i, par, g):
                    norm.act(nc, act, g, 0, na)
                    norm.act(nc, act, g, 1, na)
                    act.wait_ge(m["td_t"], g + 1)
                    nc.scalar.activation(tf[:, par], bank(0), ACT.Identity, bias=col["ln_beta"],
                                         scale=col["ln_gamma"]).then_inc(m["tf_done"], 1)

                def second(i, par, g):
                    act.wait_ge(st[par], i * 32 + 32)
                    act.wait_ge(m["pd_mm"], g + 1)
                    nc.scalar.activation(pd[:, par], bank(2, 2)[0:C], ACT.Identity, bias=col["cheb_b"][0:C]
                                         ).then_inc(m["evacuated"], 1)
                    act.wait_ge(m["back"], g + 1)
                    nc.scalar.activation(g1[:, par], as_rows(bank(1)), ACT.Copy).then_inc(m["evacuated"], 1)
                paired_loop(act, GROUPS, first, second)


def run_sums(nc, W, g, par, messages, sums, m):
    return nc.vector.tensor_tensor_scan(
        sums[:, par], W.same[:, bass.ds(g * G_ROWS, G_ROWS)], messages, sums[:, 1 - par, G_ROWS - 1:G_ROWS],
        ALU.mult, ALU.add).then_inc(m["carry"], 1)


def second_propagation(nc, A, sem, W, D, bank):
    ctx = ExitStack()
    with ctx:
        t = lambda n, sh, dt=F32: ctx.enter_context(nc.sbuf_tensor(n, sh, dt))
        near = t("p2_near", [P, 2, S], I32)
        got, msg, hr = (t("p2_" + n, [P, 2, S, C]) for n in ("got", "msg", "hr"))
        sums, pd = t("p2_sums", [C, 2, G_ROWS]), t("p2_pd", [C, 2, G_ROWS])
        pre, hf = t("p2_pre", [C, G_ROWS]), t("p2_hf", [C, G_ROWS])
        att = t("p2_att", [2 * HEADS, 2, G_ROWS])
        names = ("in0", "in1", "pd_in0", "pd_in1", "got0", "got1", "msg_done", "zeroed", "msg_t", "carry", "mm", "pre_done", "h_done",
                 "back", "att_mm", "evacuated", "st0", "st1")
        m = {n: sem("p2_" + n) for n in names}
        two = lambda n: (m[n + "0"], m[n + "1"])
        inn, pd_in, landed, st = two("in"), two("pd_in"), two("got"), two("st")
        with nc.Block() as block:
            @block.sync
            def _(sp):
                for par in (0, 1):
                    sp.sem_inc(st[par], 32)

                def load(i, par, g):
                    sp.wait_ge(m["msg_done"], g + 1)
                    sp.dma_start(near[:, par], D.ls[g]).then_inc(inn[par], 16)
                    sp.wait_ge(m["pre_done"], g + 1)
                    sp.dma_start(pd[:, par], group_cols(D.pd)[g]).then_inc(pd_in[par], 16)

                def store(i, par, g):
                    sp.wait_ge(m["evacuated"], g * 2 + 4)
                    sp.dma_start(group_rows(D.hd)[g], hr[:, par]).then_inc(st[par], 16)
                    sp.dma_start(group_cols(D.att_d)[g], att[:, par]).then_inc(st[par], 16)
                paired_loop(sp, GROUPS, load, store)
                for par in (0, 1):
                    sp.wait_ge(st[par], 2 * ODD_EVEN[par] + 32)

            @block.gpsimd
            def _(pool):
                def gather(i, par, g):
                    hold(pool, inn[par], i * 16 + 16)
                    hold(pool, m["zeroed"], g + 1)
                    gather_rows(nc, pool, D.tx1, near[:, par], got[:, par], landed[par], EP - 1)
                paired_loop(pool, GROUPS, gather)

            @block.vector
            def _(dve):
                dve.sem_inc(m["msg_done"], 2)
                dve.sem_inc(m["pre_done"], 2)
                nc.vector.memset(got[:, 0], 0.0).then_inc(m["zeroed"], 1)
                nc.vector.memset(got[:, 1], 0.0).then_inc(m["zeroed"], 1)
                nc.vector.memset(sums[:, 1, G_ROWS - 1:G_ROWS], 0.0).then_inc(m["carry"], 1)

                def first(i, par, g):
                    dve.wait_ge(landed[par], i * 128 + 128)
                    w = W.wE[:, bass.ds(g, 1)].rearrange("p a s -> p (a s)")
                    nc.vector.tensor_tensor(msg[:, par], got[:, par], spread(w), ALU.mult).then_inc(m["msg_done"], 1)
                    dve.wait_ge(m["msg_done"], g + 3)
                    nc.vector.memset(got[:, par], 0.0).then_inc(m["zeroed"], 1)

                def second(i, par, g):
                    dve.wait_ge(m["msg_t"], g + 1)
                    dve.wait_ge(m["carry"], g + 1)
                    run_sums(nc, W, g, par, bank(4 + 2 * par, 2)[0:C], sums, m)
                    dve.wait_ge(m["mm"], g + 1)
                    dve.wait_ge(pd_in[par], i * 16 + 16)
                    nc.vector.tensor_tensor(pre[:], bank(2, 2)[0:C], pd[:, par], ALU.add).then_inc(m["pre_done"], 1)
                    dve.wait_ge(m["pre_done"], g + 3)
                    nc.vector.scalar_tensor_tensor(out=hf[:], in0=pre[:], scalar=0.01, in1=pre[:], op0=ALU.mult,
                                                   op1=ALU.max).then_inc(m["h_done"], 1)
                paired_loop(dve, GROUPS, first, second)

            @block.tensor
            def _(pe):
                def first(i, par, g):
                    hold(pe, m["msg_done"], g + 3)
                    transpose_rows(nc, bank(4 + 2 * par, 2), msg[:, par], W).then_inc(m["msg_t"], 1)

                def second(i, par, g):
                    hold(pe, m["carry"], g + 2)
                    hold(pe, m["evacuated"], g * 2 + 2)
                    for h in (0, 1):
                        part = slice(HALF * h, HALF * h + HALF)
                        last = nc.tensor.matmul(bank(2, 2)[0:C, part], W.w2x2[:], sums[:, par, part], start=True, stop=True)
                    last.then_inc(m["mm"], 1)
                    hold(pe, m["h_done"], g + 1)
                    transpose_back(nc, bank(1), hf[:], W).then_inc(m["back"], 1)
                    for h in (0, 1):
                        part = slice(HALF * h, HALF * h + HALF)
                        last = nc.tensor.matmul(bank(2, 2)[0:2 * HEADS, part], W.att[:].rearrange("k q h -> k (q h)"),
                                                hf[:, part], start=True, stop=True)
                    last.then_inc(m["att_mm"], 1)
                paired_loop(pe, GROUPS, first, second)

            @block.scalar
            def _(act):
                act.sem_inc(m["evacuated"], 2)

                def second(i, par, g):
                    act.wait_ge(st[par], i * 32 + 32)
                    act.wait_ge(m["back"], g + 1)
                    nc.scalar.activation(hr[:, par], as_rows(bank(1)), ACT.Copy).then_inc(m["evacuated"], 1)
                    act.wait_ge(m["att_mm"], g + 1)
                    nc.scalar.activation(att[:, par], bank(2, 2)[0:2 * HEADS], ACT.Copy).then_inc(m["evacuated"], 1)
                paired_loop(act, GROUPS, second)


def attention_sources(nc, A, sem, W, D, bank):
    ctx = ExitStack()
    with ctx:
        t = lambda n, sh, dt=F32: ctx.enter_context(nc.sbuf_tensor(n, sh, dt))
        near = t("p3_near", [P, 2, S], I32)
        got = t("p3_got", [P, 2, S, C])
        hf = t("p3_hf", [P, HALF])
        att = t("p3_att", [HEADS, 2, G_ROWS])
        names = ("in0", "in1", "got0", "got1", "got_t", "hf_done", "mm", "att_done", "st0", "st1")
        m = {n: sem("p3_" + n) for n in names}
        two = lambda n: (m[n + "0"], m[n + "1"])
        inn, landed, st = two("in"), two("got"), two("st")
        with nc.Block() as block:
            @block.sync
            def _(sp):
                for par in (0, 1):
                    sp.sem_inc(st[par], 32)

                def load(i, par, g):
                    sp.wait_ge(m["att_done"], g + 1)
                    sp.wait_ge(st[par], i * 32 + 32)
                    sp.dma_start(near[:, par], D.ls[g]).then_inc(inn[par], 16)
                    sp.dma_start(got[:, par], group_rows(D.h_lone)[g]).then_inc(inn[par], 16)

                def store(i, par, g):
                    sp.wait_ge(landed[par], i * 128 + 128)
                    sp.dma_start(group_rows(D.hs)[g], got[:, par]).then_inc(st[par], 16)
                    sp.wait_ge(m["att_done"], g + 3)
                    sp.dma_start(group_cols(D.att_s)[g], att[:, par]).then_inc(st[par], 16)
                paired_loop(sp, GROUPS, load, store)
                for par in (0, 1):
                    sp.wait_ge(st[par], 2 * ODD_EVEN[par] + 32)

            @block.gpsimd
            def _(pool):
                def gather(i, par, g):
                    hold(pool, inn[par], i * 32 + 32)
                    gather_rows(nc, pool, D.hd, near[:, par], got[:, par], landed[par], EP - 1)
                paired_loop(pool, GROUPS, gather)

            @block.tensor
            def _(pe):
                def work(i, par, g):
                    hold(pe, landed[par], i * 128 + 128)
                    transpose_pairs(nc, bank(0), got[:, par], W).then_inc(m["got_t"], 1)
                    hold(pe, m["hf_done"], g + 1)
                    halves(nc, bank(2, 2)[0:HEADS], W.att_half, hf[:]).then_inc(m["mm"], 1)
                paired_loop(pe, GROUPS, work)

            @block.scalar
            def _(act):
                act.sem_inc(m["att_done"], 2)

                def work(i, par, g):
                    act.wait_ge(m["got_t"], g + 1)
                    nc.scalar.activation(hf[:], bank(0), ACT.Copy).then_inc(m["hf_done"], 1)
                    act.wait_ge(st[par], i * 32 + 32)
                    act.wait_ge(m["mm"], g + 1)
                    nc.scalar.activation(att[:, par], bank(2, 2)[0:HEADS], ACT.Copy).then_inc(m["att_done"], 1)
                paired_loop(act, GROUPS, work)


def edge_terms(nc, A, sem, W, D, bank):
    ctx = ExitStack()
    with ctx:
        t = lambda n, sh, dt=F32: ctx.enter_context(nc.sbuf_tensor(n, sh, dt))
        col = W.col
        ea = t("et_ea", [EDIM, 2, G_ROWS])
        hid = [t(f"et_hid{k}", [C, G_ROWS])[:] for k in (0, 1)]
        et = t("et_out", [C, 2, G_ROWS])
        m = {n: sem("et_" + n) for n in ("in0", "in1", "mm1", "hid", "mm2", "done", "st0", "st1")}
        inn, st = (m["in0"], m["in1"]), (m["st0"], m["st1"])
        with nc.Block() as block:
            @block.sync
            def _(sp):
                for par in (0, 1):
                    sp.sem_inc(st[par], 16)

                def load(i, par, g):
                    sp.wait_ge(m["done"], g + 1)
                    sp.dma_start(ea[:, par], group_cols(A["ea_cols"])[g]).then_inc(inn[par], 16)

                def store(i, par, g):
                    sp.wait_ge(m["done"], g + 3)
                    sp.dma_start(group_cols(D.et)[g], et[:, par]).then_inc(st[par], 16)
                paired_loop(sp, GROUPS, load, store)
                for par in (0, 1):
                    sp.wait_ge(st[par], ODD_EVEN[par] + 16)

            @block.tensor
            def _(pe):
                def work(i, par, g):
                    hold(pe, inn[par], i * 16 + 16)
                    for h in (0, 1):
                        part = slice(HALF * h, HALF * h + HALF)
                        last = nc.tensor.matmul(bank(2, 2)[0:C, part], W.w1e[:], ea[:, par, part], start=True, stop=True)
                    last.then_inc(m["mm1"], 1)
                    hold(pe, m["hid"], g + 1)
                    for h in (0, 1):
                        part = slice(HALF * h, HALF * h + HALF)
                        for k in (0, 1):
                            last = nc.tensor.matmul(bank(4 + 2 * par, 2)[0:C, part], W.w2e[:], hid[k][:, part],
                                                    start=k == 0, stop=k == 1)
                    last.then_inc(m["mm2"], 1)
                paired_loop(pe, GROUPS, work)

            @block.scalar
            def _(act):
                def work(i, par, g):
                    act.wait_ge(m["mm1"], g + 1)
                    leaky_parts(nc, hid, bank(2, 2)[0:C], 0.1, col["b1e_slope"][0:C], col["b1e_rest"][0:C]
                                ).then_inc(m["hid"], 1)
                paired_loop(act, GROUPS, work)

            @block.vector
            def _(dve):
                dve.sem_inc(m["done"], 2)

                def work(i, par, g):
                    dve.wait_ge(st[par], i * 16 + 16)
                    dve.wait_ge(m["mm2"], g + 1)
                    nc.vector.tensor_scalar(et[:, par], bank(4 + 2 * par, 2)[0:C], col["b2e"][0:C], col["dp"][0:C],
                                            ALU.add, ALU.mult).then_inc(m["done"], 1)
                paired_loop(dve, GROUPS, work)


def attention_weights(nc, A, sem, W, D, bank):
    ctx = ExitStack()
    with ctx:
        t = lambda n, sh, dt=F32: ctx.enter_context(nc.sbuf_tensor(n, sh, dt))
        ids = t("sm_ids", [P, 3, CHUNK], I32)
        as_, ex, big = (t("sm_" + n, [P, HEADS, CHUNK]) for n in ("as", "ex", "big"))
        ad, back = (t("sm_" + n, [P, 2 * HEADS, CHUNK]) for n in ("ad", "back"))
        prev, nxt, last, fm, rm, gate, zero = (t("sm_" + n, [P, CHUNK]) for n in
                                               ("prev", "next", "last", "fm", "rm", "gate", "zero"))
        ends = t("sm_ends", [P, 2, 2 * HEADS])
        rows = t("sm_rows", [2 * HEADS, 2, P + 2])
        carry = t("sm_carry", [P, 2 * HEADS])
        m = {n: sem("sm_" + n) for n in ("in", "step", "ends_t", "carry_t", "ex_ready", "ex_done", "exs_ready", "exs_done", "ready", "stored")}
        rev = lambda a: a[:, ::-1]
        ADD, MAX, MUL = ALU.add, ALU.max, ALU.mult
        PLAN = []
        with nc.Block() as block:
            @block.sync
            def _(sp):
                line = A["dst_line"]
                for k, off in enumerate((0, 1, 2)):
                    sp.dma_start(ids[:, k], line[:, off:off + EP].rearrange("a (p e) -> (a p) e", p=P)).then_inc(m["in"], 16)
                sp.dma_start(as_[:], D.att_s.rearrange("h (p e) -> p h e", p=P)).then_inc(m["in"], 16)
                sp.dma_start(ad[:], D.att_d.rearrange("h (p e) -> p h e", p=P)).then_inc(m["in"], 16)
                sp.wait_ge(m["ready"], 1)
                out = D.alpha.rearrange("h (p e) -> p h e", p=P)
                sp.dma_start(out[:, 0:HEADS], ex[:]).then_inc(m["stored"], 16)
                sp.dma_start(out[:, HEADS:2 * HEADS], as_[:]).then_inc(m["stored"], 16)
                sp.wait_ge(m["stored"], 32)

            @block.tensor
            def _(pe):
                for n, k in enumerate(EXCHANGES):
                    pe.wait_ge(m["ex_ready"], 2 * n + 1)
                    for q in (0, 1):
                        last = nc.tensor.transpose(bank(q)[0:k, 0:P], ends[:, q, 0:k], W.ident[:])
                    last.then_inc(m["ends_t"], 1)
                    pe.wait_ge(m["ex_ready"], 2 * n + 2)
                    nc.tensor.transpose(bank(2)[:, 0:k], rows[0:k, 1, 1:P + 1], W.ident[0:k, 0:k]).then_inc(m["carry_t"], 1)

            @block.scalar
            def _(act):
                act.wait_ge(m["exs_ready"], 1)
                nc.scalar.activation(ex[:], ex[:], ACT.Exp)
                nc.scalar.activation(ad[:, 0:HEADS], ad[:, 0:HEADS], ACT.Exp).then_inc(m["exs_done"], 1)

            @block.vector
            def _(dve):
                n, x = [0], [0]

                def done(ins):
                    n[0] += 1
                    ins.then_inc(m["step"], 1)

                def wait():
                    dve.wait_ge(m["step"], n[0])

                def exchange(k, values, flag, combine, start, backward):
                    for h in range(k):
                        done(nc.vector.tensor_copy(ends[:, 1, h:h + 1], flag))
                        done(nc.vector.tensor_copy(ends[:, 0, h:h + 1], values(h)))
                    wait()
                    dve.sem_inc(m["ex_ready"], 1)
                    x[0] += 1
                    dve.wait_ge(m["ends_t"], x[0])
                    if combine == MAX:
                        done(nc.vector.tensor_scalar(rows[0:k, 0, 0:P], bank(1)[0:k, 0:P], -1.0, FAR, ADD, MUL))
                    else:
                        done(nc.vector.tensor_copy(rows[0:k, 0, 0:P], bank(1)[0:k, 0:P]))
                    at = slice(0, P) if backward else slice(2, P + 2)
                    done(nc.vector.memset(rows[0:k, 1], start))
                    wait()
                    order = rev if backward else (lambda a: a)
                    done(nc.vector.tensor_tensor_scan(order(rows[0:k, 1, at]), order(rows[0:k, 0, 0:P]),
                                                      order(bank(0)[0:k, 0:P]), start,
                                                      ADD if combine == MAX else MUL, combine))
                    wait()
                    dve.sem_inc(m["ex_ready"], 1)
                    dve.wait_ge(m["carry_t"], x[0])
                    done(nc.vector.tensor_copy(carry[:, 0:k], bank(2)[:, 0:k]))
                    wait()

                def spread_back(k, values):
                    done(nc.vector.tensor_tensor(back[:, 0:k], values, last[:].unsqueeze(1).to_broadcast([P, k, CHUNK]), MUL))
                    wait()
                    for h in range(k):
                        done(nc.vector.tensor_tensor_scan(rev(back[:, h]), rev(nxt[:]), rev(back[:, h]), 0.0, MUL, ADD))
                    wait()
                    exchange(k, lambda h: back[:, h, 0:1], rm[:, 0:1], ADD, 0.0, True)
                    for h in range(k):
                        done(nc.vector.scalar_tensor_tensor(out=back[:, h], in0=rm[:], scalar=carry[:, h:h + 1],
                                                            in1=back[:, h], op0=MUL, op1=ADD))
                    wait()

                dve.wait_ge(m["in"], 80)
                done(nc.vector.tensor_tensor(prev[:], ids[:, 0], ids[:, 1], ALU.is_equal))
                done(nc.vector.tensor_tensor(nxt[:], ids[:, 1], ids[:, 2], ALU.is_equal))
                done(nc.vector.tensor_tensor(last[:], ids[:, 1], ids[:, 2], ALU.not_equal))
                done(nc.vector.memset(zero[:], 0.0))
                wait()
                done(nc.vector.tensor_tensor_scan(fm[:], prev[:], zero[:], 1.0, MUL, ADD))
                done(nc.vector.tensor_tensor_scan(rev(rm[:]), rev(nxt[:]), zero[:], 1.0, MUL, ADD))
                done(nc.vector.tensor_scalar(gate[:], prev[:], -1.0, FAR, ADD, MUL))
                wait()
                for h in range(HEADS):
                    done(nc.vector.tensor_tensor_scan(big[:, h], gate[:], as_[:, h], -FAR, ADD, MAX))
                wait()
                exchange(HEADS, lambda h: big[:, h, CHUNK - 1:CHUNK], fm[:, CHUNK - 1:CHUNK], MAX, -FAR, False)
                done(nc.vector.tensor_scalar(gate[:], fm[:], -1.0, FAR, ADD, MUL))
                wait()
                for h in range(HEADS):
                    done(nc.vector.scalar_tensor_tensor(out=big[:, h], in0=gate[:], scalar=carry[:, h:h + 1],
                                                        in1=big[:, h], op0=ADD, op1=MAX))
                wait()
                done(nc.vector.tensor_tensor(big[:], big[:], ad[:, 0:HEADS], MAX))
                wait()
                done(nc.vector.tensor_tensor(big[:], big[:], ad[:, HEADS:], ADD))
                done(nc.vector.tensor_tensor(ad[:, 0:HEADS], ad[:, 0:HEADS], ad[:, HEADS:], ADD))
                wait()
                done(nc.vector.scalar_tensor_tensor(out=big[:], in0=big[:], scalar=0.2, in1=big[:], op0=MUL, op1=MAX))
                done(nc.vector.scalar_tensor_tensor(out=ad[:, 0:HEADS], in0=ad[:, 0:HEADS], scalar=0.2,
                                                    in1=ad[:, 0:HEADS], op0=MUL, op1=MAX))
                wait()
                done(nc.vector.tensor_tensor(ad[:, 0:HEADS], ad[:, 0:HEADS], big[:], ALU.subtract))
                spread_back(HEADS, ad[:, HEADS:])
                done(nc.vector.tensor_tensor(ex[:], as_[:], back[:, 0:HEADS], ADD))
                wait()
                done(nc.vector.scalar_tensor_tensor(out=ex[:], in0=ex[:], scalar=0.2, in1=ex[:], op0=MUL, op1=MAX))
                wait()
                spread_back(HEADS, big[:])
                done(nc.vector.tensor_tensor(ex[:], ex[:], back[:, 0:HEADS], ALU.subtract))
                done(nc.vector.tensor_scalar(ad[:, 0:HEADS], ad[:, 0:HEADS], 0.0, None, ALU.min))
                wait()
                dve.sem_inc(m["exs_ready"], 1)
                dve.wait_ge(m["exs_done"], 1)
                for h in range(HEADS):
                    done(nc.vector.tensor_tensor_scan(big[:, h], prev[:], ex[:, h], 0.0, MUL, ADD))
                wait()
                exchange(HEADS, lambda h: big[:, h, CHUNK - 1:CHUNK], fm[:, CHUNK - 1:CHUNK], ADD, 0.0, False)
                for h in range(HEADS):
                    done(nc.vector.scalar_tensor_tensor(out=big[:, h], in0=fm[:], scalar=carry[:, h:h + 1],
                                                        in1=big[:, h], op0=MUL, op1=ADD))
                wait()
                done(nc.vector.scalar_tensor_tensor(out=big[:], in0=big[:], scalar=1e-16, in1=ad[:, 0:HEADS], op0=ADD, op1=ADD))
                wait()
                done(nc.vector.reciprocal(big[:], big[:]))
                wait()
                done(nc.vector.tensor_tensor(as_[:], ad[:, 0:HEADS], big[:], MUL))
                spread_back(HEADS, big[:])
                done(nc.vector.tensor_tensor(ex[:], ex[:], back[:, 0:HEADS], MUL))
                done(nc.vector.tensor_tensor(as_[:], as_[:], last[:].unsqueeze(1).to_broadcast([P, HEADS, CHUNK]), MUL))
                wait()
                dve.sem_inc(m["ready"], 1)
                assert x[0] == len(EXCHANGES)


def attention_sums(nc, A, sem, W, D, bank):
    ctx = ExitStack()
    with ctx:
        t = lambda n, sh, dt=F32: ctx.enter_context(nc.sbuf_tensor(n, sh, dt))
        col = W.col
        hs, hd, xd, x1 = (t("at_" + n, [P, 2, S, C]) for n in ("hs", "hd", "xd", "x1"))
        alpha = t("at_alpha", [2 * HEADS, 2, G_ROWS])
        al = t("at_al", [P, 2, S, 2 * HEADS])
        wide, own = t("at_wide", [P, S, HEADS, C]), t("at_own", [P, S, HEADS, C])
        pf = t("at_pf", [P, 2, 2, HALF])
        sums = t("at_sums", [C, 2, G_ROWS])
        parts = [t(f"at_u{k}", [C, G_ROWS])[:] for k in (0, 1)]
        names = ("in0", "in1", "al_t", "al_done", "wide_step", "wide_t", "pf_done", "mm", "carry", "u_done", "back",
                 "x1_done", "st0", "st1")
        m = {n: sem("at_" + n) for n in names}
        inn, st = (m["in0"], m["in1"]), (m["st0"], m["st1"])
        with nc.Block() as block:
            @block.sync
            def _(sp):
                for par in (0, 1):
                    sp.sem_inc(st[par], 16)

                def load(i, par, g):
                    sp.wait_ge(m["x1_done"], g + 1)
                    for b, d in ((hs, D.hs), (hd, D.hd), (xd, D.xd)):
                        sp.dma_start(b[:, par], group_rows(d)[g]).then_inc(inn[par], 16)
                    sp.dma_start(alpha[:, par], group_cols(D.alpha)[g]).then_inc(inn[par], 16)

                def store(i, par, g):
                    sp.wait_ge(m["x1_done"], g + 3)
                    sp.dma_start(group_rows(D.x1d)[g], x1[:, par]).then_inc(st[par], 16)
                paired_loop(sp, GROUPS, load, store)
                for par in (0, 1):
                    sp.wait_ge(st[par], ODD_EVEN[par] + 16)

            @block.vector
            def _(dve):
                dve.sem_inc(m["x1_done"], 2)
                nc.vector.memset(sums[:, 1, G_ROWS - 1:G_ROWS], 0.0).then_inc(m["carry"], 1)

                def first(i, par, g):
                    dve.wait_ge(inn[par], i * 64 + 64)
                    dve.wait_ge(m["al_done"], g + 1)
                    if not (isinstance(g, int) and g == 0):
                        dve.wait_ge(m["wide_t"], g * 2)
                    by = lambda x: x.unsqueeze(2).to_broadcast([P, S, HEADS, C])
                    wt = lambda k: al[:, par, :, HEADS * k:HEADS * k + HEADS].unsqueeze(3).to_broadcast([P, S, HEADS, C])
                    nc.vector.tensor_tensor(wide[:], by(hs[:, par]), wt(0), ALU.mult).then_inc(m["wide_step"], 1)
                    nc.vector.tensor_tensor(own[:], by(hd[:, par]), wt(1), ALU.mult).then_inc(m["wide_step"], 1)
                    dve.wait_ge(m["wide_step"], g * 3 + 2)
                    nc.vector.tensor_tensor(wide[:], wide[:], own[:], ALU.add).then_inc(m["wide_step"], 1)

                def second(i, par, g):
                    dve.wait_ge(m["mm"], g + 1)
                    dve.wait_ge(m["carry"], g + 1)
                    run_sums(nc, W, g, par, bank(4 + 2 * par, 2)[0:C], sums, m)
                    dve.wait_ge(st[par], i * 16 + 16)
                    dve.wait_ge(m["back"], g + 1)
                    nc.vector.tensor_tensor(x1[:, par], xd[:, par], as_rows(bank(1)), ALU.add).then_inc(m["x1_done"], 1)
                paired_loop(dve, GROUPS, first, second)

            @block.tensor
            def _(pe):
                def first(i, par, g):
                    hold(pe, inn[par], i * 64 + 64)
                    for n in range(S):
                        last = nc.tensor.transpose(bank(0)[:, 2 * HEADS * n:2 * HEADS * (n + 1)],
                                                   alpha[:, par, slot_cols(n)], W.ident[0:2 * HEADS, 0:2 * HEADS])
                    last.then_inc(m["al_t"], 1)
                    hold(pe, m["wide_step"], g * 3 + 3)
                    for h in (0, 1):
                        for j in range(S // 2):
                            for q in (0, 1):
                                last = nc.tensor.transpose(bank(2 + q)[:, P * j:P * j + P],
                                                           wide[:, 2 * j + h, 2 * q:2 * q + 2].rearrange("p h c -> p (h c)"),
                                                           W.ident[:])
                        last.then_inc(m["wide_t"], 1)
                        hold(pe, m["pf_done"], g * 2 + h + 1)
                        for q in (0, 1):
                            last = nc.tensor.matmul(bank(4 + 2 * par, 2)[0:C, HALF * h:HALF * h + HALF], W.gatw[:, q],
                                                    pf[:, h, q], start=q == 0, stop=q == 1)
                    last.then_inc(m["mm"], 1)

                def second(i, par, g):
                    hold(pe, m["u_done"], g + 1)
                    hold(pe, m["x1_done"], g + 2)
                    sum_transposed(nc, bank(1), parts, W, S).then_inc(m["back"], 1)
                paired_loop(pe, GROUPS, first, second)

            @block.scalar
            def _(act):
                def first(i, par, g):
                    act.wait_ge(m["al_t"], g + 1)
                    nc.scalar.activation(al[:, par], bank(0)[:, 0:2 * HEADS * S].rearrange("p (s h) -> p s h", s=S),
                                         ACT.Copy).then_inc(m["al_done"], 1)
                    for h in (0, 1):
                        act.wait_ge(m["wide_t"], g * 2 + h + 1)
                        nc.scalar.activation(pf[:, h], bank(2, 2).rearrange("p (q n) -> p q n", q=2), ACT.Copy
                                             ).then_inc(m["pf_done"], 1)

                def second(i, par, g):
                    act.wait_ge(m["carry"], g + 2)
                    leaky_parts(nc, parts, sums[:, par], 0.01, col["gat_b_slope"][0:C], col["gat_b_rest"][0:C]
                                ).then_inc(m["u_done"], 1)
                paired_loop(act, GROUPS, first, second)


def gated_messages(nc, A, sem, W, D, bank):
    ctx = ExitStack()
    with ctx:
        t = lambda n, sh, dt=F32: ctx.enter_context(nc.sbuf_tensor(n, sh, dt))
        col = W.col
        near = t("l1_near", [P, 2, S], I32)
        got, xd, hn, x2 = (t("l1_" + n, [P, 2, S, C]) for n in ("got", "xd", "hn", "x2"))
        hd, o1, y, xb = (t("l1_" + n, [P, S, C]) for n in ("hd", "o1", "y", "xb"))
        et, sums = t("l1_et", [C, 2, G_ROWS]), t("l1_sums", [C, 2, G_ROWS])
        msg = t("l1_msg", [C, G_ROWS])
        hf = t("l1_hf", [P, HALF])
        hid = [t(f"l1_hid{k}", [P, G_ROWS])[:] for k in (0, 1)]
        na, nb = norm_bufs(t, "l1_a"), norm_bufs(t, "l1_b")
        norm_a, norm_b = Norm(sem, "l1_a", 1), Norm(sem, "l1_b", 2)
        names = ("in0", "in1", "got0", "got1", "hn_done", "hn_t", "hf_done", "mm1", "hid_done", "mm2", "msg_done", "carry",
                 "back", "hd_done", "o1_done", "y_step", "x2_done", "st0", "st1")
        m = {n: sem("l1_" + n) for n in names}
        inn, landed, st = (m["in0"], m["in1"]), (m["got0"], m["got1"]), (m["st0"], m["st1"])
        with nc.Block() as block:
            @block.sync
            def _(sp):
                for par in (0, 1):
                    sp.sem_inc(st[par], 16)

                def load(i, par, g):
                    sp.wait_ge(m["x2_done"], g + 1)
                    sp.dma_start(near[:, par], D.ls[g]).then_inc(inn[par], 16)
                    sp.dma_start(got[:, par], group_rows(D.x1_lone)[g]).then_inc(inn[par], 16)
                    sp.dma_start(xd[:, par], group_rows(D.x1d)[g]).then_inc(inn[par], 16)
                    sp.dma_start(et[:, par], group_cols(D.et)[g]).then_inc(inn[par], 16)

                def store(i, par, g):
                    sp.wait_ge(m["x2_done"], g + 3)
                    sp.dma_start(group_rows(D.x2d)[g], x2[:, par]).then_inc(st[par], 16)
                paired_loop(sp, GROUPS, load, store)
                for par in (0, 1):
                    sp.wait_ge(st[par], ODD_EVEN[par] + 16)

            @block.gpsimd
            def _(pool):
                def gather(i, par, g):
                    hold(pool, inn[par], i * 64 + 64)
                    gather_rows(nc, pool, D.x1d, near[:, par], got[:, par], landed[par], EP - 1)
                paired_loop(pool, GROUPS, gather)

            @block.vector
            def _(dve):
                dve.sem_inc(m["x2_done"], 2)
                nc.vector.memset(sums[:, 1, G_ROWS - 1:G_ROWS], 0.0).then_inc(m["carry"], 1)

                def first(i, par, g):
                    dve.wait_ge(landed[par], i * 128 + 128)
                    norm_a.dve(nc, dve, g, 0, got[:, par], na)
                    nc.vector.scalar_tensor_tensor(out=hn[:, par], in0=na.xc, scalar=0.0, in1=spread(na.rstd),
                                                   op0=ALU.max, op1=ALU.mult).then_inc(m["hn_done"], 1)

                def second(i, par, g):
                    dve.wait_ge(inn[par], i * 64 + 64)
                    dve.wait_ge(m["mm2"], g + 1)
                    nc.vector.scalar_tensor_tensor(out=msg[:], in0=bank(4 + 2 * par, 2)[0:C], scalar=col["b2n"][0:C],
                                                   in1=et[:, par], op0=ALU.add, op1=ALU.mult).then_inc(m["msg_done"], 1)
                    dve.wait_ge(m["msg_done"], g + 1)
                    dve.wait_ge(m["carry"], g + 1)
                    run_sums(nc, W, g, par, msg[:], sums, m)
                    norm_b.dve(nc, dve, g, 0, xd[:, par], nb)
                    nc.vector.scalar_tensor_tensor(out=hd[:], in0=nb.xc, scalar=0.0, in1=spread(nb.rstd),
                                                   op0=ALU.max, op1=ALU.mult).then_inc(m["hd_done"], 1)
                    dve.wait_ge(m["hd_done"], g + 1)
                    dve.wait_ge(m["back"], g + 1)
                    nc.vector.scalar_tensor_tensor(out=o1[:], in0=as_rows(bank(1)), scalar=col["res"], in1=hd[:],
                                                   op0=ALU.mult, op1=ALU.add).then_inc(m["o1_done"], 1)
                    dve.wait_ge(m["o1_done"], g + 1)
                    norm_b.dve(nc, dve, g, 1, o1[:], nb)
                    dve.wait_ge(st[par], i * 16 + 16)
                    affine_residual(nc, dve, g, m["y_step"], nb, W, y, xb, xd[:, par], x2[:, par]).then_inc(m["x2_done"], 1)
                paired_loop(dve, GROUPS, first, second)

            @block.tensor
            def _(pe):
                def first(i, par, g):
                    hold(pe, m["hn_done"], g + 1)
                    transpose_pairs(nc, bank(0), hn[:, par], W).then_inc(m["hn_t"], 1)
                    hold(pe, m["hf_done"], g + 1)
                    halves(nc, bank(2, 2), W.w1n, hf[:]).then_inc(m["mm1"], 1)
                    hold(pe, m["hid_done"], g + 1)
                    for h in (0, 1):
                        part = slice(HALF * h, HALF * h + HALF)
                        for k in (0, 1):
                            last = nc.tensor.matmul(bank(4 + 2 * par, 2)[0:C, part], W.w2n[:], hid[k][:, part],
                                                    start=k == 0, stop=k == 1)
                    last.then_inc(m["mm2"], 1)

                def second(i, par, g):
                    hold(pe, m["carry"], g + 2)
                    hold(pe, m["x2_done"], g + 2)
                    transpose_back(nc, bank(1), sums[:, par], W).then_inc(m["back"], 1)
                paired_loop(pe, GROUPS, first, second)

            @block.scalar
            def _(act):
                def first(i, par, g):
                    norm_a.act(nc, act, g, 0, na)
                    act.wait_ge(m["hn_t"], g + 1)
                    nc.scalar.activation(hf[:], bank(0), ACT.Copy).then_inc(m["hf_done"], 1)
                    act.wait_ge(m["mm1"], g + 1)
                    leaky_parts(nc, hid, bank(2, 2), 0.1, col["b1n_slope"], col["b1n_rest"]).then_inc(m["hid_done"], 1)

                def second(i, par, g):
                    norm_b.act(nc, act, g, 0, nb)
                    norm_b.act(nc, act, g, 1, nb)
                paired_loop(act, GROUPS, first, second)


def relu_messages(nc, A, sem, W, D, bank):
    ctx = ExitStack()
    with ctx:
        t = lambda n, sh, dt=F32: ctx.enter_context(nc.sbuf_tensor(n, sh, dt))
        col = W.col
        near = t("l2_near", [P, 2, S], I32)
        got, xd, hn, x3 = (t("l2_" + n, [P, 2, S, C]) for n in ("got", "xd", "hn", "x3"))
        msg, sums = t("l2_msg", [C, 2, G_ROWS]), t("l2_sums", [C, 2, G_ROWS])
        hf = t("l2_hf", [P, HALF])
        na = norm_bufs(t, "l2_a")
        norm_a = Norm(sem, "l2_a", 1)
        names = ("in0", "in1", "got0", "got1", "hn_done", "hn_t", "hf_done", "mm", "msg_done", "carry", "back", "x3_done",
                 "st0", "st1")
        m = {n: sem("l2_" + n) for n in names}
        inn, landed, st = (m["in0"], m["in1"]), (m["got0"], m["got1"]), (m["st0"], m["st1"])
        with nc.Block() as block:
            @block.sync
            def _(sp):
                for par in (0, 1):
                    sp.sem_inc(st[par], 16)

                def load(i, par, g):
                    sp.wait_ge(m["x3_done"], g + 1)
                    sp.dma_start(near[:, par], D.ls[g]).then_inc(inn[par], 16)
                    sp.dma_start(got[:, par], group_rows(D.x2_lone)[g]).then_inc(inn[par], 16)
                    sp.dma_start(xd[:, par], group_rows(D.x2d)[g]).then_inc(inn[par], 16)

                def store(i, par, g):
                    sp.wait_ge(m["x3_done"], g + 3)
                    sp.dma_start(group_rows(D.x3d)[g], x3[:, par]).then_inc(st[par], 16)
                paired_loop(sp, GROUPS, load, store)
                for par in (0, 1):
                    sp.wait_ge(st[par], ODD_EVEN[par] + 16)

            @block.gpsimd
            def _(pool):
                def gather(i, par, g):
                    hold(pool, inn[par], i * 48 + 48)
                    gather_rows(nc, pool, D.x2d, near[:, par], got[:, par], landed[par], EP - 1)
                paired_loop(pool, GROUPS, gather)

            @block.vector
            def _(dve):
                dve.sem_inc(m["x3_done"], 2)
                nc.vector.memset(sums[:, 1, G_ROWS - 1:G_ROWS], 0.0).then_inc(m["carry"], 1)

                def first(i, par, g):
                    dve.wait_ge(landed[par], i * 128 + 128)
                    norm_a.dve(nc, dve, g, 0, got[:, par], na)
                    nc.vector.scalar_tensor_tensor(out=hn[:, par], in0=na.xc, scalar=0.0, in1=spread(na.rstd),
                                                   op0=ALU.max, op1=ALU.mult).then_inc(m["hn_done"], 1)

                def second(i, par, g):
                    dve.wait_ge(m["msg_done"], g + 1)
                    dve.wait_ge(m["carry"], g + 1)
                    run_sums(nc, W, g, par, msg[:, par], sums, m)
                    dve.wait_ge(inn[par], i * 48 + 48)
                    dve.wait_ge(st[par], i * 16 + 16)
                    dve.wait_ge(m["back"], g + 1)
                    nc.vector.tensor_tensor(x3[:, par], xd[:, par], as_rows(bank(1)), ALU.add).then_inc(m["x3_done"], 1)
                paired_loop(dve, GROUPS, first, second)

            @block.tensor
            def _(pe):
                def first(i, par, g):
                    hold(pe, m["hn_done"], g + 1)
                    transpose_pairs(nc, bank(0), hn[:, par], W).then_inc(m["hn_t"], 1)
                    hold(pe, m["hf_done"], g + 1)
                    halves(nc, bank(2, 2)[0:C], W.l2w, hf[:]).then_inc(m["mm"], 1)

                def second(i, par, g):
                    hold(pe, m["carry"], g + 2)
                    hold(pe, m["x3_done"], g + 2)
                    transpose_back(nc, bank(1), sums[:, par], W).then_inc(m["back"], 1)
                paired_loop(pe, GROUPS, first, second)

            @block.scalar
            def _(act):
                def first(i, par, g):
                    norm_a.act(nc, act, g, 0, na)
                    act.wait_ge(m["hn_t"], g + 1)
                    nc.scalar.activation(hf[:], bank(0), ACT.Copy).then_inc(m["hf_done"], 1)
                    act.wait_ge(m["mm"], g + 1)
                    nc.scalar.activation(msg[:, par], bank(2, 2)[0:C], ACT.Relu, bias=col["l2b"][0:C]
                                         ).then_inc(m["msg_done"], 1)
                paired_loop(act, GROUPS, first)


def edge_convolution(nc, A, sem, W, D, bank, stats):
    ctx = ExitStack()
    with ctx:
        t = lambda n, sh, dt=F32: ctx.enter_context(nc.sbuf_tensor(n, sh, dt))
        col = W.col
        near = t("l3_near", [P, 2, S], I32)
        got, xd, hn, dn = (t("l3_" + n, [P, 2, S, C]) for n in ("got", "xd", "hn", "dn"))
        neg, ended, hh = (t("l3_" + n, [C, 2, G_ROWS]) for n in ("neg", "ended", "hh"))
        nxt = t("l3_nxt", [C, 2, G_ROWS], U8)
        hf, df = t("l3_hf", [P, HALF]), t("l3_df", [P, HALF])
        na = norm_bufs(t, "l3_a")
        norm_a = Norm(sem, "l3_a", 2)
        names = ("in0", "in1", "got0", "got1", "hn_done", "hn_t", "hf_done", "mm", "ended", "carry", "hh_done", "stats", "nxt_done",
                 "st0", "st1")
        m = {n: sem("l3_" + n) for n in names}
        inn, landed, st = (m["in0"], m["in1"]), (m["got0"], m["got1"]), (m["st0"], m["st1"])
        back = lambda g: g * -1 + (GROUPS - 1)
        with nc.Block() as block:
            @block.sync
            def _(sp):
                for par in (0, 1):
                    sp.sem_inc(st[par], 16)

                def load(i, par, g):
                    sp.wait_ge(m["hh_done"], g + 1)
                    sp.dma_start(near[:, par], D.ls[back(g)]).then_inc(inn[par], 16)
                    sp.dma_start(got[:, par], group_rows(D.x2_lone)[back(g)]).then_inc(inn[par], 16)
                    sp.dma_start(xd[:, par], group_rows(D.x3d)[back(g)]).then_inc(inn[par], 16)

                def store(i, par, g):
                    sp.wait_ge(m["hh_done"], g + 3)
                    sp.dma_start(group_cols(D.hh)[back(g)], hh[:, par]).then_inc(st[par], 16)
                paired_loop(sp, GROUPS, load, store)
                for par in (0, 1):
                    sp.wait_ge(st[par], ODD_EVEN[par] + 16)

            @block.gpsimd
            def _(pool):
                def gather(i, par, g):
                    hold(pool, inn[par], i * 48 + 48)
                    gather_rows(nc, pool, D.x3d, near[:, par], got[:, par], landed[par], EP - 1)
                paired_loop(pool, GROUPS, gather)

            @block.vector
            def _(dve):
                dve.sem_inc(m["hh_done"], 2)
                nc.vector.memset(neg[:, 1, 0:1], 0.0).then_inc(m["carry"], 1)

                def first(i, par, g):
                    dve.wait_ge(inn[par], i * 48 + 48)
                    norm_a.dve(nc, dve, g, 0, xd[:, par], na)
                    nc.vector.scalar_tensor_tensor(out=dn[:, par], in0=na.xc, scalar=0.0, in1=spread(na.rstd),
                                                   op0=ALU.max, op1=ALU.mult)
                    dve.wait_ge(landed[par], i * 128 + 128)
                    norm_a.dve(nc, dve, g, 1, got[:, par], na)
                    nc.vector.scalar_tensor_tensor(out=hn[:, par], in0=na.xc, scalar=0.0, in1=spread(na.rstd),
                                                   op0=ALU.max, op1=ALU.mult).then_inc(m["hn_done"], 1)

                def second(i, par, g):
                    dve.wait_ge(m["nxt_done"], g + 1)
                    dve.wait_ge(m["mm"], g + 1)
                    nc.vector.scalar_tensor_tensor(out=ended[:, par], in0=nxt[:, par], scalar=-1.0, in1=bank(2, 2)[0:C],
                                                   op0=ALU.add, op1=ALU.mult).then_inc(m["ended"], 1)
                    dve.wait_ge(m["ended"], g + 1)
                    dve.wait_ge(m["carry"], g + 1)
                    nc.vector.tensor_tensor_scan(neg[:, par, ::-1], nxt[:, par, ::-1], ended[:, par, ::-1],
                                                 neg[:, 1 - par, 0:1], ALU.mult, ALU.add).then_inc(m["carry"], 1)
                    dve.wait_ge(m["carry"], g + 2)
                    dve.wait_ge(st[par], i * 16 + 16)
                    nc.vector.scalar_tensor_tensor(out=hh[:, par], in0=bank(4 + 2 * par, 2)[0:C],
                                                   scalar=col["l3b"][0:C], in1=neg[:, par], op0=ALU.add,
                                                   op1=ALU.subtract).then_inc(m["hh_done"], 1)
                    dve.wait_ge(m["hh_done"], g + 3)
                    for h in (0, 1):
                        at = bass.ds(back(g) * 12 + 6 * h, 6)
                        nc.vector.bn_stats(stats[:, at], hh[:, par, HALF * h:HALF * h + HALF]).then_inc(m["stats"], 1)
                paired_loop(dve, GROUPS, first, second)
                dve.wait_ge(m["stats"], 2 * GROUPS)

            @block.tensor
            def _(pe):
                def first(i, par, g):
                    hold(pe, m["hn_done"], g + 1)
                    transpose_pairs(nc, bank(1), dn[:, par], W)
                    transpose_pairs(nc, bank(0), hn[:, par], W).then_inc(m["hn_t"], 1)

                def second(i, par, g):
                    hold(pe, m["hf_done"], g + 1)
                    hold(pe, m["hh_done"], g + 2)
                    halves(nc, bank(2, 2)[0:C], W.l3ab, df[:])
                    halves(nc, bank(4 + 2 * par, 2)[0:C], W.l3b, hf[:]).then_inc(m["mm"], 1)
                
                def work(i, par, g):
                    first(i, par, g)
                    second(i, par, g)
                paired_loop(pe, GROUPS, work)

            @block.scalar
            def _(act):
                def first(i, par, g):
                    norm_a.act(nc, act, g, 0, na)
                    norm_a.act(nc, act, g, 1, na)
                    nc.scalar.activation(nxt[:, par], W.same[:, bass.ds(back(g) * G_ROWS + 1, G_ROWS)], ACT.Copy
                                         ).then_inc(m["nxt_done"], 1)
                    act.wait_ge(m["hn_t"], g + 1)
                    nc.scalar.activation(df[:], bank(1), ACT.Copy)
                    nc.scalar.activation(hf[:], bank(0), ACT.Copy).then_inc(m["hf_done"], 1)
                paired_loop(act, GROUPS, first)


def finish_rows(nc, A, sem, W, D, bank, out, stats):
    ctx = ExitStack()
    with ctx:
        t = lambda n, sh, dt=F32: ctx.enter_context(nc.sbuf_tensor(n, sh, dt))
        col = W.col
        near = t("fi_near", [P, 2, S], I32)
        xd, res = (t("fi_" + n, [P, 2, S, C]) for n in ("xd", "res"))
        hh, z, sums, count = (t("fi_" + n, [C, 2, G_ROWS]) for n in ("hh", "z", "sums", "count"))
        msg, inv, avg, ones = (t("fi_" + n, [C, G_ROWS]) for n in ("msg", "inv", "avg", "ones"))
        tail_n = EDGES % HALF
        tail = t("fi_tail", [C, tail_n])
        mv, sc = t("fi_mv", [C, 2]), t("fi_sc", [C, 4])
        names = ("tail", "bn_step", "root", "in0", "in1", "z_done", "msg_done", "carry", "counted", "inv_step", "avg_done",
                 "back", "res_done", "freed", "ids0", "ids1", "st0", "st1")
        m = {n: sem("fi_" + n) for n in names}
        inn, st, ids_in = (m["in0"], m["in1"]), (m["st0"], m["st1"]), (m["ids0"], m["ids1"])
        with nc.Block() as block:
            @block.sync
            def _(sp):
                sp.dma_start(tail[:], D.hh[:, EDGES - tail_n:EDGES]).then_inc(m["tail"], 16)

                def load(i, par, g):
                    sp.wait_ge(m["res_done"], g + 1)
                    sp.dma_start(xd[:, par], group_rows(D.x3d)[g]).then_inc(inn[par], 16)
                    sp.dma_start(hh[:, par], group_cols(D.hh)[g]).then_inc(inn[par], 16)

                def load_indices(i, par, g):
                    sp.wait_ge(m["freed"], g + 1)
                    sp.dma_start(near[:, par], D.final_idx[g]).then_inc(ids_in[par], 16)
                paired_loop(sp, GROUPS, load, load_indices)

            @block.gpsimd
            def _(pool):
                pool.sem_inc(m["freed"], 2)

                def scatter(i, par, g):
                    hold(pool, ids_in[par], i * 16 + 16)
                    hold(pool, m["res_done"], g + 3)
                    for q in range(S):
                        nc.gpsimd.indirect_dma_start(
                            out=out, out_offset=bass.IndirectOffsetOnAxis(ap=near[:, par, q:q + 1], axis=0),
                            in_=res[:, par, q], in_offset=None, bounds_check=NP_ - 1, oob_is_err=False
                        ).then_inc(st[par], 16)
                    if not (isinstance(g, int) and g == 0):
                        hold(pool, st[1 - par], i * 128 + par * 128)
                        pool.sem_inc(m["freed"], 1)
                paired_loop(pool, GROUPS, scatter)
                for par in (0, 1):
                    pool.wait_ge(st[par], 8 * ODD_EVEN[par])

            @block.vector
            def _(dve):
                n = [0]

                def done(ins):
                    n[0] += 1
                    ins.then_inc(m["bn_step"], 1)

                def wait():
                    dve.wait_ge(m["bn_step"], n[0])
                dve.sem_inc(m["res_done"], 2)
                done(nc.vector.memset(ones[:], 1.0))
                done(nc.vector.memset(sums[:, 1, G_ROWS - 1:G_ROWS], 0.0))
                done(nc.vector.memset(count[:, 1, G_ROWS - 1:G_ROWS], 0.0))
                dve.wait_ge(m["tail"], 16)
                at = 6 * ((EDGES - tail_n) // HALF)
                done(nc.vector.bn_stats(stats[:, at:at + 6], tail[:]))
                wait()
                done(nc.vector.bn_aggr(mv[:], stats[:, 0:at + 6]))
                wait()
                done(nc.vector.tensor_scalar(sc[:, 0:1], mv[:, 1:2], EPS, None, ALU.add))
                dve.wait_ge(m["root"], 1)
                done(nc.vector.reciprocal(sc[:, 0:1], sc[:, 1:2]))
                wait()
                done(nc.vector.tensor_tensor(sc[:, 2:3], sc[:, 0:1], col["bn_gamma"][0:C], ALU.mult))
                wait()
                done(nc.vector.tensor_tensor(sc[:, 3:4], mv[:, 0:1], sc[:, 2:3], ALU.mult))
                wait()
                done(nc.vector.tensor_tensor(sc[:, 3:4], col["bn_beta"][0:C], sc[:, 3:4], ALU.subtract))
                wait()
                dve.sem_inc(m["carry"], 1)
                dve.sem_inc(m["counted"], 1)
                assert n[0] == BN_STEPS

                def first(i, par, g):
                    dve.wait_ge(m["counted"], g + 1)
                    nc.vector.tensor_tensor_scan(count[:, par], W.same[:, bass.ds(g * G_ROWS, G_ROWS)], ones[:],
                                                 count[:, 1 - par, G_ROWS - 1:G_ROWS], ALU.mult, ALU.add
                                                 ).then_inc(m["counted"], 1)
                    dve.wait_ge(m["z_done"], g + 1)
                    nc.vector.scalar_tensor_tensor(out=msg[:], in0=z[:, par], scalar=0.3, in1=z[:, par], op0=ALU.mult,
                                                   op1=ALU.max).then_inc(m["msg_done"], 1)
                    dve.wait_ge(m["counted"], g + 2)
                    nc.vector.reciprocal(inv[:], count[:, par]).then_inc(m["inv_step"], 1)
                    dve.wait_ge(m["msg_done"], g + 1)
                    dve.wait_ge(m["carry"], g + 1)
                    run_sums(nc, W, g, par, msg[:], sums, m)
                    dve.wait_ge(m["carry"], g + 2)
                    if not (isinstance(g, int) and g == 0):
                        dve.wait_ge(m["back"], g)
                    nc.vector.tensor_tensor(avg[:], sums[:, par], inv[:], ALU.mult).then_inc(m["avg_done"], 1)

                def second(i, par, g):
                    dve.wait_ge(inn[par], i * 32 + 32)
                    dve.wait_ge(m["freed"], g + 1)
                    dve.wait_ge(m["back"], g + 1)
                    nc.vector.tensor_tensor(res[:, par], xd[:, par], as_rows(bank(par)), ALU.add
                                            ).then_inc(m["res_done"], 1)
                paired_loop(dve, GROUPS, first, second)

            @block.tensor
            def _(pe):
                def work(i, par, g):
                    hold(pe, m["avg_done"], g + 1)
                    transpose_back(nc, bank(par), avg[:], W).then_inc(m["back"], 1)
                paired_loop(pe, GROUPS, work)

            @block.scalar
            def _(act):
                act.wait_ge(m["bn_step"], 6)
                nc.scalar.activation(sc[:, 1:2], sc[:, 0:1], ACT.Sqrt).then_inc(m["root"], 1)
                act.wait_ge(m["bn_step"], BN_STEPS)

                def work(i, par, g):
                    act.wait_ge(inn[par], i * 32 + 32)
                    if not (isinstance(g, int) and g == 0):
                        act.wait_ge(m["avg_done"], g)
                    nc.scalar.activation(z[:, par], hh[:, par], ACT.Identity, bias=sc[:, 3:4], scale=sc[:, 2:3]
                                         ).then_inc(m["z_done"], 1)
                paired_loop(act, GROUPS, work)


def lay_out(inputs):
    import numpy as np
    a = {k: np.ascontiguousarray(v) for k, v in inputs.items()}
    src, dst = a.pop("src").astype(np.int32), a.pop("dst").astype(np.int32)
    ew, ea, x = a.pop("edge_weight"), a.pop("edge_attr_32"), a.pop("x")

    def padded(v, fill):
        return np.concatenate([v, np.full((EP - EDGES,) + v.shape[1:], fill, v.dtype)])

    def rows(v):
        return np.ascontiguousarray(v.reshape(GROUPS, 2, S // 2, P).transpose(0, 3, 2, 1).reshape(GROUPS, P, S))

    end = np.array([-2], np.int32)
    dp = padded(dst, NODES)
    a["src_rows"], a["dst_rows"] = rows(padded(src, 0)), rows(dp)
    a["next_rows"] = rows(np.concatenate([dp[1:], end]))
    a["ew_rows"] = rows(padded(ew, 0))
    a["dst_line"] = np.concatenate([end, dp, end])[None]
    a["ea_cols"] = np.ascontiguousarray(padded(ea, 0).T)
    a["x"] = np.concatenate([x, np.zeros((NP_ - NODES, C), x.dtype)])
    a["l3_wt"] = np.ascontiguousarray(a.pop("L3_gnn_W").T)
    return a


def kernel(**inputs):
    import concourse.bacc as bacc
    from concourse.bass_utils import run_bass_kernel_spmd
    arrays = lay_out(inputs)
    nc = bacc.Bacc("TRN2", target_bir_lowering=False, num_devices=1)
    args = {n: nc.dram_tensor("in_" + n, v.shape, mybir.dt.from_np(v.dtype), kind="ExternalInput").ap()
            for n, v in arrays.items()}
    out = nc.dram_tensor("out_0", (NP_, C), F32, kind="ExternalOutput").ap()
    build(nc, args, out)
    r = run_bass_kernel_spmd(nc, [{"in_" + n: v for n, v in arrays.items()}], core_ids=[0])
    return r.results[0]["out_0"][:NODES]
```

```python
from contextlib import ExitStack
import concourse.bass as bass
from concourse import mybir

ALU = mybir.AluOpType
ACT = mybir.ActivationFunctionType
F32 = mybir.dt.float32
I32 = mybir.dt.int32
BF16 = mybir.dt.bfloat16
F16 = mybir.dt.float16
U8 = mybir.dt.uint8
AX_X = mybir.AxisListType.X

P = 128
C = 64
S = 8
G_ROWS = P * S
HALF = G_ROWS // 2
EDGES, NODES = 50000, 100000
GROUPS = -(-EDGES // G_ROWS)
EP = GROUPS * G_ROWS
NODE_GROUPS = -(-NODES // G_ROWS)
NP_ = NODE_GROUPS * G_ROWS
TILES = GROUPS * S
HEADS = 4
EDIM = 32
LO_BITS = 10
LO = 1 << LO_BITS
HI = NP_ // LO
NOWHERE = 1.0e6
FAR = 1.0e30
EPS = 1e-5
PARTS = 5
CHUNK = EP // P
ALPHAS = 2 * HEADS + 1
EXCHANGES = (HEADS, HEADS, HEADS, HEADS + 1, HEADS)
BN_STEPS = 9
PREP_STEPS = 22
ODD_EVEN = (16 * ((GROUPS + 1) // 2), 16 * (GROUPS // 2))
RING = 4


def of_slot(r, n):
    return (n - r + RING - 1) // RING


def take_turns(stages):
    due = [(0, k, gen) for k, gen in enumerate(stages)]
    while due:
        due.sort(key=lambda x: x[:2])
        t, k, gen = due.pop(0)
        nxt = next(gen, None)
        if nxt is not None:
            assert nxt >= t, (nxt, t)
            due.append((nxt, k, gen))


def ring_loop(eng, n, *lags):
    k_max = len(lags) + 1
    assert n > k_max + RING

    def step(group_of):
        started = []
        for k, stages in enumerate(lags):
            at = group_of(k)
            if at is not None:
                started += [s for s in (f(*at) for f in stages) if s is not None]
        take_turns(started)

    def fixed(s):
        def at(k):
            g = s - k
            return (g // RING, g % RING, g) if 0 <= g < n else None
        step(at)

    for s in range(k_max):
        fixed(s)
    turns = (n - k_max) // RING
    with eng.Fori(0, turns) as i:
        for q in range(RING):
            def at(k):
                off = k_max + q - k
                return i + off // RING, off % RING, i * RING + off
            step(at)
    for s in range(k_max + RING * turns, n + len(lags) - 1):
        fixed(s)


def hold(eng, sem, value):
    if not (isinstance(value, int) and value < 1):
        eng.wait_ge(sem, value)
        eng.sem_inc(HELD[0], 1)


def after(eng, sem, value):
    if not (isinstance(value, int) and value < 1):
        eng.wait_ge(sem, value)


def half_turns(i, r):
    return i * 2 + r // 2


HELD = [None]


class Norm:

    def __init__(self, sem, t, name, per=1):
        self.per = per
        self.step, self.centred, self.squared, self.varied, self.rooted = (
            sem(f"{name}_{n}") for n in ("dve_step", "centred", "squared", "variance", "rooted"))
        self.xc, self.sq = t(name + "_xc", [P, S, C])[:], t(name + "_sq", [P, S, C])[:]
        self.mean, self.var, self.sd, self.rstd = (t(f"{name}_{n}", [P, S])[:] for n in ("mean", "var", "sd", "rstd"))

    def dve(self, nc, dve, g, k, x, t=0):
        n = g * self.per + k
        yield t
        nc.vector.reduce_sum(self.mean, x, AX_X).then_inc(self.step, 1)
        yield t + 1
        dve.wait_ge(self.step, n * 4 + 1)
        nc.vector.tensor_scalar(self.mean, self.mean, -1.0 / C, None, ALU.mult).then_inc(self.step, 1)
        yield t + 2
        dve.wait_ge(self.step, n * 4 + 2)
        nc.vector.tensor_tensor(self.xc, x, spread(self.mean), ALU.add).then_inc(self.centred, 1)
        yield t + 4
        dve.wait_ge(self.squared, n + 1)
        nc.vector.reduce_sum(self.var, self.sq, AX_X).then_inc(self.step, 1)
        yield t + 5
        dve.wait_ge(self.step, n * 4 + 3)
        nc.vector.tensor_scalar(self.var, self.var, 1.0 / C, EPS, ALU.mult, ALU.add).then_inc(self.varied, 1)
        yield t + 7
        dve.wait_ge(self.rooted, n + 1)
        nc.vector.reciprocal(self.rstd, self.sd).then_inc(self.step, 1)
        yield t + 8
        dve.wait_ge(self.step, n * 4 + 4)

    def act(self, nc, act, g, k, t=0):
        n = g * self.per + k
        yield t + 3
        act.wait_ge(self.centred, n + 1)
        nc.scalar.activation(self.sq, self.xc, ACT.Square).then_inc(self.squared, 1)
        yield t + 6
        act.wait_ge(self.varied, n + 1)
        nc.scalar.activation(self.sd, self.var, ACT.Sqrt).then_inc(self.rooted, 1)


class NormTwice:

    def __init__(self, sem, t, name):
        self.step, self.centred, self.relu, self.squared, self.varied, self.rooted = (
            sem(f"{name}_{n}") for n in ("dve_step", "centred", "relu", "squared", "variance", "rooted"))
        self.xc = t(name + "_xc", [P, S, C])[:]
        self.three = t(name + "_three", [P, 3, S, C])[:]
        self.y = self.three[:, 1]
        self.mean, self.my, self.my2, self.vy = (t(f"{name}_{n}", [P, S])[:] for n in ("mean", "my", "my2", "vy"))
        self.sums = t(name + "_sums", [P, 3, S])[:]
        self.var, self.sd, self.inv = (t(f"{name}_{n}", [P, 2, S])[:] for n in ("var", "sd", "inv"))
        self.first, self.gain = self.inv[:, 0], self.inv[:, 1]

    def dve(self, nc, dve, g, x, t=0):
        yield t
        nc.vector.reduce_sum(self.mean, x, AX_X).then_inc(self.step, 1)
        yield t + 1
        dve.wait_ge(self.step, g * 7 + 1)
        nc.vector.tensor_scalar(self.mean, self.mean, -1.0 / C, None, ALU.mult).then_inc(self.step, 1)
        yield t + 2
        dve.wait_ge(self.step, g * 7 + 2)
        nc.vector.tensor_tensor(self.xc, x, spread(self.mean), ALU.add).then_inc(self.centred, 1)
        yield t + 5
        dve.wait_ge(self.squared, g + 1)
        nc.vector.reduce_sum(self.sums, self.three, AX_X).then_inc(self.step, 1)
        yield t + 6
        dve.wait_ge(self.step, g * 7 + 3)
        nc.vector.tensor_scalar(self.var[:, 0], self.sums[:, 0], 1.0 / C, EPS, ALU.mult, ALU.add)
        nc.vector.tensor_scalar(self.my, self.sums[:, 1], 1.0 / C, None, ALU.mult).then_inc(self.step, 1)
        yield t + 7
        dve.wait_ge(self.step, g * 7 + 4)
        nc.vector.tensor_tensor(self.my2, self.my, self.my, ALU.mult).then_inc(self.step, 1)
        yield t + 8
        dve.wait_ge(self.step, g * 7 + 5)
        nc.vector.scalar_tensor_tensor(out=self.vy, in0=self.sums[:, 2], scalar=1.0 / C, in1=self.my2, op0=ALU.mult,
                                       op1=ALU.subtract).then_inc(self.step, 1)
        yield t + 9
        dve.wait_ge(self.step, g * 7 + 6)
        nc.vector.scalar_tensor_tensor(out=self.var[:, 1], in0=self.var[:, 0], scalar=EPS, in1=self.vy, op0=ALU.mult,
                                       op1=ALU.add).then_inc(self.varied, 1)
        yield t + 11
        dve.wait_ge(self.rooted, g + 1)
        nc.vector.reciprocal(self.inv, self.sd).then_inc(self.step, 1)
        yield t + 12
        dve.wait_ge(self.step, g * 7 + 7)

    def act(self, nc, act, g, t=0):
        yield t + 3
        act.wait_ge(self.centred, g + 1)
        nc.scalar.activation(self.y, self.xc, ACT.Relu).then_inc(self.relu, 1)
        nc.scalar.activation(self.three[:, 0], self.xc, ACT.Square)
        yield t + 4
        act.wait_ge(self.relu, g + 1)
        nc.scalar.activation(self.three[:, 2], self.y, ACT.Square).then_inc(self.squared, 1)
        yield t + 10
        act.wait_ge(self.varied, g + 1)
        nc.scalar.activation(self.sd, self.var, ACT.Sqrt).then_inc(self.rooted, 1)


def paired_loop(eng, n, first, second=None):
    def two(f, i, par):
        f(i, par, i * 2 + par)

    def step(i):
        two(first, i, 1)
        if second:
            two(second, i, 0)
        two(first, i + 1, 0)
        if second:
            two(second, i, 1)

    two(first, 0, 0)
    pairs = (n - 1) // 2
    with eng.Fori(0, pairs) as i:
        step(i)
    if n % 2 == 0:
        two(first, pairs, 1)
    if second:
        two(second, pairs, 0)
        if n % 2 == 0:
            two(second, pairs, 1)


def group_rows(a):
    return a.rearrange("(g p s) c -> g p s c", p=P, s=S)


def group_cols(a):
    return a.rearrange("f (g e) -> g f e", e=G_ROWS)


def slot_cols(n):
    at = (n % 2) * HALF + (n // 2) * P
    return slice(at, at + P)


def transpose_rows(nc, out, rows, W):
    for n in range(S):
        last = nc.tensor.transpose(out[0:C, slot_cols(n)], rows[:, n], W.ident[:])
    return last


def transpose_pairs(nc, out, rows, W):
    flat = rows.rearrange("p s c -> p (s c)")
    for n in range(S // 2):
        last = nc.tensor.transpose(out[:, P * n:P * n + P], flat[:, P * n:P * n + P], W.ident[:])
    return last


def transpose_back(nc, out, columns, W):
    for n in range(S):
        last = nc.tensor.transpose(out[:, C * n:C * n + C], columns[:, slot_cols(n)], W.ident[0:C, 0:C])
    return last


def halves(nc, out, weights, paired):
    for h in (0, 1):
        last = nc.tensor.matmul(out[:, HALF * h:HALF * h + HALF], weights[:, h], paired, start=True, stop=True)
    return last


def leaky_parts(nc, out, x, slope, bias=None, rest=None):
    b = dict(bias=bias) if bias is not None else {}
    r = dict(bias=rest) if rest is not None else {}
    nc.scalar.activation(out[0], x, ACT.Identity, scale=slope, **b)
    return nc.scalar.activation(out[1], x, ACT.Relu, scale=1.0 - slope, **r)


def sum_transposed(nc, out, parts, W, n):
    k = parts[0].shape[0]
    for q in range(n):
        at = slice(P * q, P * q + P) if n < S else slot_cols(q)
        for j in (0, 1):
            last = nc.tensor.matmul(out[:, k * q:k * q + k], parts[j][:, at], W.ident[0:k, 0:k],
                                    start=j == 0, stop=j == 1)
    return last


def as_rows(x):
    return x.rearrange("p (s c) -> p s c", c=C)


def spread(v):
    return v.unsqueeze(2).to_broadcast([P, S, C])


def along(v):
    return v.unsqueeze(1).to_broadcast([P, S, C])


class Bufs:
    pass


def build(nc, A, out):
    ctx = ExitStack()
    with ctx:
        def sb(name, shape, dt=F32):
            return ctx.enter_context(nc.sbuf_tensor(name, shape, dt))

        def sem(name):
            return ctx.enter_context(nc.semaphore(name))

        def dram(name, shape, dt=F32):
            return nc.dram_tensor(name, shape, dt, kind=KIND).ap()

        KIND = "Internal"
        ps = ctx.enter_context(nc.psum_tensor("ps", [P, 4096], F32))
        bank = lambda n, k=1: ps[:, 512 * n:512 * (n + k)]

        D = Bufs()
        (D.xs, D.xd, D.t0s, D.h_lone, D.x1_lone, D.x2_lone, D.tx1, D.hd, D.hs, D.x1d, D.x2d, D.x3d) = (
            dram("d_" + name, (EP, C)) for name in
            ("xs", "xd", "t0s", "h_lone", "x1_lone", "x2_lone", "tx1", "hd", "hs", "x1d", "x2d", "x3d"))
        D.table = dram("d_table", (NP_, 2))
        D.ls = dram("d_ls", (GROUPS, P, S), I32)
        D.final_idx = dram("d_final_idx", (GROUPS, P, S), I32)
        D.et = dram("d_et", (C, EP))
        D.pd = dram("d_pd", (C, EP))
        D.hh = dram("d_hh", (C, EP))
        D.att_s = dram("d_att_s", (HEADS, EP))
        D.att_d = dram("d_att_d", (2 * HEADS, EP))
        D.alpha = dram("d_alpha", (ALPHAS, EP))
        grp = lambda a: a.rearrange("(g p s) c -> g p s c", p=P, s=S)
        cols = lambda a: a.rearrange("f (g e) -> g f e", e=G_ROWS)

        W = Bufs()
        W.ident = sb("ident", [P, P])
        W.w02 = sb("w02", [P, P])
        W.w1 = sb("w1", [C, C])
        W.w2x2 = sb("w2x2", [C, C])
        W.gmean = sb("gmean", [P, P])
        W.gatw = sb("gatw", [P, 2, C])
        W.att = sb("att", [C, 2, HEADS])
        W.att_half = sb("att_half", [P, 2, HEADS])
        W.w1n = sb("w1n", [P, 2, P])
        W.w2n = sb("w2n", [P, C])
        W.w1e = sb("w1e", [EDIM, C])
        W.w2e = sb("w2e", [C, C])
        W.l2w = sb("l2w", [P, 2, C])
        W.l3b = sb("l3b", [P, 2, C])
        W.l3ab = sb("l3ab", [P, 2, C])
        W.vecs = sb("vecs", [P, 16])
        VEC = ("cheb_b", "gat_b", "b1n", "b1e", "ln_gamma", "ln_beta", "b2n", "b2e", "dp", "res", "l2b",
               "l3b", "bn_gamma", "bn_beta")
        W.slanted = sb("slanted", [P, 2, 4])
        col = {n: W.vecs[:, i:i + 1] for i, n in enumerate(VEC)}
        for i, n in enumerate(VEC[:4]):
            col[n + "_slope"], col[n + "_rest"] = W.slanted[:, 0, i:i + 1], W.slanted[:, 1, i:i + 1]
        W.rows = sb("rowvecs", [P, 4, C])
        W.idsE = sb("idsE", [P, 2 * GROUPS, S], I32)
        srcE, dstE = W.idsE[:, 0:GROUPS], W.idsE[:, GROUPS:2 * GROUPS]
        W.countE = sb("countE", [P, GROUPS, S])
        lastE = sb("lastE", [P, GROUPS, S])
        ewE = sb("ewE", [P, GROUPS, S])
        wE = sb("wE", [P, GROUPS, S])
        same = sb("same", [C, EP + 1], U8)

        with ExitStack() as loc:
            t = lambda n, sh, dt=F32: loc.enter_context(nc.sbuf_tensor(n, sh, dt))
            loaded, stepped, consts, masks_in0, masks_in1, masks_used = map(sem, (
                "weights_loaded", "prep_step", "pool_consts", "masks_loaded0", "masks_loaded1", "masks_used"))
            gw2 = t("gw2", [P, HEADS, C])
            chw = t("chw", [P, 3, C])
            attb = t("attb", [C, 2, HEADS, C])
            prod = t("attprod", [C, 2, HEADS, C])
            dnE = t("dnE", [P, GROUPS, S], I32)
            idx0 = t("finidx", [P, GROUPS, S])
            idx0i = t("finidxi", [P, GROUPS, S], I32)
            l3a = t("l3a", [P, C])
            pairrow = t("pairrow", [C, 2, 2, G_ROWS], I32)
            linear = A["dst_line"]
            n_loads = [0]
            fin_st = sem("final_idx_stored")
            with nc.Block() as block:
                @block.sync
                def _(sp):
                    def ld(o, i):
                        n_loads[0] += 1
                        sp.dma_start(o, i).then_inc(loaded, 16)
                    sp.wait_ge(consts, 1)
                    for h in (0, 1):
                        lanes = slice(C * h, C * h + C)
                        ld(gw2[lanes], A["L0_gnn_gat_w"].rearrange("k (h f) -> k h f", h=HEADS))
                        ld(chw[lanes], A["L0_gnn_cheb_w"].rearrange("k i o -> i k o"))
                        ld(W.w1n[lanes, h, :], A["L1_gnn_W1n"])
                        ld(W.l2w[lanes, h, :], A["L2_gnn_W"])
                        ld(W.l3b[lanes, h, :], A["l3_wt"][C:2 * C, :])
                        ld(l3a[lanes], A["l3_wt"][0:C, :])
                        for n, name in (("ln_gamma", "L0_gnn_ln_gamma"), ("ln_beta", "L0_gnn_ln_beta"),
                                        ("cheb_b", "L0_gnn_cheb_b"), ("gat_b", "L0_gnn_gat_b"),
                                        ("b2n", "L1_gnn_b2n"), ("b1e", "L1_gnn_b1e"), ("b2e", "L1_gnn_b2e"),
                                        ("l2b", "L2_gnn_b"), ("l3b", "L3_gnn_b"),
                                        ("bn_gamma", "L3_gnn_gamma"), ("bn_beta", "L3_gnn_beta")):
                            ld(col[n][lanes], A[name].rearrange("(c a) -> c a", a=1))
                    ld(col["b1n"], A["L1_gnn_b1n"].rearrange("(c a) -> c a", a=1))
                    ld(col["dp"], A["L1_gnn_dp_scale"].rearrange("(c a) -> c a", a=1).to_broadcast([P, 1]))
                    ld(col["res"], A["L1_gnn_res_w"].rearrange("(c a) -> c a", a=1).to_broadcast([P, 1]))
                    ld(W.w1[:], A["L0_gnn_cheb_w"][1])
                    ld(W.w2x2[:], A["L0_gnn_cheb_w"][2])
                    for q in (0, 1):
                        ld(W.gatw[C * q:C * q + C], A["L0_gnn_gat_w"].rearrange("k (a b f) -> b k a f", a=2, b=2)[q])
                    for q, name in enumerate(("L0_gnn_att_src", "L0_gnn_att_dst")):
                        ld(attb[:, q], A[name].unsqueeze(0).to_broadcast([C, HEADS, C]))
                    ld(W.w2n[:], A["L1_gnn_W2n"])
                    ld(W.w1e[:], A["L1_gnn_W1e"])
                    ld(W.w2e[:], A["L1_gnn_W2e"])
                    for q, name in enumerate(("L0_gnn_ln_gamma", "L0_gnn_ln_beta", "L1_gnn_gamma", "L1_gnn_beta")):
                        ld(W.rows[:, q], A[name].unsqueeze(0).to_broadcast([P, C]))
                    ld(srcE[:], A["src_rows"].rearrange("g p s -> p g s"))
                    ld(dstE[:], A["dst_rows"].rearrange("g p s -> p g s"))
                    ld(dnE[:], A["next_rows"].rearrange("g p s -> p g s"))
                    ld(ewE[:], A["ew_rows"].rearrange("g p s -> p g s"))

                    def load(i, par, g):
                        sp.wait_ge(masks_used, g + 1)
                        for q in (0, 1):
                            at = g * G_ROWS + (1 - q)
                            sp.dma_start(pairrow[:, par, q], linear[:, bass.ds(at, G_ROWS)].to_broadcast([C, G_ROWS])
                                         ).then_inc((masks_in0, masks_in1)[par], 16)
                    paired_loop(sp, GROUPS, load)
                    sp.wait_ge(stepped, PREP_STEPS)
                    sp.dma_start(D.final_idx.rearrange("g p s -> p g s"), idx0i[:]).then_inc(fin_st, 16)
                    sp.wait_ge(fin_st, 16)

                @block.gpsimd
                def _(pool):
                    for x in (W.w02, W.gmean, W.w1n, W.l2w, W.l3b, W.l3ab, W.att_half, W.vecs):
                        last = nc.gpsimd.memset(x[:], 0.0)
                    last.then_inc(consts, 1)
                    nc.gpsimd.memset(W.ident[:], 0.0).then_inc(consts, 1)
                    pool.wait_ge(consts, 2)
                    nc.gpsimd.affine_select(out=W.ident[:], in_=W.ident[:], compare_op=ALU.not_equal, fill=1.0,
                                            base=0, pattern=[[-1, P]], channel_multiplier=1).then_inc(consts, 1)

                @block.vector
                def _(dve):
                    dve.sem_inc(masks_used, 2)
                    n = [0]

                    def done(ins):
                        n[0] += 1
                        ins.then_inc(stepped, 1)

                    def wait():
                        dve.wait_ge(stepped, n[0])
                    dve.wait_ge(loaded, 16 * n_loads[0])
                    dve.wait_ge(consts, 1)
                    for h in (0, 1):
                        lanes, out_cols = slice(C * h, C * h + C), slice(C * h, C * h + C)
                        done(nc.vector.tensor_tensor(W.w02[lanes, out_cols], chw[lanes, 0], chw[lanes, 2], ALU.subtract))
                        done(nc.vector.tensor_tensor(W.l3ab[lanes, h], l3a[lanes], W.l3b[lanes, h], ALU.subtract))
                        done(nc.vector.reduce_sum(W.gmean[lanes, out_cols], gw2[lanes].rearrange("k h f -> k f h"), AX_X))
                    for at, slope in ((0, 0.01), (2, 0.1)):
                        for k, f in enumerate((slope, 1.0 - slope)):
                            done(nc.vector.tensor_scalar(W.slanted[:, k, at:at + 2], W.vecs[:, at:at + 2], f, None, ALU.mult))
                    wait()
                    done(nc.vector.tensor_scalar(W.gmean[:], W.gmean[:], 1.0 / HEADS, None, ALU.mult))
                    done(nc.vector.tensor_scalar(W.gatw[:], W.gatw[:], 1.0 / HEADS, None, ALU.mult))
                    done(nc.vector.tensor_scalar(W.w2x2[:], W.w2x2[:], 2.0, None, ALU.mult))
                    for q in (0, 1):
                        done(nc.vector.tensor_tensor(prod[:, q], gw2[0:C], attb[:, q], ALU.mult))
                    wait()
                    for q in (0, 1):
                        done(nc.vector.reduce_sum(W.att[:, q], prod[:, q], AX_X))
                    wait()
                    done(nc.vector.tensor_copy(W.att_half[0:C, 0], W.att[:, 0]))
                    done(nc.vector.tensor_copy(W.att_half[C:P, 1], W.att[:, 0]))
                    done(nc.vector.tensor_tensor(lastE[:], dstE[:], dnE[:], ALU.not_equal))
                    wait()
                    done(nc.vector.tensor_scalar(idx0[:], lastE[:], -NOWHERE, NOWHERE, ALU.mult, ALU.add))
                    wait()
                    done(nc.vector.tensor_tensor(idx0i[:], idx0[:], dstE[:], ALU.add))
                    wait()
                    assert n[0] == PREP_STEPS, n[0]
                    nc.vector.memset(same[:, EP:EP + 1], 0)

                    def mask(i, par, g):
                        dve.wait_ge((masks_in0, masks_in1)[par], i * 32 + 32)
                        nc.vector.tensor_tensor(same[:, bass.ds(g * G_ROWS, G_ROWS)], pairrow[:, par, 0],
                                                pairrow[:, par, 1], ALU.is_equal).then_inc(masks_used, 1)
                    paired_loop(dve, GROUPS, mask)
        def phase(part, *args):
            own = []

            def new(name):
                own.append(nc.alloc_semaphore(name=name))
                return own[-1]
            HELD[0] = new("held_" + part.__name__)
            part(nc, A, new, *args)
            nc.clear_and_free_semaphores(own)
            nc.all_engine_barrier()

        W.col, W.ewE, W.wE, W.same = col, ewE, wE, same
        W.cm, W.w02c, W.cm0, W.cm1, W.gamma1 = (sb(n, [P, P]) for n in ("cm", "w02c", "cm0", "cm1", "gamma1"))
        W.b2e_dp = sb("b2e_dp", [P, 1])
        W.base_b, W.base_slanted = sb("base_b", [P, 1]), sb("base_slanted", [P, 2])
        W.ones_row, W.beta_rows = sb("ones_row", [1, P]), sb("beta_rows", [1, 2, P // C * 4, C])
        phase(fold_norms, W, D, bank)
        phase(degrees, W, D, bank, srcE, dstE, lastE, ewE)
        phase(lone_states, W, D, bank, out)
        phase(first_propagation, W, D, bank)
        phase(second_propagation, W, D, bank)
        phase(attention_sources, W, D, bank)
        phase(edge_terms, W, D, bank)
        phase(attention_weights, W, D, bank)
        phase(attention_sums, W, D, bank)
        phase(gated_messages, W, D, bank)
        phase(relu_messages, W, D, bank)
        stats = sb("bn_stats", [C, 2 * GROUPS * 6])
        phase(edge_convolution, W, D, bank, stats)
        phase(finish_rows, W, D, bank, out, stats)


def degrees(nc, A, sem, W, D, bank, srcE, dstE, lastE, ewE):
    ctx = ExitStack()
    with ctx:
        t = lambda n, sh, dt=F32: ctx.enter_context(nc.sbuf_tensor(n, sh, dt))
        hiS, loS, hiD, loD = (t(n, [P, GROUPS, S]) for n in ("hiS", "loS", "hiD", "loD"))
        posI, tmpI = t("posI", [P, GROUPS, S], I32), t("tmpI", [P, GROUPS, S], I32)
        posF, rem = t("posF", [P, GROUPS, S]), t("rem", [P, GROUPS, S])
        part = t("part", [P, GROUPS, S])
        vals = t("vals", [P, GROUPS, S, PARTS], BF16)
        iota_i = t("iota_i", [P, LO], I32)
        iota_hi = t("iota_hi", [P, P], BF16)
        iota_lo = t("iota_lo", [P, LO], F16)
        hot_w = t("hot_w", [P, 2, 3, P], BF16)
        hot_p = t("hot_p", [P, 2, 2, P], BF16)
        hot_lo = t("hot_lo", [P, 2, 2, LO], BF16)
        zero = t("zero_bf", [P, P], BF16)
        deg = t("deg", [P, LO])
        msk = t("degmask", [P, LO])
        tab = t("tab", [P, LO, 2])
        rows = t("gathered", [P, 2, S, C])
        near = [t(f"near{k}", [P, 2, S], I32) for k in (0, 1)]
        (pool_ready, dstep, guarded, hots, products, rooted, table_st, g_in0, g_in1, st0, st1) = map(sem, (
            "iotas", "degree_step", "degree_guarded", "onehots_built", "products_done", "degree_rooted", "table_stored",
            "rows_gathered0", "rows_gathered1", "rows_stored0", "rows_stored1"))
        gin, st = (g_in0, g_in1), (st0, st1)
        id_in = (sem("indices_loaded0"), sem("indices_loaded1"))
        grp = lambda a: a.rearrange("(g p s) c -> g p s c", p=P, s=S)
        N_STEPS = []
        with nc.Block() as block:
            @block.gpsimd
            def _(pool):
                nc.gpsimd.iota(posI[:], pattern=[[G_ROWS, GROUPS], [1, S]], base=1, channel_multiplier=S)
                nc.gpsimd.iota(iota_i[:], pattern=[[1, LO]], base=0, channel_multiplier=0)
                nc.gpsimd.memset(zero[:], 0.0).then_inc(pool_ready, 1)
                for k, ids in enumerate((near[0], near[1])):
                    def gather(i, par, g):
                        hold(pool, id_in[par], i * 16 + k * ODD_EVEN[par] + 16)
                        hold(pool, st[par], i * 16 + k * ODD_EVEN[par] + 16)
                        for q in range(S):
                            pool.indirect_dma_start(
                                out=rows[:, par, q], out_offset=None, in_=A["x"],
                                in_offset=bass.IndirectOffsetOnAxis(ap=ids[:, par, q:q + 1], axis=0),
                                bounds_check=NP_ - 1, oob_is_err=False).then_inc(gin[par], 16)
                    paired_loop(pool, GROUPS, gather)

            @block.vector
            def _(dve):
                n = [0]

                def done(ins):
                    n[0] += 1
                    ins.then_inc(dstep, 1)

                def wait():
                    dve.wait_ge(dstep, n[0])
                dve.wait_ge(pool_ready, 1)
                done(nc.vector.tensor_copy(iota_hi[:], iota_i[:, 0:P]))
                done(nc.vector.tensor_copy(iota_lo[:], iota_i[:]))
                for ids, hi, lo in ((srcE, hiS, loS), (dstE, hiD, loD)):
                    done(nc.vector.tensor_scalar(tmpI[:], ids[:], LO_BITS, None, ALU.logical_shift_right))
                    wait()
                    done(nc.vector.tensor_copy(hi[:], tmpI[:]))
                    wait()
                    done(nc.vector.tensor_scalar(tmpI[:], ids[:], LO - 1, None, ALU.bitwise_and))
                    wait()
                    done(nc.vector.tensor_copy(lo[:], tmpI[:]))
                    wait()
                done(nc.vector.tensor_copy(rem[:], ewE[:]))
                for k in range(3):
                    wait()
                    done(nc.vector.tensor_copy(vals[:, :, :, k], rem[:]))
                    wait()
                    if k < 2:
                        done(nc.vector.tensor_copy(part[:], vals[:, :, :, k]))
                        wait()
                        done(nc.vector.tensor_tensor(rem[:], rem[:], part[:], ALU.subtract))
                for k, (bits) in enumerate((0xFF00, 0xFF)):
                    done(nc.vector.tensor_scalar(tmpI[:], posI[:], bits, None, ALU.bitwise_and))
                    wait()
                    done(nc.vector.tensor_copy(posF[:], tmpI[:]))
                    wait()
                    done(nc.vector.tensor_tensor(vals[:, :, :, 3 + k], posF[:], lastE[:], ALU.mult))
                wait()
                hs, ls, hd, ld = (x[:].rearrange("p g s -> p (g s)") for x in (hiS, loS, hiD, loD))
                v = vals[:].rearrange("p g s k -> p (g s) k")
                wide = lambda x, k: x.unsqueeze(1).to_broadcast([P, k, P])
                dve.sem_inc(products, 2)

                def hot(i, par, tile):
                    dve.wait_ge(products, tile + 1)
                    one = bass.ds(tile, 1)
                    vt = v[:, one, :].rearrange("p a k -> p (a k)")
                    nc.vector.scalar_tensor_tensor(
                        out=hot_w[:, par], in0=wide(iota_hi[:], 3), scalar=hs[:, one],
                        in1=vt[:, 0:3].unsqueeze(2).to_broadcast([P, 3, P]), op0=ALU.is_equal, op1=ALU.mult)
                    nc.vector.scalar_tensor_tensor(
                        out=hot_p[:, par], in0=wide(iota_hi[:], 2), scalar=hd[:, one],
                        in1=vt[:, 3:5].unsqueeze(2).to_broadcast([P, 2, P]), op0=ALU.is_equal, op1=ALU.mult)
                    nc.vector.tensor_scalar(hot_lo[:, par, 0], iota_lo[:], ls[:, one], None, ALU.is_equal)
                    nc.vector.tensor_scalar(hot_lo[:, par, 1], iota_lo[:], ld[:, one], None,
                                            ALU.is_equal).then_inc(hots, 1)
                paired_loop(dve, TILES, hot)
                dve.wait_ge(products, TILES + 3)
                done(nc.vector.tensor_scalar(msk[:], bank(0, 2), 0.0, None, ALU.is_gt))
                done(nc.vector.tensor_scalar(deg[:], bank(0, 2), 0.0, None, ALU.is_le))
                wait()
                done(nc.vector.tensor_tensor(tab[:, :, 0], msk[:], bank(0, 2), ALU.mult))
                wait()
                nc.vector.tensor_tensor(deg[:], deg[:], tab[:, :, 0], ALU.add).then_inc(guarded, 1)
                dve.wait_ge(rooted, 1)
                done(nc.vector.reciprocal(deg[:], tab[:, :, 1]))
                wait()
                done(nc.vector.tensor_tensor(tab[:, :, 0], deg[:], msk[:], ALU.mult))
                wait()
                done(nc.vector.tensor_scalar(msk[:], bank(2, 2), 0.0, NOWHERE, ALU.is_le, ALU.mult))
                wait()
                done(nc.vector.scalar_tensor_tensor(out=deg[:], in0=bank(2, 2), scalar=-1.0, in1=msk[:],
                                                    op0=ALU.add, op1=ALU.add))
                wait()
                done(nc.vector.tensor_copy(tab[:, :, 1].bitcast(I32), deg[:]))
                N_STEPS.append(n[0])

            @block.tensor
            def _(pe):
                pe.wait_ge(pool_ready, 1)
                for b in range(4):
                    nc.tensor.matmul(bank(b), zero[0:1, :], zero[0:1, 0:1].to_broadcast([1, 512]), start=True, stop=False)

                def product(i, par, tile):
                    hold(pe, hots, tile + 1)
                    for k in range(3):
                        for h in (0, 1):
                            last = nc.tensor.matmul(bank(h), hot_w[:, par, k], hot_lo[:, par, 0, 512 * h:512 * h + 512],
                                                    start=False, stop=False)
                    for k in range(2):
                        for h in (0, 1):
                            last = nc.tensor.matmul(bank(2 + h), hot_p[:, par, k],
                                                    hot_lo[:, par, 1, 512 * h:512 * h + 512], start=False, stop=False)
                    last.then_inc(products, 1)
                paired_loop(pe, TILES, product)
                for b in range(4):
                    last = nc.tensor.matmul(bank(b), zero[0:1, :], zero[0:1, 0:1].to_broadcast([1, 512]), start=False, stop=True)
                last.then_inc(products, 1)

            @block.scalar
            def _(act):
                act.wait_ge(guarded, 1)
                nc.scalar.activation(tab[:, :, 1], deg[:], ACT.Sqrt).then_inc(rooted, 1)

            @block.sync
            def _(sp):
                for par in (0, 1):
                    sp.sem_inc(st[par], 16)
                for k, (ids, dest) in enumerate((("src_rows", D.xs), ("dst_rows", D.xd))):
                    def load(i, par, g):
                        sp.wait_ge(st[par], i * 16 + k * ODD_EVEN[par] + 16)
                        sp.dma_start(near[k][:, par], A[ids][g]).then_inc(id_in[par], 16)

                    def store(i, par, g):
                        sp.wait_ge(gin[par], (i * 16 + k * ODD_EVEN[par] + 16) * S)
                        sp.dma_start(grp(dest)[g], rows[:, par]).then_inc(st[par], 16)
                    paired_loop(sp, GROUPS, load, store)
                for par in (0, 1):
                    sp.wait_ge(st[par], 2 * ODD_EVEN[par] + 16)
                sp.wait_ge(dstep, N_STEPS[0])
                sp.dma_start(D.table.rearrange("(h l) c -> h l c", l=LO), tab[0:HI]).then_inc(table_st, 16)
                sp.wait_ge(table_st, 16)



def fold_norms(nc, A, sem, W, D, bank):
    ctx = ExitStack()
    with ctx:
        t = lambda n, sh, dt=F32: ctx.enter_context(nc.sbuf_tensor(n, sh, dt))
        scaled = t("fold_scaled", [P, P])
        step, ready, product, loaded = (sem("fold_" + n) for n in ("step", "ready", "product", "loaded"))
        with nc.Block() as block:
            @block.sync
            def _(sp):
                for q, name in enumerate(("L0_gnn_ln_beta", "L1_gnn_beta")):
                    sp.dma_start(W.beta_rows[:, q], A[name].unsqueeze(0).unsqueeze(1).to_broadcast([1, S, C])
                                 ).then_inc(loaded, 16)
                sp.wait_ge(loaded, 32)

            @block.vector
            def _(dve):
                nc.vector.memset(W.ones_row[:], 1.0)
                nc.vector.memset(W.cm[:], 0.0).then_inc(step, 1)
                dve.wait_ge(step, 1)
                nc.vector.memset(W.cm[0:C, 0:C], -1.0 / C)
                nc.vector.memset(W.cm[C:P, C:P], -1.0 / C).then_inc(step, 1)
                nc.vector.tensor_scalar(scaled[:], W.w02[:], W.col["ln_gamma"], None, ALU.mult).then_inc(step, 1)
                dve.wait_ge(step, 3)
                nc.vector.tensor_tensor(W.cm[:], W.cm[:], W.ident[:], ALU.add).then_inc(step, 1)
                dve.wait_ge(step, 4)
                for q, out, mat in ((0, W.cm0, W.cm), (2, W.cm1, W.cm), (2, W.gamma1, W.ident)):
                    nc.vector.tensor_tensor(out[:].rearrange("p (h c) -> p h c", h=2),
                                            mat[:].rearrange("p (h c) -> p h c", h=2),
                                            W.rows[:, q].unsqueeze(1).to_broadcast([P, 2, C]), ALU.mult)
                nc.vector.tensor_tensor(W.b2e_dp[:], W.col["b2e"], W.col["dp"], ALU.mult)
                dve.sem_inc(ready, 1)
                dve.wait_ge(product, 1)
                nc.vector.tensor_copy(W.w02c[:], bank(0)[:, 0:P])
                nc.vector.tensor_tensor(W.base_b[:], bank(1)[:, 0:1], W.col["cheb_b"], ALU.add).then_inc(step, 1)
                dve.wait_ge(step, 5)
                for k, f in enumerate((0.01, 0.99)):
                    nc.vector.tensor_scalar(W.base_slanted[:, k:k + 1], W.base_b[:], f, None, ALU.mult)

            @block.tensor
            def _(pe):
                pe.wait_ge(ready, 1)
                nc.tensor.matmul(bank(0)[:, 0:P], W.cm[:], scaled[:], start=True, stop=True)
                nc.tensor.matmul(bank(1)[:, 0:1], W.w02[:], W.col["ln_beta"], start=True, stop=True).then_inc(product, 1)


def rows_by(nc, out, paired, weights, beta, W):
    nc.tensor.matmul(out, W.ones_row[:], beta.rearrange("a s c -> a (s c)"), start=True, stop=False)
    for q in range(S // 2):
        last = nc.tensor.matmul(out[:, P * q:P * q + P], paired[:, P * q:P * q + P], weights[:], start=False,
                                stop=q == S // 2 - 1)
    return last


def lone_states(nc, A, sem, W, D, bank, out):
    for name, count, source, dests in (("lone_nodes", NODE_GROUPS, A["x"], None),
                                       ("lone_sources", GROUPS, D.xs, (D.t0s, D.h_lone))):
        lone_run(nc, sem, W, D, bank, out, name, count, source, dests)


def lone_run(nc, sem, W, D, bank, out, name, count, source, dests):
    ctx = ExitStack()
    with ctx:
        t = lambda n, sh, dt=F32: ctx.enter_context(nc.sbuf_tensor(name + n, sh, dt))
        col = W.col
        x, x1, x2 = (t(n, [P, RING, S, C]) for n in ("x", "x1", "x2"))
        if dests:
            tr, hb = (t(n, [P, RING, S, C]) for n in ("tr", "hb"))
        ya, yb = (t(n, [P, S, C]) for n in ("ya", "yb"))
        yaf, ybf = (t(n, [P, HALF]) for n in ("yaf", "ybf"))
        hf, uf = ([t(f"{n}{k}", [P, HALF])[:] for k in (0, 1)] for n in ("hf", "uf"))
        norm_a, norm_b = NormTwice(sem, t, name + "a"), NormTwice(sem, t, name + "b")
        names = ("ya_done", "ya_t", "yaf_done", "base_done", "h_done", "mean_done", "u_done", "u_rows", "x1_done",
                 "yb_done", "yb_t", "ybf_done", "residual", "x2_done", "extra_rows", "extra_done")
        m = {n: sem(name + n) for n in names}
        x_in, stored = ([sem(f"{name}{n}{r}") for r in range(RING)] for n in ("x_in", "stored"))
        n_st = 4 if dests else 1
        if not dests:
            near, tab = t("near", [P, RING, S], I32), t("tab", [P, RING, S, 2])
            tabs, ls = t("tabs", [P, 2 * GROUPS, S, 2]), t("ls", [P, GROUPS, S], I32)
            ids_done, taken, w_step, ls_stored = (sem(name + n) for n in ("ids_done", "taken", "w_step", "ls_stored"))
            landed = [sem(f"{name}tab{r}") for r in range(RING)]
            assert NODE_GROUPS == 2 * GROUPS
        with nc.Block() as block:
            if not dests:
                @block.gpsimd
                def _(pool):
                    def gather(i, r, g):
                        hold(pool, ids_done, g + 1)
                        gather_rows(nc, pool, D.table, near[:, r], tab[:, r], landed[r], NP_ - 1)
                    ring_loop(pool, 2 * GROUPS, [gather])

            @block.sync
            def _(sp):
                for r in range(RING):
                    sp.sem_inc(stored[r], 16 * n_st)

                def load(i, r, g):
                    sp.wait_ge(m["x1_done"], g + 1)
                    sp.dma_start(x[:, r], group_rows(source)[g]).then_inc(x_in[r], 16)

                def store(i, r, g):
                    sp.wait_ge(m["x2_done"], g + 1)
                    if dests:
                        sp.dma_start(group_rows(D.x1_lone)[g], x1[:, r]).then_inc(stored[r], 16)
                        sp.dma_start(group_rows(D.x2_lone)[g], x2[:, r]).then_inc(stored[r], 16)
                        sp.wait_ge(m["extra_done"], g * 2 + 2)
                        sp.dma_start(group_rows(D.t0s)[g], tr[:, r]).then_inc(stored[r], 16)
                        sp.dma_start(group_rows(D.h_lone)[g], hb[:, r]).then_inc(stored[r], 16)
                    else:
                        sp.dma_start(group_rows(out)[g], x2[:, r]).then_inc(stored[r], 16)
                ring_loop(sp, count, [load], [], [], [], [], [store])
                for r in range(RING):
                    sp.wait_ge(stored[r], 16 * n_st * (of_slot(r, count) + 1))
                if not dests:
                    sp.wait_ge(w_step, 2)
                    sp.dma_start(D.ls.rearrange("g p s -> p g s"), ls[:]).then_inc(ls_stored, 16)
                    sp.wait_ge(ls_stored, 16)

            @block.vector
            def _(dve):
                dve.sem_inc(m["x1_done"], RING)

                def indices(i, r, g):
                    nc.vector.tensor_copy(near[:, r], W.idsE[:, bass.ds(g, 1)].rearrange("p a s -> p (a s)")
                                          ).then_inc(ids_done, 1)

                def take(i, r, g):
                    dve.wait_ge(landed[r], i * 128 + 128)
                    nc.vector.tensor_copy(tabs[:, bass.ds(g, 1)], tab[:, r].unsqueeze(1)).then_inc(taken, 1)

                def a(i, r, g):
                    dve.wait_ge(x_in[r], i * 16 + 16)
                    yield from norm_a.dve(nc, dve, g, x[:, r])
                    if not (isinstance(g, int) and g == 0):
                        dve.wait_ge(m["ya_t"], g)
                    nc.vector.tensor_tensor(ya[:], norm_a.y, spread(norm_a.gain), ALU.mult).then_inc(m["ya_done"], 1)

                def b(i, r, g):
                    yield 0
                    dve.wait_ge(stored[r], 16 * n_st * (i + 1))
                    dve.wait_ge(m["u_rows"], g + 1)
                    nc.vector.tensor_tensor(x1[:, r], x[:, r], as_rows(bank(1)), ALU.add).then_inc(m["x1_done"], 1)
                    dve.wait_ge(m["x1_done"], g + RING + 1)
                    yield from norm_b.dve(nc, dve, g, x1[:, r])
                    if not (isinstance(g, int) and g == 0):
                        dve.wait_ge(m["yb_t"], g)
                    nc.vector.tensor_tensor(yb[:], norm_b.y, spread(norm_b.gain), ALU.mult).then_inc(m["yb_done"], 1)

                def c(i, r, g):
                    yield 13
                    dve.wait_ge(m["residual"], g + 1)
                    nc.vector.tensor_tensor(x2[:, r], x1[:, r], as_rows(bank(5)), ALU.add).then_inc(m["x2_done"], 1)
                if dests:
                    ring_loop(dve, count, [a], [], [b], [c])
                else:
                    ring_loop(dve, count, [a, indices], [], [b], [c, take])
                    dve.wait_ge(taken, 2 * GROUPS)
                    nc.vector.scalar_tensor_tensor(out=W.wE[:], in0=tabs[:, 0:GROUPS, :, 0], scalar=-1.0,
                                                   in1=tabs[:, GROUPS:, :, 0], op0=ALU.mult, op1=ALU.mult
                                                   ).then_inc(w_step, 1)
                    nc.vector.tensor_copy(ls[:], tabs[:, 0:GROUPS, :, 1].bitcast(I32)).then_inc(w_step, 1)
                    dve.wait_ge(w_step, 2)
                    nc.vector.tensor_tensor(W.wE[:], W.wE[:], W.ewE[:], ALU.mult)

            @block.tensor
            def _(pe):
                def b(i, r, g):
                    yield 0
                    hold(pe, m["ya_done"], g + 1)
                    transpose_pairs(nc, bank(0), ya[:], W).then_inc(m["ya_t"], 1)
                    yield 2
                    hold(pe, m["yaf_done"], g + 1)
                    nc.tensor.matmul(bank(2), W.w02c[:], yaf[:], start=True, stop=True).then_inc(m["base_done"], 1)
                    if dests:
                        if not (isinstance(g, int) and g == 0):
                            hold(pe, m["extra_done"], g * 2)
                        rows_by(nc, bank(6), yaf[:], W.cm0, W.beta_rows[:, 0], W).then_inc(m["extra_rows"], 1)
                    yield 6
                    hold(pe, m["h_done"], g + 1)
                    for k in (0, 1):
                        last = nc.tensor.matmul(bank(3), W.gmean[:], hf[k], start=k == 0, stop=k == 1)
                    last.then_inc(m["mean_done"], 1)
                    if dests:
                        sum_transposed(nc, bank(7), hf, W, S // 2).then_inc(m["extra_rows"], 1)
                    yield 9
                    hold(pe, m["u_done"], g + 1)
                    hold(pe, m["x1_done"], g + RING)
                    sum_transposed(nc, bank(1), uf, W, S // 2).then_inc(m["u_rows"], 1)

                def d(i, r, g):
                    yield 1
                    hold(pe, m["yb_done"], g + 1)
                    transpose_pairs(nc, bank(4), yb[:], W).then_inc(m["yb_t"], 1)
                    yield 4
                    hold(pe, m["ybf_done"], g + 1)
                    if not (isinstance(g, int) and g == 0):
                        hold(pe, m["x2_done"], g)
                    rows_by(nc, bank(5), ybf[:], W.cm1, W.beta_rows[:, 1], W).then_inc(m["residual"], 1)
                ring_loop(pe, count, [], [b], [], [d])

            @block.scalar
            def _(act):
                def a(i, r, g):
                    yield from norm_a.act(nc, act, g)

                def b(i, r, g):
                    yield 1
                    act.wait_ge(m["ya_t"], g + 1)
                    nc.scalar.activation(yaf[:], bank(0), ACT.Copy).then_inc(m["yaf_done"], 1)
                    yield 5
                    act.wait_ge(m["base_done"], g + 1)
                    leaky_parts(nc, hf, bank(2), 0.01, W.base_slanted[:, 0:1], W.base_slanted[:, 1:2]
                                ).then_inc(m["h_done"], 1)
                    yield 8
                    act.wait_ge(m["mean_done"], g + 1)
                    leaky_parts(nc, uf, bank(3), 0.01, col["gat_b_slope"], col["gat_b_rest"]).then_inc(m["u_done"], 1)
                    if dests:
                        yield 9
                        act.wait_ge(stored[r], 16 * n_st * (i + 1))
                        for k, (buf, n) in enumerate(((tr, 6), (hb, 7))):
                            act.wait_ge(m["extra_rows"], g * 2 + k + 1)
                            nc.scalar.activation(buf[:, r], as_rows(bank(n)), ACT.Copy).then_inc(m["extra_done"], 1)

                def c(i, r, g):
                    yield from norm_b.act(nc, act, g)

                def d(i, r, g):
                    yield 3
                    act.wait_ge(m["yb_t"], g + 1)
                    nc.scalar.activation(ybf[:], bank(4), ACT.Copy).then_inc(m["ybf_done"], 1)
                ring_loop(act, count, [a], [b], [c], [d])


def gather_rows(nc, pool, source, ids, out, landed, limit):
    for q in range(S):
        nc.gpsimd.indirect_dma_start(
            out=out[:, q], out_offset=None, in_=source,
            in_offset=bass.IndirectOffsetOnAxis(ap=ids[:, q:q + 1], axis=0),
            bounds_check=limit, oob_is_err=False).then_inc(landed, 16)


def first_propagation(nc, A, sem, W, D, bank):
    ctx = ExitStack()
    with ctx:
        t = lambda n, sh, dt=F32: ctx.enter_context(nc.sbuf_tensor(n, sh, dt))
        ts, xd, g1 = (t("p1_" + n, [P, RING, S, C]) for n in ("ts", "xd", "g1"))
        msg, yd = t("p1_msg", [P, S, C]), t("p1_yd", [P, S, C])
        yf = t("p1_yf", [P, 2, HALF])
        sums = t("p1_sums", [C, 2, G_ROWS])
        pd = t("p1_pd", [C, RING, G_ROWS])
        norm = NormTwice(sem, t, "p1_n")
        names = ("msg_done", "yd_done", "msg_t", "yd_t", "yf_done", "pd_mm", "back", "evacuated", "carry")
        m = {n: sem("p1_" + n) for n in names}
        inn, st = ([sem(f"p1_{n}{r}") for r in range(RING)] for n in ("in", "st"))
        with nc.Block() as block:
            @block.sync
            def _(sp):
                for r in range(RING):
                    sp.sem_inc(st[r], 32)

                def load(i, r, g):
                    sp.wait_ge(m["yd_done"], g + 1)
                    sp.dma_start(ts[:, r], group_rows(D.t0s)[g]).then_inc(inn[r], 16)
                    sp.dma_start(xd[:, r], group_rows(D.xd)[g]).then_inc(inn[r], 16)

                def store(i, r, g):
                    sp.wait_ge(m["evacuated"], g * 2 + 2)
                    sp.dma_start(group_cols(D.pd)[g], pd[:, r]).then_inc(st[r], 16)
                    sp.dma_start(group_rows(D.tx1)[g], g1[:, r]).then_inc(st[r], 16)
                ring_loop(sp, GROUPS, [load], [], [], [], [store])
                for r in range(RING):
                    sp.wait_ge(st[r], 32 * (of_slot(r, GROUPS) + 1))

            @block.vector
            def _(dve):
                dve.sem_inc(m["yd_done"], RING)
                nc.vector.memset(sums[:, 1, G_ROWS - 1:G_ROWS], 0.0).then_inc(m["carry"], 1)

                def a(i, r, g):
                    dve.wait_ge(inn[r], i * 32 + 32)
                    yield from norm.dve(nc, dve, g, xd[:, r])
                    if not (isinstance(g, int) and g == 0):
                        dve.wait_ge(m["yd_t"], g)
                    nc.vector.tensor_tensor(yd[:], norm.y, spread(norm.gain), ALU.mult).then_inc(m["yd_done"], 1)

                def messages(i, r, g):
                    yield 3
                    w = W.wE[:, bass.ds(g, 1)].rearrange("p a s -> p (a s)")
                    if not (isinstance(g, int) and g == 0):
                        dve.wait_ge(m["msg_t"], g)
                    nc.vector.tensor_tensor(msg[:], ts[:, r], spread(w), ALU.mult).then_inc(m["msg_done"], 1)

                def scan(i, r, g):
                    yield 4
                    dve.wait_ge(m["msg_t"], g + 1)
                    if not (isinstance(g, int) and g < 2):
                        dve.wait_ge(m["back"], g - 1)
                    dve.wait_ge(m["carry"], g + 1)
                    run_sums(nc, W, g, r % 2, bank(4, 2)[0:C], sums, m)
                ring_loop(dve, GROUPS, [a, messages], [scan])

            @block.tensor
            def _(pe):
                def b(i, r, g):
                    yield 1
                    hold(pe, m["msg_done"], g + 1)
                    hold(pe, m["carry"], g + 1)
                    transpose_rows(nc, bank(4, 2), msg[:], W).then_inc(m["msg_t"], 1)
                    yield 2
                    hold(pe, m["yd_done"], g + RING + 1)
                    hold(pe, m["yf_done"], g)
                    transpose_pairs(nc, bank(0), yd[:], W).then_inc(m["yd_t"], 1)

                def c(i, r, g):
                    yield 3
                    hold(pe, m["yf_done"], g + 1)
                    hold(pe, m["carry"], g + 2)
                    hold(pe, m["evacuated"], g * 2)
                    for h in (0, 1):
                        part = slice(HALF * h, HALF * h + HALF)
                        nc.tensor.matmul(bank(2, 2)[0:C, part], W.w02c[:, C * h:C * h + C], yf[:, r % 2], start=True,
                                         stop=False)
                        last = nc.tensor.matmul(bank(2, 2)[0:C, part], W.w1[:], sums[:, r % 2, part], start=False,
                                                stop=True)
                    last.then_inc(m["pd_mm"], 1)
                    transpose_back(nc, bank(1), sums[:, r % 2], W).then_inc(m["back"], 1)
                ring_loop(pe, GROUPS, [], [b], [c])

            @block.scalar
            def _(act):
                def a(i, r, g):
                    yield from norm.act(nc, act, g)

                def b(i, r, g):
                    yield 5
                    act.wait_ge(m["yd_t"], g + 1)
                    nc.scalar.activation(yf[:, r % 2], bank(0), ACT.Copy).then_inc(m["yf_done"], 1)

                def c(i, r, g):
                    yield 6
                    act.wait_ge(st[r], i * 32 + 32)
                    act.wait_ge(m["pd_mm"], g + 1)
                    nc.scalar.activation(pd[:, r], bank(2, 2)[0:C], ACT.Identity, bias=W.base_b[0:C]
                                         ).then_inc(m["evacuated"], 1)
                    yield 7
                    act.wait_ge(m["back"], g + 1)
                    nc.scalar.activation(g1[:, r], as_rows(bank(1)), ACT.Copy).then_inc(m["evacuated"], 1)
                ring_loop(act, GROUPS, [a], [b], [c])


def run_sums(nc, W, g, par, messages, sums, m):
    return nc.vector.tensor_tensor_scan(
        sums[:, par], W.same[:, bass.ds(g * G_ROWS, G_ROWS)], messages, sums[:, 1 - par, G_ROWS - 1:G_ROWS],
        ALU.mult, ALU.add).then_inc(m["carry"], 1)


def second_propagation(nc, A, sem, W, D, bank):
    ctx = ExitStack()
    with ctx:
        t = lambda n, sh, dt=F32: ctx.enter_context(nc.sbuf_tensor(n, sh, dt))
        near = t("p2_near", [P, RING, S], I32)
        got, hr = (t("p2_" + n, [P, RING, S, C]) for n in ("got", "hr"))
        msg = t("p2_msg", [P, 2, S, C])
        sums, hf = t("p2_sums", [C, 2, G_ROWS]), t("p2_hf", [C, 2, G_ROWS])
        pd, pre = t("p2_pd", [C, 2, G_ROWS]), t("p2_pre", [C, G_ROWS])
        att = t("p2_att", [2 * HEADS, RING, G_ROWS])
        names = ("msg_done", "zeroed", "msg_t", "carry", "mm", "pre_done", "h_done", "back", "att_mm", "evacuated",
                 "pd_in0", "pd_in1")
        m = {n: sem("p2_" + n) for n in names}
        pd_in = (m["pd_in0"], m["pd_in1"])
        inn, landed, st = ([sem(f"p2_{n}{r}") for r in range(RING)] for n in ("in", "got", "st"))
        with nc.Block() as block:
            @block.sync
            def _(sp):
                for r in range(RING):
                    sp.sem_inc(st[r], 32)

                def load(i, r, g):
                    sp.wait_ge(m["msg_done"], g + 1)
                    sp.dma_start(near[:, r], D.ls[g]).then_inc(inn[r], 16)

                def load_later(i, r, g):
                    sp.wait_ge(m["pre_done"], g + 1)
                    sp.dma_start(pd[:, r % 2], group_cols(D.pd)[g]).then_inc(pd_in[r % 2], 16)

                def store(i, r, g):
                    sp.wait_ge(m["evacuated"], g * 2 + 2)
                    sp.dma_start(group_rows(D.hd)[g], hr[:, r]).then_inc(st[r], 16)
                    sp.dma_start(group_cols(D.att_d)[g], att[:, r]).then_inc(st[r], 16)
                ring_loop(sp, GROUPS, [load], [], [load_later], [], [], [store])
                for r in range(RING):
                    sp.wait_ge(st[r], 32 * (of_slot(r, GROUPS) + 1))

            @block.gpsimd
            def _(pool):
                def gather(i, r, g):
                    hold(pool, inn[r], i * 16 + 16)
                    hold(pool, m["zeroed"], g + 1)
                    gather_rows(nc, pool, D.tx1, near[:, r], got[:, r], landed[r], EP - 1)
                ring_loop(pool, GROUPS, [gather])

            @block.vector
            def _(dve):
                dve.sem_inc(m["msg_done"], RING)
                dve.sem_inc(m["pre_done"], 2)
                for r in range(RING):
                    nc.vector.memset(got[:, r], 0.0).then_inc(m["zeroed"], 1)
                nc.vector.memset(sums[:, 1, G_ROWS - 1:G_ROWS], 0.0).then_inc(m["carry"], 1)

                def messages(i, r, g):
                    yield 4
                    dve.wait_ge(landed[r], i * 128 + 128)
                    if not (isinstance(g, int) and g < 2):
                        dve.wait_ge(m["msg_t"], g - 1)
                    w = W.wE[:, bass.ds(g, 1)].rearrange("p a s -> p (a s)")
                    nc.vector.tensor_tensor(msg[:, r % 2], got[:, r], spread(w), ALU.mult).then_inc(m["msg_done"], 1)
                    yield 5
                    dve.wait_ge(m["msg_done"], g + RING + 1)
                    nc.vector.memset(got[:, r], 0.0).then_inc(m["zeroed"], 1)

                def scan(i, r, g):
                    yield 1
                    dve.wait_ge(m["msg_t"], g + 1)
                    if not (isinstance(g, int) and g < 2):
                        dve.wait_ge(m["mm"], g - 1)
                    dve.wait_ge(m["carry"], g + 1)
                    run_sums(nc, W, g, r % 2, bank(4, 2)[0:C], sums, m)

                def h(i, r, g):
                    yield 2
                    dve.wait_ge(m["mm"], g + 1)
                    after(dve, m["h_done"], g)
                    dve.wait_ge(pd_in[r % 2], half_turns(i, r) * 16 + 16)
                    nc.vector.tensor_tensor(pre[:], bank(2, 2)[0:C], pd[:, r % 2], ALU.add).then_inc(m["pre_done"], 1)
                    yield 3
                    dve.wait_ge(m["pre_done"], g + 3)
                    if not (isinstance(g, int) and g < 2):
                        dve.wait_ge(m["att_mm"], g - 1)
                    nc.vector.scalar_tensor_tensor(out=hf[:, r % 2], in0=pre[:], scalar=0.01, in1=pre[:], op0=ALU.mult,
                                                   op1=ALU.max).then_inc(m["h_done"], 1)
                ring_loop(dve, GROUPS, [messages], [scan], [h])

            @block.tensor
            def _(pe):
                def b(i, r, g):
                    yield 0
                    hold(pe, m["msg_done"], g + RING + 1)
                    hold(pe, m["carry"], g + 1)
                    transpose_rows(nc, bank(4, 2), msg[:, r % 2], W).then_inc(m["msg_t"], 1)

                def c(i, r, g):
                    yield 1
                    hold(pe, m["carry"], g + 2)
                    hold(pe, m["pre_done"], g + 2)
                    for h in (0, 1):
                        part = slice(HALF * h, HALF * h + HALF)
                        last = nc.tensor.matmul(bank(2, 2)[0:C, part], W.w2x2[:], sums[:, r % 2, part], start=True,
                                                stop=True)
                    last.then_inc(m["mm"], 1)

                def d(i, r, g):
                    yield 2
                    hold(pe, m["h_done"], g + 1)
                    hold(pe, m["evacuated"], g * 2)
                    transpose_back(nc, bank(1), hf[:, r % 2], W).then_inc(m["back"], 1)
                    for h in (0, 1):
                        part = slice(HALF * h, HALF * h + HALF)
                        last = nc.tensor.matmul(bank(6, 2)[0:2 * HEADS, part], W.att[:].rearrange("k q h -> k (q h)"),
                                                hf[:, r % 2, part], start=True, stop=True)
                    last.then_inc(m["att_mm"], 1)
                ring_loop(pe, GROUPS, [], [b], [c], [d])

            @block.scalar
            def _(act):
                def d(i, r, g):
                    act.wait_ge(st[r], i * 32 + 32)
                    act.wait_ge(m["back"], g + 1)
                    nc.scalar.activation(hr[:, r], as_rows(bank(1)), ACT.Copy).then_inc(m["evacuated"], 1)
                    act.wait_ge(m["att_mm"], g + 1)
                    nc.scalar.activation(att[:, r], bank(6, 2)[0:2 * HEADS], ACT.Copy).then_inc(m["evacuated"], 1)
                ring_loop(act, GROUPS, [], [], [], [d])


def attention_sources(nc, A, sem, W, D, bank):
    ctx = ExitStack()
    with ctx:
        t = lambda n, sh, dt=F32: ctx.enter_context(nc.sbuf_tensor(n, sh, dt))
        near = t("p3_near", [P, RING, S], I32)
        got = t("p3_got", [P, RING, S, C])
        hf = t("p3_hf", [P, 2, HALF])
        att = t("p3_att", [HEADS, RING, G_ROWS])
        m = {n: sem("p3_" + n) for n in ("got_t", "hf_done", "mm", "att_done")}
        inn, landed, st = ([sem(f"p3_{n}{r}") for r in range(RING)] for n in ("in", "got", "st"))
        with nc.Block() as block:
            @block.sync
            def _(sp):
                for r in range(RING):
                    sp.sem_inc(st[r], 32)

                def load(i, r, g):
                    sp.wait_ge(m["att_done"], g + 1)
                    sp.wait_ge(st[r], i * 32 + 32)
                    sp.dma_start(near[:, r], D.ls[g]).then_inc(inn[r], 16)
                    sp.dma_start(got[:, r], group_rows(D.h_lone)[g]).then_inc(inn[r], 16)

                def store(i, r, g):
                    sp.wait_ge(landed[r], i * 128 + 128)
                    sp.dma_start(group_rows(D.hs)[g], got[:, r]).then_inc(st[r], 16)
                    sp.wait_ge(m["att_done"], g + RING + 1)
                    sp.dma_start(group_cols(D.att_s)[g], att[:, r]).then_inc(st[r], 16)
                ring_loop(sp, GROUPS, [load], [], [store])
                for r in range(RING):
                    sp.wait_ge(st[r], 32 * (of_slot(r, GROUPS) + 1))

            @block.gpsimd
            def _(pool):
                def gather(i, r, g):
                    hold(pool, inn[r], i * 32 + 32)
                    gather_rows(nc, pool, D.hd, near[:, r], got[:, r], landed[r], EP - 1)
                ring_loop(pool, GROUPS, [gather])

            @block.tensor
            def _(pe):
                def work(i, r, g):
                    hold(pe, landed[r], i * 128 + 128)
                    if not (isinstance(g, int) and g == 0):
                        hold(pe, m["hf_done"], g)
                    transpose_pairs(nc, bank(0), got[:, r], W).then_inc(m["got_t"], 1)
                    hold(pe, m["hf_done"], g + 1)
                    hold(pe, m["att_done"], g + RING)
                    halves(nc, bank(2, 2)[0:HEADS], W.att_half, hf[:, r % 2]).then_inc(m["mm"], 1)
                ring_loop(pe, GROUPS, [work])

            @block.scalar
            def _(act):
                act.sem_inc(m["att_done"], RING)

                def work(i, r, g):
                    act.wait_ge(m["got_t"], g + 1)
                    nc.scalar.activation(hf[:, r % 2], bank(0), ACT.Copy).then_inc(m["hf_done"], 1)
                    act.wait_ge(st[r], i * 32 + 32)
                    act.wait_ge(m["mm"], g + 1)
                    nc.scalar.activation(att[:, r], bank(2, 2)[0:HEADS], ACT.Copy).then_inc(m["att_done"], 1)
                ring_loop(act, GROUPS, [work])


def edge_terms(nc, A, sem, W, D, bank):
    ctx = ExitStack()
    with ctx:
        t = lambda n, sh, dt=F32: ctx.enter_context(nc.sbuf_tensor(n, sh, dt))
        col = W.col
        ea = t("et_ea", [EDIM, RING, G_ROWS])
        hid = t("et_hid", [C, 2, G_ROWS])
        et = t("et_out", [C, RING, G_ROWS])
        m = {n: sem("et_" + n) for n in ("mm1", "pre", "hid", "mm2", "done")}
        inn, st = ([sem(f"et_{n}{r}") for r in range(RING)] for n in ("in", "st"))
        with nc.Block() as block:
            @block.sync
            def _(sp):
                for r in range(RING):
                    sp.sem_inc(st[r], 16)

                def load(i, r, g):
                    sp.wait_ge(m["done"], g + 1)
                    sp.dma_start(ea[:, r], group_cols(A["ea_cols"])[g]).then_inc(inn[r], 16)

                def store(i, r, g):
                    sp.wait_ge(m["done"], g + RING + 1)
                    sp.dma_start(group_cols(D.et)[g], et[:, r]).then_inc(st[r], 16)
                ring_loop(sp, GROUPS, [load], [], [], [store])
                for r in range(RING):
                    sp.wait_ge(st[r], 16 * (of_slot(r, GROUPS) + 1))

            @block.tensor
            def _(pe):
                def a(i, r, g):
                    hold(pe, inn[r], i * 16 + 16)
                    if not (isinstance(g, int) and g == 0):
                        hold(pe, m["hid"], g)
                    for h in (0, 1):
                        part = slice(HALF * h, HALF * h + HALF)
                        last = nc.tensor.matmul(bank(2, 2)[0:C, part], W.w1e[:], ea[:, r, part], start=True, stop=True)
                    last.then_inc(m["mm1"], 1)

                def b(i, r, g):
                    hold(pe, m["hid"], g + 1)
                    hold(pe, m["done"], g + RING)
                    for h in (0, 1):
                        part = slice(HALF * h, HALF * h + HALF)
                        last = nc.tensor.matmul(bank(4, 2)[0:C, part], W.w2e[:], hid[:, r % 2, part], start=True, stop=True)
                    last.then_inc(m["mm2"], 1)
                ring_loop(pe, GROUPS, [a], [b])

            @block.scalar
            def _(act):
                act.sem_inc(m["done"], RING)

                def a(i, r, g):
                    act.wait_ge(m["mm1"], g + 1)
                    if not (isinstance(g, int) and g < 2):
                        act.wait_ge(m["mm2"], g - 1)
                    nc.scalar.activation(hid[:, r % 2], bank(2, 2)[0:C], ACT.Identity, bias=col["b1e"][0:C]
                                         ).then_inc(m["pre"], 1)

                def b(i, r, g):
                    act.wait_ge(st[r], i * 16 + 16)
                    act.wait_ge(m["mm2"], g + 1)
                    nc.scalar.activation(et[:, r], bank(4, 2)[0:C], ACT.Identity, bias=W.b2e_dp[0:C],
                                         scale=col["dp"][0:C]).then_inc(m["done"], 1)
                ring_loop(act, GROUPS, [a], [b])

            @block.vector
            def _(dve):
                def a(i, r, g):
                    dve.wait_ge(m["pre"], g + 1)
                    h = hid[:, r % 2]
                    nc.vector.scalar_tensor_tensor(out=h, in0=h, scalar=0.1, in1=h, op0=ALU.mult, op1=ALU.max
                                                   ).then_inc(m["hid"], 1)
                ring_loop(dve, GROUPS, [a])


def attention_weights(nc, A, sem, W, D, bank):
    ctx = ExitStack()
    with ctx:
        t = lambda n, sh, dt=F32: ctx.enter_context(nc.sbuf_tensor(n, sh, dt))
        ids = t("sm_ids", [P, 3, CHUNK], I32)
        as_, ex = (t("sm_" + n, [P, HEADS, CHUNK]) for n in ("as", "ex"))
        sums = t("sm_sums", [P, HEADS + 1, CHUNK])
        big = sums[:, 0:HEADS]
        ad, back = (t("sm_" + n, [P, 2 * HEADS, CHUNK]) for n in ("ad", "back"))
        prev, nxt, last, fm, rm, gate, zero, ones = (t("sm_" + n, [P, CHUNK]) for n in
                                                     ("prev", "next", "last", "fm", "rm", "gate", "zero", "ones"))
        ends = t("sm_ends", [P, 2, 2 * HEADS])
        rows = t("sm_rows", [2 * HEADS, 2, P + 2])
        carry = t("sm_carry", [P, 2 * HEADS])
        m = {n: sem("sm_" + n) for n in ("in", "step", "ends_t", "carry_t", "ex_ready", "ex_done", "exs_ready", "exs_done", "ready", "stored")}
        rev = lambda a: a[:, ::-1]
        ADD, MAX, MUL = ALU.add, ALU.max, ALU.mult
        PLAN = []
        with nc.Block() as block:
            @block.sync
            def _(sp):
                line = A["dst_line"]
                for k, off in enumerate((0, 1, 2)):
                    sp.dma_start(ids[:, k], line[:, off:off + EP].rearrange("a (p e) -> (a p) e", p=P)).then_inc(m["in"], 16)
                sp.dma_start(as_[:], D.att_s.rearrange("h (p e) -> p h e", p=P)).then_inc(m["in"], 16)
                sp.dma_start(ad[:], D.att_d.rearrange("h (p e) -> p h e", p=P)).then_inc(m["in"], 16)
                sp.wait_ge(m["ready"], 1)
                out = D.alpha.rearrange("h (p e) -> p h e", p=P)
                sp.dma_start(out[:, 0:HEADS], ex[:]).then_inc(m["stored"], 16)
                sp.dma_start(out[:, HEADS:2 * HEADS], as_[:]).then_inc(m["stored"], 16)
                sp.dma_start(out[:, 2 * HEADS:], sums[:, HEADS:]).then_inc(m["stored"], 16)
                sp.wait_ge(m["stored"], 48)

            @block.tensor
            def _(pe):
                for n, k in enumerate(EXCHANGES):
                    pe.wait_ge(m["ex_ready"], 2 * n + 1)
                    for q in (0, 1):
                        last = nc.tensor.transpose(bank(q)[0:k, 0:P], ends[:, q, 0:k], W.ident[:])
                    last.then_inc(m["ends_t"], 1)
                    pe.wait_ge(m["ex_ready"], 2 * n + 2)
                    nc.tensor.transpose(bank(2)[:, 0:k], rows[0:k, 1, 1:P + 1], W.ident[0:k, 0:k]).then_inc(m["carry_t"], 1)

            @block.scalar
            def _(act):
                act.wait_ge(m["exs_ready"], 1)
                nc.scalar.activation(ex[:], ex[:], ACT.Exp)
                nc.scalar.activation(ad[:, 0:HEADS], ad[:, 0:HEADS], ACT.Exp).then_inc(m["exs_done"], 1)

            @block.vector
            def _(dve):
                n, x = [0], [0]

                def done(ins):
                    n[0] += 1
                    ins.then_inc(m["step"], 1)

                def wait():
                    dve.wait_ge(m["step"], n[0])

                def exchange(k, values, flag, combine, start, backward):
                    for h in range(k):
                        done(nc.vector.tensor_copy(ends[:, 1, h:h + 1], flag))
                        done(nc.vector.tensor_copy(ends[:, 0, h:h + 1], values(h)))
                    wait()
                    dve.sem_inc(m["ex_ready"], 1)
                    x[0] += 1
                    dve.wait_ge(m["ends_t"], x[0])
                    if combine == MAX:
                        done(nc.vector.tensor_scalar(rows[0:k, 0, 0:P], bank(1)[0:k, 0:P], -1.0, FAR, ADD, MUL))
                    else:
                        done(nc.vector.tensor_copy(rows[0:k, 0, 0:P], bank(1)[0:k, 0:P]))
                    at = slice(0, P) if backward else slice(2, P + 2)
                    done(nc.vector.memset(rows[0:k, 1], start))
                    wait()
                    order = rev if backward else (lambda a: a)
                    done(nc.vector.tensor_tensor_scan(order(rows[0:k, 1, at]), order(rows[0:k, 0, 0:P]),
                                                      order(bank(0)[0:k, 0:P]), start,
                                                      ADD if combine == MAX else MUL, combine))
                    wait()
                    dve.sem_inc(m["ex_ready"], 1)
                    dve.wait_ge(m["carry_t"], x[0])
                    done(nc.vector.tensor_copy(carry[:, 0:k], bank(2)[:, 0:k]))
                    wait()

                def spread_back(k, values):
                    done(nc.vector.tensor_tensor(back[:, 0:k], values, last[:].unsqueeze(1).to_broadcast([P, k, CHUNK]), MUL))
                    wait()
                    for h in range(k):
                        done(nc.vector.tensor_tensor_scan(rev(back[:, h]), rev(nxt[:]), rev(back[:, h]), 0.0, MUL, ADD))
                    wait()
                    exchange(k, lambda h: back[:, h, 0:1], rm[:, 0:1], ADD, 0.0, True)
                    for h in range(k):
                        done(nc.vector.scalar_tensor_tensor(out=back[:, h], in0=rm[:], scalar=carry[:, h:h + 1],
                                                            in1=back[:, h], op0=MUL, op1=ADD))
                    wait()

                dve.wait_ge(m["in"], 80)
                done(nc.vector.tensor_tensor(prev[:], ids[:, 0], ids[:, 1], ALU.is_equal))
                done(nc.vector.tensor_tensor(nxt[:], ids[:, 1], ids[:, 2], ALU.is_equal))
                done(nc.vector.tensor_tensor(last[:], ids[:, 1], ids[:, 2], ALU.not_equal))
                done(nc.vector.memset(zero[:], 0.0))
                done(nc.vector.memset(ones[:], 1.0))
                wait()
                done(nc.vector.tensor_tensor_scan(fm[:], prev[:], zero[:], 1.0, MUL, ADD))
                done(nc.vector.tensor_tensor_scan(rev(rm[:]), rev(nxt[:]), zero[:], 1.0, MUL, ADD))
                done(nc.vector.tensor_scalar(gate[:], prev[:], -1.0, FAR, ADD, MUL))
                wait()
                for h in range(HEADS):
                    done(nc.vector.tensor_tensor_scan(big[:, h], gate[:], as_[:, h], -FAR, ADD, MAX))
                wait()
                exchange(HEADS, lambda h: big[:, h, CHUNK - 1:CHUNK], fm[:, CHUNK - 1:CHUNK], MAX, -FAR, False)
                done(nc.vector.tensor_scalar(gate[:], fm[:], -1.0, FAR, ADD, MUL))
                wait()
                for h in range(HEADS):
                    done(nc.vector.scalar_tensor_tensor(out=big[:, h], in0=gate[:], scalar=carry[:, h:h + 1],
                                                        in1=big[:, h], op0=ADD, op1=MAX))
                wait()
                done(nc.vector.tensor_tensor(big, big, ad[:, 0:HEADS], MAX))
                wait()
                done(nc.vector.tensor_tensor(big, big, ad[:, HEADS:], ADD))
                done(nc.vector.tensor_tensor(ad[:, 0:HEADS], ad[:, 0:HEADS], ad[:, HEADS:], ADD))
                wait()
                done(nc.vector.scalar_tensor_tensor(out=big, in0=big, scalar=0.2, in1=big, op0=MUL, op1=MAX))
                done(nc.vector.scalar_tensor_tensor(out=ad[:, 0:HEADS], in0=ad[:, 0:HEADS], scalar=0.2,
                                                    in1=ad[:, 0:HEADS], op0=MUL, op1=MAX))
                wait()
                done(nc.vector.tensor_tensor(ad[:, 0:HEADS], ad[:, 0:HEADS], big, ALU.subtract))
                spread_back(HEADS, ad[:, HEADS:])
                done(nc.vector.tensor_tensor(ex[:], as_[:], back[:, 0:HEADS], ADD))
                wait()
                done(nc.vector.scalar_tensor_tensor(out=ex[:], in0=ex[:], scalar=0.2, in1=ex[:], op0=MUL, op1=MAX))
                wait()
                spread_back(HEADS, big)
                done(nc.vector.tensor_tensor(ex[:], ex[:], back[:, 0:HEADS], ALU.subtract))
                done(nc.vector.tensor_scalar(ad[:, 0:HEADS], ad[:, 0:HEADS], 0.0, None, ALU.min))
                wait()
                dve.sem_inc(m["exs_ready"], 1)
                dve.wait_ge(m["exs_done"], 1)
                for h in range(HEADS):
                    done(nc.vector.tensor_tensor_scan(sums[:, h], prev[:], ex[:, h], 0.0, MUL, ADD))
                done(nc.vector.tensor_tensor_scan(sums[:, HEADS], prev[:], ones[:], 0.0, MUL, ADD))
                wait()
                exchange(HEADS + 1, lambda h: sums[:, h, CHUNK - 1:CHUNK], fm[:, CHUNK - 1:CHUNK], ADD, 0.0, False)
                for h in range(HEADS + 1):
                    done(nc.vector.scalar_tensor_tensor(out=sums[:, h], in0=fm[:], scalar=carry[:, h:h + 1],
                                                        in1=sums[:, h], op0=MUL, op1=ADD))
                wait()
                done(nc.vector.scalar_tensor_tensor(out=big, in0=big, scalar=1e-16, in1=ad[:, 0:HEADS], op0=ADD, op1=ADD))
                wait()
                done(nc.vector.reciprocal(big, big))
                wait()
                done(nc.vector.tensor_tensor(as_[:], ad[:, 0:HEADS], big, MUL))
                spread_back(HEADS, big)
                done(nc.vector.tensor_tensor(ex[:], ex[:], back[:, 0:HEADS], MUL))
                done(nc.vector.tensor_tensor(as_[:], as_[:], last[:].unsqueeze(1).to_broadcast([P, HEADS, CHUNK]), MUL))
                wait()
                dve.sem_inc(m["ready"], 1)
                assert x[0] == len(EXCHANGES)


def attention_sums(nc, A, sem, W, D, bank):
    ctx = ExitStack()
    with ctx:
        t = lambda n, sh, dt=F32: ctx.enter_context(nc.sbuf_tensor(n, sh, dt))
        col = W.col
        hs, hd = (t("at_" + n, [P, 2, S, C]) for n in ("hs", "hd"))
        xd, x1 = (t("at_" + n, [P, 2, S, C]) for n in ("xd", "x1"))
        alpha = t("at_alpha", [ALPHAS, 2, G_ROWS])
        al = t("at_al", [P, 2, S, ALPHAS])
        wide, own = t("at_wide", [P, 2, S, HEADS, C]), t("at_own", [P, S, HEADS, C])
        pf = t("at_pf", [P, 2, 2, HALF])
        sums = t("at_sums", [C, 2, G_ROWS])
        parts = [t(f"at_u{k}", [C, G_ROWS])[:] for k in (0, 1)]
        names = ("al_t", "al_done", "wide_step", "wide_t", "pf_done", "mm", "carry", "u_done", "back", "x1_done")
        m = {n: sem("at_" + n) for n in names}
        inn, x_in, st = ([sem(f"at_{n}{k}") for k in (0, 1)] for n in ("in", "x_in", "st"))
        with nc.Block() as block:
            @block.sync
            def _(sp):
                for k in (0, 1):
                    sp.sem_inc(st[k], 16)

                def load(i, r, g):
                    sp.wait_ge(m["wide_step"], g * 3 + 2)
                    for b, d in ((hs, D.hs), (hd, D.hd)):
                        sp.dma_start(b[:, r % 2], group_rows(d)[g]).then_inc(inn[r % 2], 16)
                    sp.dma_start(alpha[:, r % 2], group_cols(D.alpha)[g]).then_inc(inn[r % 2], 16)

                def load_x(i, r, g):
                    sp.wait_ge(m["x1_done"], g + 1)
                    sp.dma_start(xd[:, r % 2], group_rows(D.xd)[g]).then_inc(x_in[r % 2], 16)

                def store(i, r, g):
                    sp.wait_ge(m["x1_done"], g + 3)
                    sp.dma_start(group_rows(D.x1d)[g], x1[:, r % 2]).then_inc(st[r % 2], 16)
                ring_loop(sp, GROUPS, [load], [], [], [load_x], [], [store])
                for k in (0, 1):
                    sp.wait_ge(st[k], ODD_EVEN[k] + 16)

            @block.vector
            def _(dve):
                dve.sem_inc(m["wide_step"], 6)
                dve.sem_inc(m["x1_done"], 2)
                nc.vector.memset(sums[:, 1, G_ROWS - 1:G_ROWS], 0.0).then_inc(m["carry"], 1)

                def a(i, r, g):
                    yield 3
                    dve.wait_ge(inn[r % 2], half_turns(i, r) * 48 + 48)
                    dve.wait_ge(m["al_done"], g + 1)
                    dve.wait_ge(m["wide_step"], g * 3 + 6)
                    after(dve, m["wide_t"], g * 2 - 2)
                    by = lambda x: x.unsqueeze(2).to_broadcast([P, S, HEADS, C])
                    wt = lambda k: al[:, r % 2, :, HEADS * k:HEADS * k + HEADS].unsqueeze(3).to_broadcast([P, S, HEADS, C])
                    nc.vector.tensor_copy(W.countE[:, bass.ds(g, 1)], al[:, r % 2, :, 2 * HEADS].unsqueeze(1))
                    nc.vector.tensor_tensor(wide[:, r % 2], by(hs[:, r % 2]), wt(0), ALU.mult).then_inc(m["wide_step"], 1)
                    nc.vector.tensor_tensor(own[:], by(hd[:, r % 2]), wt(1), ALU.mult).then_inc(m["wide_step"], 1)
                    yield 7
                    dve.wait_ge(m["wide_step"], g * 3 + 8)
                    nc.vector.tensor_tensor(wide[:, r % 2], wide[:, r % 2], own[:], ALU.add).then_inc(m["wide_step"], 1)

                def scan(i, r, g):
                    yield 0
                    dve.wait_ge(m["mm"], g + 1)
                    dve.wait_ge(m["carry"], g + 1)
                    after(dve, m["u_done"], g - 1)
                    run_sums(nc, W, g, r % 2, bank(4, 2)[0:C], sums, m)

                def x(i, r, g):
                    yield 4
                    dve.wait_ge(x_in[r % 2], half_turns(i, r) * 16 + 16)
                    dve.wait_ge(st[r % 2], half_turns(i, r) * 16 + 16)
                    dve.wait_ge(m["back"], g + 1)
                    nc.vector.tensor_tensor(x1[:, r % 2], xd[:, r % 2], as_rows(bank(1)), ALU.add).then_inc(m["x1_done"], 1)
                ring_loop(dve, GROUPS, [a], [], [scan], [x])

            @block.tensor
            def _(pe):
                def a(i, r, g):
                    yield 1
                    hold(pe, inn[r % 2], half_turns(i, r) * 48 + 48)
                    hold(pe, m["al_done"], g)
                    for n in range(S):
                        last = nc.tensor.transpose(bank(0)[:, ALPHAS * n:ALPHAS * (n + 1)],
                                                   alpha[:, r % 2, slot_cols(n)], W.ident[0:ALPHAS, 0:ALPHAS])
                    last.then_inc(m["al_t"], 1)

                def b(i, r, g):
                    for h in (0, 1):
                        yield 0 if h == 0 else 3
                        if h == 0:
                            hold(pe, m["wide_step"], g * 3 + 9)
                        hold(pe, m["pf_done"], g * 2 + h)
                        for j in range(S // 2):
                            for q in (0, 1):
                                last = nc.tensor.transpose(bank(2 + q)[:, P * j:P * j + P],
                                                           wide[:, r % 2, 2 * j + h, 2 * q:2 * q + 2].rearrange("p h c -> p (h c)"),
                                                           W.ident[:])
                        last.then_inc(m["wide_t"], 1)
                        yield 2 if h == 0 else 5
                        if h == 0:
                            hold(pe, m["carry"], g + 1)
                        hold(pe, m["pf_done"], g * 2 + h + 1)
                        for q in (0, 1):
                            last = nc.tensor.matmul(bank(4, 2)[0:C, HALF * h:HALF * h + HALF], W.gatw[:, q],
                                                    pf[:, h, q], start=q == 0, stop=q == 1)
                    last.then_inc(m["mm"], 1)

                def d(i, r, g):
                    yield 2
                    hold(pe, m["u_done"], g + 1)
                    hold(pe, m["x1_done"], g + 2)
                    sum_transposed(nc, bank(1), parts, W, S).then_inc(m["back"], 1)
                ring_loop(pe, GROUPS, [a], [b], [], [d])

            @block.scalar
            def _(act):
                def a(i, r, g):
                    yield 2
                    after(act, m["wide_step"], g * 3 + 2)
                    act.wait_ge(m["al_t"], g + 1)
                    nc.scalar.activation(al[:, r % 2], bank(0)[:, 0:ALPHAS * S].rearrange("p (s h) -> p s h", s=S),
                                         ACT.Copy).then_inc(m["al_done"], 1)

                def b(i, r, g):
                    for h in (0, 1):
                        yield 1 if h == 0 else 4
                        act.wait_ge(m["wide_t"], g * 2 + h + 1)
                        nc.scalar.activation(pf[:, h], bank(2, 2).rearrange("p (q n) -> p q n", q=2), ACT.Copy
                                             ).then_inc(m["pf_done"], 1)

                def c(i, r, g):
                    yield 5
                    act.wait_ge(m["carry"], g + 2)
                    after(act, m["back"], g)
                    leaky_parts(nc, parts, sums[:, r % 2], 0.01, col["gat_b_slope"][0:C], col["gat_b_rest"][0:C]
                                ).then_inc(m["u_done"], 1)
                ring_loop(act, GROUPS, [a], [b], [c])


def gated_messages(nc, A, sem, W, D, bank):
    ctx = ExitStack()
    with ctx:
        t = lambda n, sh, dt=F32: ctx.enter_context(nc.sbuf_tensor(n, sh, dt))
        col = W.col
        near = t("l1_near", [P, RING, S], I32)
        got, xd = (t("l1_" + n, [P, RING, S, C]) for n in ("got", "xd"))
        x2 = t("l1_x2", [P, 2, S, C])
        hn, hd, o1, xn = (t("l1_" + n, [P, S, C]) for n in ("hn", "hd", "o1", "xn"))
        et, sums = t("l1_et", [C, 2, G_ROWS]), t("l1_sums", [C, 2, G_ROWS])
        msg = t("l1_msg", [C, G_ROWS])
        hf, xf = t("l1_hf", [P, HALF]), t("l1_xf", [P, HALF])
        hid = [t(f"l1_hid{k}", [P, G_ROWS])[:] for k in (0, 1)]
        norm_s, norm_d, norm_o = (Norm(sem, t, "l1_" + n) for n in ("s", "d", "o"))
        names = ("hn_done", "hn_t", "hf_done", "mm1", "hid_done", "mm2", "msg_done", "carry", "back", "hd_done",
                 "o1_done", "xn_done", "xn_t", "xf_done", "residual", "x2_done")
        m = {n: sem("l1_" + n) for n in names}
        inn, landed, x_in = ([sem(f"l1_{n}{r}") for r in range(RING)] for n in ("in", "got", "x_in"))
        et_in, st = ([sem(f"l1_{n}{k}") for k in (0, 1)] for n in ("et_in", "st"))
        with nc.Block() as block:
            @block.sync
            def _(sp):
                for k in (0, 1):
                    sp.sem_inc(st[k], 16)

                def load(i, r, g):
                    sp.wait_ge(m["hn_done"], g + 1)
                    sp.dma_start(near[:, r], D.ls[g]).then_inc(inn[r], 16)
                    sp.dma_start(got[:, r], group_rows(D.x1_lone)[g]).then_inc(inn[r], 16)

                def load_et(i, r, g):
                    sp.wait_ge(m["msg_done"], g + 1)
                    sp.dma_start(et[:, r % 2], group_cols(D.et)[g]).then_inc(et_in[r % 2], 16)

                def load_x(i, r, g):
                    sp.wait_ge(m["x2_done"], g + 1)
                    sp.dma_start(xd[:, r], group_rows(D.x1d)[g]).then_inc(x_in[r], 16)

                def store(i, r, g):
                    sp.wait_ge(m["x2_done"], g + RING + 1)
                    sp.dma_start(group_rows(D.x2d)[g], x2[:, r % 2]).then_inc(st[r % 2], 16)
                ring_loop(sp, GROUPS, [load], [], [], [load_et], [load_x], [], [], [], [store])
                for k in (0, 1):
                    sp.wait_ge(st[k], ODD_EVEN[k] + 16)

            @block.gpsimd
            def _(pool):
                def gather(i, r, g):
                    hold(pool, inn[r], i * 32 + 32)
                    gather_rows(nc, pool, D.x1d, near[:, r], got[:, r], landed[r], EP - 1)
                ring_loop(pool, GROUPS, [gather])

            @block.vector
            def _(dve):
                dve.sem_inc(m["hn_done"], RING)
                dve.sem_inc(m["msg_done"], 2)
                dve.sem_inc(m["x2_done"], RING)
                nc.vector.memset(sums[:, 1, G_ROWS - 1:G_ROWS], 0.0).then_inc(m["carry"], 1)

                def sources(i, r, g):
                    dve.wait_ge(landed[r], i * 128 + 128)
                    yield from norm_s.dve(nc, dve, g, 0, got[:, r])
                    after(dve, m["hn_t"], g)
                    nc.vector.scalar_tensor_tensor(out=hn[:], in0=norm_s.xc, scalar=0.0, in1=spread(norm_s.rstd),
                                                   op0=ALU.max, op1=ALU.mult).then_inc(m["hn_done"], 1)

                def sums_of(i, r, g):
                    yield 3
                    dve.wait_ge(et_in[r % 2], half_turns(i, r) * 16 + 16)
                    dve.wait_ge(m["mm2"], g + 1)
                    nc.vector.scalar_tensor_tensor(out=msg[:], in0=bank(4, 2)[0:C], scalar=col["b2n"][0:C],
                                                   in1=et[:, r % 2], op0=ALU.add, op1=ALU.mult).then_inc(m["msg_done"], 1)
                    yield 6
                    dve.wait_ge(m["msg_done"], g + 3)
                    dve.wait_ge(m["carry"], g + 1)
                    after(dve, m["back"], g - 1)
                    run_sums(nc, W, g, r % 2, msg[:], sums, m)

                def dests(i, r, g):
                    dve.wait_ge(x_in[r], i * 16 + 16)
                    yield from norm_d.dve(nc, dve, g, 0, xd[:, r])
                    nc.vector.scalar_tensor_tensor(out=hd[:], in0=norm_d.xc, scalar=0.0, in1=spread(norm_d.rstd),
                                                   op0=ALU.max, op1=ALU.mult).then_inc(m["hd_done"], 1)
                    yield 9
                    dve.wait_ge(m["hd_done"], g + 1)
                    dve.wait_ge(m["back"], g + 1)
                    nc.vector.scalar_tensor_tensor(out=o1[:], in0=as_rows(bank(1)), scalar=col["res"], in1=hd[:],
                                                   op0=ALU.mult, op1=ALU.add).then_inc(m["o1_done"], 1)

                def normed(i, r, g):
                    yield 0
                    dve.wait_ge(m["o1_done"], g + 1)
                    yield from norm_o.dve(nc, dve, g, 0, o1[:])
                    after(dve, m["xn_t"], g)
                    nc.vector.tensor_tensor(xn[:], norm_o.xc, spread(norm_o.rstd), ALU.mult).then_inc(m["xn_done"], 1)

                def result(i, r, g):
                    yield 10
                    dve.wait_ge(st[r % 2], half_turns(i, r) * 16 + 16)
                    dve.wait_ge(m["residual"], g + 1)
                    nc.vector.tensor_tensor(x2[:, r % 2], xd[:, r], as_rows(bank(6)), ALU.add
                                            ).then_inc(m["x2_done"], 1)
                ring_loop(dve, GROUPS, [sources], [], [sums_of], [dests], [normed], [result])

            @block.tensor
            def _(pe):
                def b(i, r, g):
                    yield 0
                    hold(pe, m["hn_done"], g + RING + 1)
                    transpose_pairs(nc, bank(0), hn[:], W).then_inc(m["hn_t"], 1)
                    yield 2
                    hold(pe, m["hf_done"], g + 1)
                    hold(pe, m["hid_done"], g)
                    halves(nc, bank(2, 2), W.w1n, hf[:]).then_inc(m["mm1"], 1)
                    yield 6
                    hold(pe, m["hid_done"], g + 1)
                    hold(pe, m["msg_done"], g + 2)
                    for h in (0, 1):
                        part = slice(HALF * h, HALF * h + HALF)
                        for k in (0, 1):
                            last = nc.tensor.matmul(bank(4, 2)[0:C, part], W.w2n[:], hid[k][:, part],
                                                    start=k == 0, stop=k == 1)
                    last.then_inc(m["mm2"], 1)

                def back(i, r, g):
                    yield 1
                    hold(pe, m["carry"], g + 2)
                    hold(pe, m["o1_done"], g)
                    transpose_back(nc, bank(1), sums[:, r % 2], W).then_inc(m["back"], 1)

                def residual(i, r, g):
                    yield 1
                    hold(pe, m["xn_done"], g + 1)
                    transpose_pairs(nc, bank(7), xn[:], W).then_inc(m["xn_t"], 1)
                    yield 4
                    hold(pe, m["xf_done"], g + 1)
                    hold(pe, m["x2_done"], g + RING)
                    rows_by(nc, bank(6), xf[:], W.gamma1, W.beta_rows[:, 1], W).then_inc(m["residual"], 1)
                ring_loop(pe, GROUPS, [], [b], [], [back], [], [residual])

            @block.scalar
            def _(act):
                def sources(i, r, g):
                    yield from norm_s.act(nc, act, g, 0)

                def b(i, r, g):
                    yield 1
                    act.wait_ge(m["hn_t"], g + 1)
                    nc.scalar.activation(hf[:], bank(0), ACT.Copy).then_inc(m["hf_done"], 1)
                    yield 5
                    act.wait_ge(m["mm1"], g + 1)
                    leaky_parts(nc, hid, bank(2, 2), 0.1, col["b1n_slope"], col["b1n_rest"]).then_inc(m["hid_done"], 1)

                def dests(i, r, g):
                    yield from norm_d.act(nc, act, g, 0)

                def normed(i, r, g):
                    yield from norm_o.act(nc, act, g, 0)

                def residual(i, r, g):
                    yield 2
                    act.wait_ge(m["xn_t"], g + 1)
                    nc.scalar.activation(xf[:], bank(7), ACT.Copy).then_inc(m["xf_done"], 1)
                ring_loop(act, GROUPS, [sources], [b], [], [dests], [normed], [residual])


def relu_messages(nc, A, sem, W, D, bank):
    ctx = ExitStack()
    with ctx:
        t = lambda n, sh, dt=F32: ctx.enter_context(nc.sbuf_tensor(n, sh, dt))
        col = W.col
        near = t("l2_near", [P, RING, S], I32)
        got = t("l2_got", [P, RING, S, C])
        xd, x3 = (t("l2_" + n, [P, 2, S, C]) for n in ("xd", "x3"))
        hn = t("l2_hn", [P, S, C])
        msg, sums = t("l2_msg", [C, 2, G_ROWS]), t("l2_sums", [C, 2, G_ROWS])
        hf = t("l2_hf", [P, HALF])
        norm = Norm(sem, t, "l2_n")
        names = ("hn_done", "hn_t", "hf_done", "mm", "msg_done", "carry", "back", "x3_done")
        m = {n: sem("l2_" + n) for n in names}
        inn, landed = ([sem(f"l2_{n}{r}") for r in range(RING)] for n in ("in", "got"))
        x_in, st = ([sem(f"l2_{n}{k}") for k in (0, 1)] for n in ("x_in", "st"))
        with nc.Block() as block:
            @block.sync
            def _(sp):
                for k in (0, 1):
                    sp.sem_inc(st[k], 16)

                def load(i, r, g):
                    sp.wait_ge(m["hn_done"], g + 1)
                    sp.dma_start(near[:, r], D.ls[g]).then_inc(inn[r], 16)
                    sp.dma_start(got[:, r], group_rows(D.x2_lone)[g]).then_inc(inn[r], 16)

                def load_x(i, r, g):
                    sp.wait_ge(m["x3_done"], g + 1)
                    sp.dma_start(xd[:, r % 2], group_rows(D.x2d)[g]).then_inc(x_in[r % 2], 16)

                def store(i, r, g):
                    sp.wait_ge(m["x3_done"], g + 3)
                    sp.dma_start(group_rows(D.x3d)[g], x3[:, r % 2]).then_inc(st[r % 2], 16)
                ring_loop(sp, GROUPS, [load], [], [], [], [load_x], [], [store])
                for k in (0, 1):
                    sp.wait_ge(st[k], ODD_EVEN[k] + 16)

            @block.gpsimd
            def _(pool):
                def gather(i, r, g):
                    hold(pool, inn[r], i * 32 + 32)
                    gather_rows(nc, pool, D.x2d, near[:, r], got[:, r], landed[r], EP - 1)
                ring_loop(pool, GROUPS, [gather])

            @block.vector
            def _(dve):
                dve.sem_inc(m["hn_done"], RING)
                dve.sem_inc(m["x3_done"], 2)
                nc.vector.memset(sums[:, 1, G_ROWS - 1:G_ROWS], 0.0).then_inc(m["carry"], 1)

                def sources(i, r, g):
                    dve.wait_ge(landed[r], i * 128 + 128)
                    yield from norm.dve(nc, dve, g, 0, got[:, r])
                    after(dve, m["hn_t"], g)
                    nc.vector.scalar_tensor_tensor(out=hn[:], in0=norm.xc, scalar=0.0, in1=spread(norm.rstd),
                                                   op0=ALU.max, op1=ALU.mult).then_inc(m["hn_done"], 1)

                def scan(i, r, g):
                    yield 3
                    dve.wait_ge(m["msg_done"], g + 1)
                    dve.wait_ge(m["carry"], g + 1)
                    after(dve, m["back"], g - 1)
                    run_sums(nc, W, g, r % 2, msg[:, r % 2], sums, m)

                def result(i, r, g):
                    yield 6
                    dve.wait_ge(x_in[r % 2], half_turns(i, r) * 16 + 16)
                    dve.wait_ge(st[r % 2], half_turns(i, r) * 16 + 16)
                    dve.wait_ge(m["back"], g + 1)
                    nc.vector.tensor_tensor(x3[:, r % 2], xd[:, r % 2], as_rows(bank(1)), ALU.add).then_inc(m["x3_done"], 1)
                ring_loop(dve, GROUPS, [sources], [], [scan], [result])

            @block.tensor
            def _(pe):
                def b(i, r, g):
                    yield 0
                    hold(pe, m["hn_done"], g + RING + 1)
                    transpose_pairs(nc, bank(0), hn[:], W).then_inc(m["hn_t"], 1)
                    yield 2
                    hold(pe, m["hf_done"], g + 1)
                    hold(pe, m["msg_done"], g)
                    halves(nc, bank(2, 2)[0:C], W.l2w, hf[:]).then_inc(m["mm"], 1)

                def back(i, r, g):
                    yield 3
                    hold(pe, m["carry"], g + 2)
                    hold(pe, m["x3_done"], g + 2)
                    transpose_back(nc, bank(1), sums[:, r % 2], W).then_inc(m["back"], 1)
                ring_loop(pe, GROUPS, [], [b], [], [back])

            @block.scalar
            def _(act):
                def sources(i, r, g):
                    yield from norm.act(nc, act, g, 0)

                def b(i, r, g):
                    yield 1
                    act.wait_ge(m["hn_t"], g + 1)
                    nc.scalar.activation(hf[:], bank(0), ACT.Copy).then_inc(m["hf_done"], 1)
                    yield 5
                    after(act, m["carry"], g)
                    act.wait_ge(m["mm"], g + 1)
                    nc.scalar.activation(msg[:, r % 2], bank(2, 2)[0:C], ACT.Relu, bias=col["l2b"][0:C]
                                         ).then_inc(m["msg_done"], 1)
                ring_loop(act, GROUPS, [sources], [b])


def edge_convolution(nc, A, sem, W, D, bank, stats):
    ctx = ExitStack()
    with ctx:
        t = lambda n, sh, dt=F32: ctx.enter_context(nc.sbuf_tensor(n, sh, dt))
        col = W.col
        near = t("l3_near", [P, RING, S], I32)
        got, xd = (t("l3_" + n, [P, RING, S, C]) for n in ("got", "xd"))
        hn, dn = (t("l3_" + n, [P, S, C]) for n in ("hn", "dn"))
        neg, hh = (t("l3_" + n, [C, 2, G_ROWS]) for n in ("neg", "hh"))
        ended = t("l3_ended", [C, 2, G_ROWS])
        nxt = t("l3_nxt", [C, 2, G_ROWS], U8)
        hf, df = t("l3_hf", [P, HALF]), t("l3_df", [P, HALF])
        norm_s, norm_d = Norm(sem, t, "l3_s"), Norm(sem, t, "l3_d")
        names = ("hn_done", "hn_t", "hf_done", "mm", "ended", "carry", "hh_done", "stats", "nxt_done")
        m = {n: sem("l3_" + n) for n in names}
        inn, landed = ([sem(f"l3_{n}{r}") for r in range(RING)] for n in ("in", "got"))
        st = [sem(f"l3_st{k}") for k in (0, 1)]
        back = lambda g: g * -1 + (GROUPS - 1)
        with nc.Block() as block:
            @block.sync
            def _(sp):
                for k in (0, 1):
                    sp.sem_inc(st[k], 16)

                def load(i, r, g):
                    sp.wait_ge(m["hn_done"], g + 1)
                    sp.dma_start(near[:, r], D.ls[back(g)]).then_inc(inn[r], 16)
                    sp.dma_start(got[:, r], group_rows(D.x2_lone)[back(g)]).then_inc(inn[r], 16)
                    sp.dma_start(xd[:, r], group_rows(D.x3d)[back(g)]).then_inc(inn[r], 16)

                def store(i, r, g):
                    sp.wait_ge(m["hh_done"], g + 1)
                    sp.dma_start(group_cols(D.hh)[back(g)], hh[:, r % 2]).then_inc(st[r % 2], 16)
                ring_loop(sp, GROUPS, [load], [], [], [], [], [store])
                for k in (0, 1):
                    sp.wait_ge(st[k], ODD_EVEN[k] + 16)

            @block.gpsimd
            def _(pool):
                def gather(i, r, g):
                    hold(pool, inn[r], i * 48 + 48)
                    gather_rows(nc, pool, D.x3d, near[:, r], got[:, r], landed[r], EP - 1)
                ring_loop(pool, GROUPS, [gather])

            @block.vector
            def _(dve):
                dve.sem_inc(m["hn_done"], RING)
                nc.vector.memset(neg[:, 1, 0:1], 0.0).then_inc(m["carry"], 1)

                def dests(i, r, g):
                    dve.wait_ge(inn[r], i * 48 + 48)
                    yield from norm_d.dve(nc, dve, g, 0, xd[:, r])
                    after(dve, m["hn_t"], g)
                    nc.vector.scalar_tensor_tensor(out=dn[:], in0=norm_d.xc, scalar=0.0, in1=spread(norm_d.rstd),
                                                   op0=ALU.max, op1=ALU.mult)

                def sources(i, r, g):
                    dve.wait_ge(landed[r], i * 128 + 128)
                    yield from norm_s.dve(nc, dve, g, 0, got[:, r])
                    after(dve, m["hn_t"], g)
                    nc.vector.scalar_tensor_tensor(out=hn[:], in0=norm_s.xc, scalar=0.0, in1=spread(norm_s.rstd),
                                                   op0=ALU.max, op1=ALU.mult).then_inc(m["hn_done"], 1)

                def c(i, r, g):
                    yield 3
                    dve.wait_ge(m["nxt_done"], g + 1)
                    dve.wait_ge(m["mm"], g + 1)
                    nc.vector.scalar_tensor_tensor(out=ended[:, r % 2], in0=nxt[:, r % 2], scalar=-1.0,
                                                   in1=bank(2, 2)[0:C], op0=ALU.add, op1=ALU.mult).then_inc(m["ended"], 1)

                def scan(i, r, g):
                    yield 2
                    dve.wait_ge(m["ended"], g + 1)
                    dve.wait_ge(m["carry"], g + 1)
                    nc.vector.tensor_tensor_scan(neg[:, r % 2, ::-1], nxt[:, r % 2, ::-1], ended[:, r % 2, ::-1],
                                                 neg[:, 1 - r % 2, 0:1], ALU.mult, ALU.add).then_inc(m["carry"], 1)
                    yield 6
                    dve.wait_ge(m["carry"], g + 2)
                    dve.wait_ge(st[r % 2], half_turns(i, r) * 16 + 16)
                    nc.vector.scalar_tensor_tensor(out=hh[:, r % 2], in0=bank(4 + 2 * (r % 2), 2)[0:C],
                                                   scalar=col["l3b"][0:C], in1=neg[:, r % 2], op0=ALU.add,
                                                   op1=ALU.subtract).then_inc(m["hh_done"], 1)
                    yield 8
                    dve.wait_ge(m["hh_done"], g + 1)
                    for h in (0, 1):
                        at = bass.ds(back(g) * 12 + 6 * h, 6)
                        nc.vector.bn_stats(stats[:, at], hh[:, r % 2, HALF * h:HALF * h + HALF]).then_inc(m["stats"], 1)
                ring_loop(dve, GROUPS, [dests, sources], [], [c], [scan])
                dve.wait_ge(m["stats"], 2 * GROUPS)

            @block.tensor
            def _(pe):
                def b(i, r, g):
                    yield 0
                    hold(pe, m["hn_done"], g + RING + 1)
                    hold(pe, m["hf_done"], g)
                    transpose_pairs(nc, bank(1), dn[:], W)
                    transpose_pairs(nc, bank(0), hn[:], W).then_inc(m["hn_t"], 1)

                def c(i, r, g):
                    yield 1
                    hold(pe, m["hf_done"], g + 1)
                    hold(pe, m["ended"], g)
                    hold(pe, m["hh_done"], g - 1)
                    halves(nc, bank(2, 2)[0:C], W.l3ab, df[:])
                    halves(nc, bank(4 + 2 * (r % 2), 2)[0:C], W.l3b, hf[:]).then_inc(m["mm"], 1)
                ring_loop(pe, GROUPS, [], [b], [c])

            @block.scalar
            def _(act):
                def norms(i, r, g):
                    yield from norm_d.act(nc, act, g, 0)

                def norms_s(i, r, g):
                    yield from norm_s.act(nc, act, g, 0)

                def b(i, r, g):
                    yield 2
                    act.wait_ge(m["hn_t"], g + 1)
                    after(act, m["mm"], g)
                    nc.scalar.activation(df[:], bank(1), ACT.Copy)
                    nc.scalar.activation(hf[:], bank(0), ACT.Copy).then_inc(m["hf_done"], 1)
                    yield 5
                    after(act, m["carry"], g)
                    nc.scalar.activation(nxt[:, r % 2], W.same[:, bass.ds(back(g) * G_ROWS + 1, G_ROWS)], ACT.Copy
                                         ).then_inc(m["nxt_done"], 1)
                ring_loop(act, GROUPS, [norms, norms_s], [b])


def finish_rows(nc, A, sem, W, D, bank, out, stats):
    ctx = ExitStack()
    with ctx:
        t = lambda n, sh, dt=F32: ctx.enter_context(nc.sbuf_tensor(n, sh, dt))
        col = W.col
        near = t("fi_near", [P, RING, S], I32)
        res = t("fi_res", [P, RING, S, C])
        xd = t("fi_xd", [P, 2, S, C])
        avg = t("fi_avg", [P, S, C])
        hh, z, sums = (t("fi_" + n, [C, 2, G_ROWS]) for n in ("hh", "z", "sums"))
        msg = t("fi_msg", [C, G_ROWS])
        inv = t("fi_inv", [P, GROUPS, S])
        tail_n = EDGES % HALF
        tail = t("fi_tail", [C, tail_n])
        mv, sc = t("fi_mv", [C, 2]), t("fi_sc", [C, 4])
        names = ("tail", "bn_step", "root", "z_done", "msg_done", "carry", "avg_done", "back", "res_done", "freed")
        m = {n: sem("fi_" + n) for n in names}
        ids_in, st = ([sem(f"fi_{n}{r}") for r in range(RING)] for n in ("ids", "st"))
        hh_in, x_in = ([sem(f"fi_{n}{k}") for k in (0, 1)] for n in ("hh_in", "x_in"))
        with nc.Block() as block:
            @block.sync
            def _(sp):
                sp.dma_start(tail[:], D.hh[:, EDGES - tail_n:EDGES]).then_inc(m["tail"], 16)

                def load(i, r, g):
                    sp.wait_ge(m["z_done"], g + 1)
                    sp.dma_start(hh[:, r % 2], group_cols(D.hh)[g]).then_inc(hh_in[r % 2], 16)

                def load_x(i, r, g):
                    sp.wait_ge(m["res_done"], g + 1)
                    sp.dma_start(xd[:, r % 2], group_rows(D.x3d)[g]).then_inc(x_in[r % 2], 16)
                    sp.wait_ge(m["freed"], g + 1)
                    sp.dma_start(near[:, r], D.final_idx[g]).then_inc(ids_in[r], 16)
                ring_loop(sp, GROUPS, [load], [], [load_x])

            @block.gpsimd
            def _(pool):
                pool.sem_inc(m["freed"], RING)

                def scatter(i, r, g):
                    hold(pool, ids_in[r], i * 16 + 16)
                    hold(pool, m["res_done"], g + 3)
                    for q in range(S):
                        nc.gpsimd.indirect_dma_start(
                            out=out, out_offset=bass.IndirectOffsetOnAxis(ap=near[:, r, q:q + 1], axis=0),
                            in_=res[:, r, q], in_offset=None, bounds_check=NP_ - 1, oob_is_err=False
                        ).then_inc(st[r], 16)

                def free(i, r, g):
                    hold(pool, st[r], i * 128 + 128)
                    pool.sem_inc(m["freed"], 1)
                ring_loop(pool, GROUPS, [scatter], [free])

            @block.vector
            def _(dve):
                n = [0]

                def done(ins):
                    n[0] += 1
                    ins.then_inc(m["bn_step"], 1)

                def wait():
                    dve.wait_ge(m["bn_step"], n[0])
                dve.sem_inc(m["res_done"], 2)
                done(nc.vector.reciprocal(inv[:], W.countE[:]))
                done(nc.vector.memset(sums[:, 1, G_ROWS - 1:G_ROWS], 0.0))
                dve.wait_ge(m["tail"], 16)
                at = 6 * ((EDGES - tail_n) // HALF)
                done(nc.vector.bn_stats(stats[:, at:at + 6], tail[:]))
                wait()
                done(nc.vector.bn_aggr(mv[:], stats[:, 0:at + 6]))
                wait()
                done(nc.vector.tensor_scalar(sc[:, 0:1], mv[:, 1:2], EPS, None, ALU.add))
                dve.wait_ge(m["root"], 1)
                done(nc.vector.reciprocal(sc[:, 0:1], sc[:, 1:2]))
                wait()
                done(nc.vector.tensor_tensor(sc[:, 2:3], sc[:, 0:1], col["bn_gamma"][0:C], ALU.mult))
                wait()
                done(nc.vector.tensor_tensor(sc[:, 3:4], mv[:, 0:1], sc[:, 2:3], ALU.mult))
                wait()
                done(nc.vector.tensor_tensor(sc[:, 3:4], col["bn_beta"][0:C], sc[:, 3:4], ALU.subtract))
                wait()
                dve.sem_inc(m["carry"], 1)
                assert n[0] == BN_STEPS

                def a(i, r, g):
                    dve.wait_ge(m["z_done"], g + 3)
                    after(dve, m["carry"], g + 1)
                    nc.vector.scalar_tensor_tensor(out=msg[:], in0=z[:, r % 2], scalar=0.3, in1=z[:, r % 2], op0=ALU.mult,
                                                   op1=ALU.max).then_inc(m["msg_done"], 1)
                    yield 2
                    dve.wait_ge(m["msg_done"], g + 1)
                    dve.wait_ge(m["carry"], g + 1)
                    after(dve, m["back"], g - 1)
                    run_sums(nc, W, g, r % 2, msg[:], sums, m)

                def b(i, r, g):
                    yield 1
                    dve.wait_ge(m["back"], g + 1)
                    dve.wait_ge(m["res_done"], g + 2)
                    nc.vector.tensor_tensor(avg[:], as_rows(bank(1)),
                                            spread(inv[:, bass.ds(g, 1)].rearrange("p a s -> p (a s)")), ALU.mult
                                            ).then_inc(m["avg_done"], 1)
                    yield 3
                    dve.wait_ge(x_in[r % 2], half_turns(i, r) * 16 + 16)
                    dve.wait_ge(m["freed"], g + 1)
                    dve.wait_ge(m["avg_done"], g + 1)
                    nc.vector.tensor_tensor(res[:, r], xd[:, r % 2], avg[:], ALU.add).then_inc(m["res_done"], 1)
                ring_loop(dve, GROUPS, [a], [b])

            @block.tensor
            def _(pe):
                def work(i, r, g):
                    hold(pe, m["carry"], g + 2)
                    hold(pe, m["avg_done"], g)
                    transpose_back(nc, bank(1), sums[:, r % 2], W).then_inc(m["back"], 1)
                ring_loop(pe, GROUPS, [work])

            @block.scalar
            def _(act):
                act.wait_ge(m["bn_step"], 5)
                nc.scalar.activation(sc[:, 1:2], sc[:, 0:1], ACT.Sqrt).then_inc(m["root"], 1)
                act.wait_ge(m["bn_step"], BN_STEPS)
                act.sem_inc(m["z_done"], 2)

                def work(i, r, g):
                    act.wait_ge(hh_in[r % 2], half_turns(i, r) * 16 + 16)
                    after(act, m["msg_done"], g - 1)
                    nc.scalar.activation(z[:, r % 2], hh[:, r % 2], ACT.Identity, bias=sc[:, 3:4], scale=sc[:, 2:3]
                                         ).then_inc(m["z_done"], 1)
                ring_loop(act, GROUPS, [work])


def lay_out(inputs):
    import numpy as np
    a = {k: np.ascontiguousarray(v) for k, v in inputs.items()}
    src, dst = a.pop("src").astype(np.int32), a.pop("dst").astype(np.int32)
    ew, ea, x = a.pop("edge_weight"), a.pop("edge_attr_32"), a.pop("x")

    def padded(v, fill):
        return np.concatenate([v, np.full((EP - EDGES,) + v.shape[1:], fill, v.dtype)])

    def rows(v):
        return np.ascontiguousarray(v.reshape(GROUPS, 2, S // 2, P).transpose(0, 3, 2, 1).reshape(GROUPS, P, S))

    end = np.array([-2], np.int32)
    dp = padded(dst, NODES)
    a["src_rows"], a["dst_rows"] = rows(padded(src, 0)), rows(dp)
    a["next_rows"] = rows(np.concatenate([dp[1:], end]))
    a["ew_rows"] = rows(padded(ew, 0))
    a["dst_line"] = np.concatenate([end, dp, end])[None]
    a["ea_cols"] = np.ascontiguousarray(padded(ea, 0).T)
    a["x"] = np.concatenate([x, np.zeros((NP_ - NODES, C), x.dtype)])
    a["l3_wt"] = np.ascontiguousarray(a.pop("L3_gnn_W").T)
    return a


def kernel(**inputs):
    import concourse.bacc as bacc
    from concourse.bass_utils import run_bass_kernel_spmd
    arrays = lay_out(inputs)
    nc = bacc.Bacc("TRN2", target_bir_lowering=False, num_devices=1)
    args = {n: nc.dram_tensor("in_" + n, v.shape, mybir.dt.from_np(v.dtype), kind="ExternalInput").ap()
            for n, v in arrays.items()}
    out = nc.dram_tensor("out_0", (NP_, C), F32, kind="ExternalOutput").ap()
    build(nc, args, out)
    r = run_bass_kernel_spmd(nc, [{"in_" + n: v for n, v in arrays.items()}], core_ids=[0])
    return r.results[0]["out_0"][:NODES]
```

```python
from contextlib import ExitStack
import concourse.bass as bass
from concourse import mybir

ALU = mybir.AluOpType
ACT = mybir.ActivationFunctionType
F32 = mybir.dt.float32
I32 = mybir.dt.int32
BF16 = mybir.dt.bfloat16
F16 = mybir.dt.float16
U8 = mybir.dt.uint8
AX_X = mybir.AxisListType.X

P = 128
C = 64
S = 8
G_ROWS = P * S
HALF = G_ROWS // 2
EDGES, NODES = 50000, 100000
GROUPS = -(-EDGES // G_ROWS)
EP = GROUPS * G_ROWS
NODE_GROUPS = -(-NODES // G_ROWS)
NP_ = NODE_GROUPS * G_ROWS
TILES = GROUPS * S
HEADS = 4
EDIM = 32
LO_BITS = 10
LO = 1 << LO_BITS
HI = NP_ // LO
NOWHERE = 1.0e6
FAR = 1.0e30
EPS = 1e-5
PARTS = 3
CHUNK = EP // P
ALPHAS = 2 * HEADS + 1
EXCHANGES = (HEADS, HEADS, HEADS, HEADS + 1, HEADS)
BN_STEPS = 9
PREP_STEPS = 22
ODD_EVEN = (16 * ((GROUPS + 1) // 2), 16 * (GROUPS // 2))
RING = 4


def of_slot(r, n):
    return (n - r + RING - 1) // RING


def take_turns(stages):
    due = [(0, k, gen) for k, gen in enumerate(stages)]
    while due:
        due.sort(key=lambda x: x[:2])
        t, k, gen = due.pop(0)
        nxt = next(gen, None)
        if nxt is not None:
            assert nxt >= t, (nxt, t)
            due.append((nxt, k, gen))


def ring_loop(eng, n, *lags):
    k_max = len(lags) + 1
    assert n > k_max + RING

    def step(group_of):
        started = []
        for k, stages in enumerate(lags):
            at = group_of(k)
            if at is not None:
                started += [s for s in (f(*at) for f in stages) if s is not None]
        take_turns(started)

    def fixed(s):
        def at(k):
            g = s - k
            return (g // RING, g % RING, g) if 0 <= g < n else None
        step(at)

    for s in range(k_max):
        fixed(s)
    turns = (n - k_max) // RING
    with eng.Fori(0, turns) as i:
        for q in range(RING):
            def at(k):
                off = k_max + q - k
                return i + off // RING, off % RING, i * RING + off
            step(at)
    for s in range(k_max + RING * turns, n + len(lags) - 1):
        fixed(s)


def hold(eng, sem, value):
    if not (isinstance(value, int) and value < 1):
        eng.wait_ge(sem, value)
        eng.sem_inc(HELD[0], 1)


def after(eng, sem, value):
    if not (isinstance(value, int) and value < 1):
        eng.wait_ge(sem, value)


def of_group(x, g):
    return x[:, bass.ds(g, 1)].rearrange("p a s -> p (a s)")


def half_turns(i, r):
    return i * 2 + r // 2


HELD = [None]


class Norm:

    def __init__(self, sem, t, name, per=1):
        self.per = per
        self.step, self.centred, self.squared, self.varied, self.rooted = (
            sem(f"{name}_{n}") for n in ("dve_step", "centred", "squared", "variance", "rooted"))
        self.xc, self.sq = t(name + "_xc", [P, S, C])[:], t(name + "_sq", [P, S, C])[:]
        self.sum, self.var, self.sd, self.rstd = (t(f"{name}_{n}", [P, S])[:] for n in ("sum", "var", "sd", "rstd"))

    def dve(self, nc, dve, g, k, x, t=0):
        n = g * self.per + k
        yield t
        nc.vector.reduce_sum(self.sum, x, AX_X).then_inc(self.step, 1)
        yield t + 2
        dve.wait_ge(self.step, n * 3 + 1)
        nc.vector.scalar_tensor_tensor(out=self.xc, in0=spread(self.sum), scalar=-1.0 / C, in1=x, op0=ALU.mult,
                                       op1=ALU.add).then_inc(self.centred, 1)
        yield t + 4
        dve.wait_ge(self.squared, n + 1)
        nc.vector.reduce_sum(self.var, self.sq, AX_X).then_inc(self.step, 1)
        yield t + 5
        dve.wait_ge(self.step, n * 3 + 2)
        nc.vector.tensor_scalar(self.var, self.var, 1.0 / C, EPS, ALU.mult, ALU.add).then_inc(self.varied, 1)
        yield t + 7
        dve.wait_ge(self.rooted, n + 1)
        nc.vector.reciprocal(self.rstd, self.sd).then_inc(self.step, 1)
        yield t + 8
        dve.wait_ge(self.step, n * 3 + 3)

    def act(self, nc, act, g, k, t=0):
        n = g * self.per + k
        yield t + 3
        act.wait_ge(self.centred, n + 1)
        nc.scalar.activation(self.sq, self.xc, ACT.Square).then_inc(self.squared, 1)
        yield t + 6
        act.wait_ge(self.varied, n + 1)
        nc.scalar.activation(self.sd, self.var, ACT.Sqrt).then_inc(self.rooted, 1)


class NormTwice:

    def __init__(self, sem, t, name):
        self.summed, self.step, self.centred, self.relu, self.squared, self.varied, self.rooted = (
            sem(f"{name}_{n}") for n in ("summed", "dve_step", "centred", "relu", "squared", "variance", "rooted"))
        self.xc = t(name + "_xc", [P, S, C])[:]
        self.three = t(name + "_three", [P, 3, S, C])[:]
        self.y = self.three[:, 1]
        self.sum, self.my2, self.vy = (t(f"{name}_{n}", [P, S])[:] for n in ("sum", "my2", "vy"))
        self.sums = t(name + "_sums", [P, 3, S])[:]
        self.var, self.sd, self.inv = (t(f"{name}_{n}", [P, 2, S])[:] for n in ("var", "sd", "inv"))
        self.first, self.gain = self.inv[:, 0], self.inv[:, 1]

    def centre(self, nc, dve, g, x, ticks=(0, 2)):
        yield ticks[0]
        nc.vector.reduce_sum(self.sum, x, AX_X).then_inc(self.summed, 1)
        yield ticks[1]
        dve.wait_ge(self.summed, g + 1)
        nc.vector.scalar_tensor_tensor(out=self.xc, in0=spread(self.sum), scalar=-1.0 / C, in1=x, op0=ALU.mult,
                                       op1=ALU.add).then_inc(self.centred, 1)

    def scale(self, nc, dve, g, ticks=(5, 7, 8, 9, 11, 12)):
        yield ticks[0]
        dve.wait_ge(self.squared, g + 1)
        nc.vector.reduce_sum(self.sums, self.three, AX_X).then_inc(self.step, 1)
        yield ticks[1]
        dve.wait_ge(self.step, g * 4 + 1)
        nc.vector.scalar_tensor_tensor(out=self.my2, in0=self.sums[:, 1], scalar=1.0 / C ** 2, in1=self.sums[:, 1],
                                       op0=ALU.mult, op1=ALU.mult).then_inc(self.step, 1)
        nc.vector.tensor_scalar(self.var[:, 0], self.sums[:, 0], 1.0 / C, EPS, ALU.mult, ALU.add)
        yield ticks[2]
        dve.wait_ge(self.step, g * 4 + 2)
        nc.vector.scalar_tensor_tensor(out=self.vy, in0=self.sums[:, 2], scalar=1.0 / C, in1=self.my2, op0=ALU.mult,
                                       op1=ALU.subtract).then_inc(self.step, 1)
        yield ticks[3]
        dve.wait_ge(self.step, g * 4 + 3)
        nc.vector.scalar_tensor_tensor(out=self.var[:, 1], in0=self.var[:, 0], scalar=EPS, in1=self.vy, op0=ALU.mult,
                                       op1=ALU.add).then_inc(self.varied, 1)
        yield ticks[4]
        dve.wait_ge(self.rooted, g + 1)
        nc.vector.reciprocal(self.inv, self.sd).then_inc(self.step, 1)
        yield ticks[5]
        dve.wait_ge(self.step, g * 4 + 4)

    def square(self, nc, act, g, ticks=(3, 4)):
        yield ticks[0]
        act.wait_ge(self.centred, g + 1)
        nc.scalar.activation(self.y, self.xc, ACT.Relu).then_inc(self.relu, 1)
        nc.scalar.activation(self.three[:, 0], self.xc, ACT.Square)
        yield ticks[1]
        act.wait_ge(self.relu, g + 1)
        nc.scalar.activation(self.three[:, 2], self.y, ACT.Square).then_inc(self.squared, 1)

    def root(self, nc, act, g, tick=10):
        yield tick
        act.wait_ge(self.varied, g + 1)
        nc.scalar.activation(self.sd, self.var, ACT.Sqrt).then_inc(self.rooted, 1)


def group_rows(a):
    return a.rearrange("(g p s) c -> g p s c", p=P, s=S)


def group_cols(a):
    return a.rearrange("f (g e) -> g f e", e=G_ROWS)


def pairs(a):
    return a.rearrange("f (g e) -> g f e", e=HALF)


def slot_cols(n):
    at = (n % 2) * HALF + (n // 2) * P
    return slice(at, at + P)


def transpose_rows(nc, out, rows, W):
    for n in range(S):
        last = nc.tensor.transpose(out[0:C, slot_cols(n)], rows[:, n], W.ident[:])
    return last


def transpose_pairs(nc, out, rows, W):
    flat = rows.rearrange("p s c -> p (s c)")
    for n in range(S // 2):
        last = nc.tensor.transpose(out[:, P * n:P * n + P], flat[:, P * n:P * n + P], W.ident[:])
    return last


def transpose_back(nc, out, columns, W):
    for n in range(S):
        last = nc.tensor.transpose(out[:, C * n:C * n + C], columns[:, slot_cols(n)], W.ident[0:C, 0:C])
    return last


def halves(nc, out, weights, paired):
    for h in (0, 1):
        last = nc.tensor.matmul(out[:, HALF * h:HALF * h + HALF], weights[:, h], paired, start=True, stop=True)
    return last


def leaky_parts(nc, out, x, slope, bias=None, rest=None):
    b = dict(bias=bias) if bias is not None else {}
    r = dict(bias=rest) if rest is not None else {}
    nc.scalar.activation(out[0], x, ACT.Identity, scale=slope, **b)
    return nc.scalar.activation(out[1], x, ACT.Relu, scale=1.0 - slope, **r)


def sum_transposed(nc, out, parts, W, n):
    k = parts[0].shape[0]
    for q in range(n):
        at = slice(P * q, P * q + P) if n < S else slot_cols(q)
        for j in (0, 1):
            last = nc.tensor.matmul(out[:, k * q:k * q + k], parts[j][:, at], W.ident[0:k, 0:k],
                                    start=j == 0, stop=j == 1)
    return last


def as_rows(x):
    return x.rearrange("p (s c) -> p s c", c=C)


def spread(v):
    return v.unsqueeze(2).to_broadcast([P, S, C])


def along(v):
    return v.unsqueeze(1).to_broadcast([P, S, C])


class Bufs:
    pass


def build(nc, A, out):
    ctx = ExitStack()
    with ctx:
        def sb(name, shape, dt=F32):
            return ctx.enter_context(nc.sbuf_tensor(name, shape, dt))

        def sem(name):
            return ctx.enter_context(nc.semaphore(name))

        def dram(name, shape, dt=F32):
            return nc.dram_tensor(name, shape, dt, kind=KIND).ap()

        KIND = "Internal"
        ps = ctx.enter_context(nc.psum_tensor("ps", [P, 4096], F32))
        bank = lambda n, k=1: ps[:, 512 * n:512 * (n + k)]

        D = Bufs()
        (D.xs, D.t0s, D.h_lone, D.x1_lone, D.x2_lone, D.tx1, D.hd, D.hs, D.x1d, D.x2d, D.x3d) = (
            dram("d_" + name, (EP, C)) for name in
            ("xs", "t0s", "h_lone", "x1_lone", "x2_lone", "tx1", "hd", "hs", "x1d", "x2d", "x3d"))
        D.table = dram("d_table", (NP_, 2))
        D.ls = dram("d_ls", (GROUPS, P, S), I32)
        D.final_idx = dram("d_final_idx", (GROUPS, P, S), I32)
        D.et = dram("d_et", (C, EP))
        D.pd = dram("d_pd", (C, EP))
        D.hh = dram("d_hh", (C, EP))
        D.att_s = dram("d_att_s", (HEADS, EP))
        D.att_d = dram("d_att_d", (2 * HEADS, EP))
        D.alpha = dram("d_alpha", (ALPHAS, EP))

        W = Bufs()
        W.ident = sb("ident", [P, P])
        W.w02 = sb("w02", [P, P])
        W.w1 = sb("w1", [C, C])
        W.w2x2 = sb("w2x2", [C, C])
        W.gmean = sb("gmean", [P, P])
        W.gatw = sb("gatw", [P, 2, C])
        W.att = sb("att", [C, 2, HEADS])
        W.att_half = sb("att_half", [P, 2, HEADS])
        W.w1n = sb("w1n", [P, 2, P])
        W.w2n = sb("w2n", [P, C])
        W.w1e = sb("w1e", [2 * EDIM, P])
        W.w2e = sb("w2e", [P, P])
        W.l2w = sb("l2w", [P, 2, C])
        W.l3b = sb("l3b", [P, 2, C])
        W.l3ab = sb("l3ab", [P, 2, C])
        W.vecs = sb("vecs", [P, 16])
        VEC = ("cheb_b", "gat_b", "b1n", "b1e", "ln_gamma", "ln_beta", "b2n", "b2e", "dp", "res", "l2b",
               "l3b", "bn_gamma", "bn_beta")
        W.slanted = sb("slanted", [P, 2, 4])
        col = {n: W.vecs[:, i:i + 1] for i, n in enumerate(VEC)}
        for i, n in enumerate(VEC[:4]):
            col[n + "_slope"], col[n + "_rest"] = W.slanted[:, 0, i:i + 1], W.slanted[:, 1, i:i + 1]
        W.rows = sb("rowvecs", [P, 4, C])
        W.idsE = sb("idsE", [P, 2 * GROUPS, S], I32)
        srcE, dstE = W.idsE[:, 0:GROUPS], W.idsE[:, GROUPS:2 * GROUPS]
        W.countE = sb("countE", [P, GROUPS, S])
        lastE = sb("lastE", [P, GROUPS, S])
        W.finE = sb("finE", [P, GROUPS, S], I32)
        W.posE = sb("posE", [P, GROUPS, S], I32)
        ewE = sb("ewE", [P, GROUPS, S])
        wE = sb("wE", [P, GROUPS, S])
        same = sb("same", [C, EP + 1], U8)

        with ExitStack() as loc:
            t = lambda n, sh, dt=F32: loc.enter_context(nc.sbuf_tensor(n, sh, dt))
            loaded, stepped, consts, masks_used = map(sem, (
                "weights_loaded", "prep_step", "pool_consts", "masks_used"))
            masks_in = [sem(f"masks_loaded{r}") for r in range(RING)]
            gw2 = t("gw2", [P, HEADS, C])
            chw = t("chw", [P, 3, C])
            attb = t("attb", [C, 2, HEADS, C])
            prod = t("attprod", [C, 2, HEADS, C])
            dnE = t("dnE", [P, GROUPS, S], I32)
            idx0 = t("finidx", [P, GROUPS, S])
            l3a = t("l3a", [P, C])
            pairrow = t("pairrow", [C, RING, 2, G_ROWS], I32)
            linear = A["dst_line"]
            n_loads = [0]
            fin_st = sem("final_idx_stored")
            with nc.Block() as block:
                @block.sync
                def _(sp):
                    def ld(o, i):
                        n_loads[0] += 1
                        sp.dma_start(o, i).then_inc(loaded, 16)
                    sp.wait_ge(consts, 1)
                    for h in (0, 1):
                        lanes = slice(C * h, C * h + C)
                        ld(gw2[lanes], A["L0_gnn_gat_w"].rearrange("k (h f) -> k h f", h=HEADS))
                        ld(chw[lanes], A["L0_gnn_cheb_w"].rearrange("k i o -> i k o"))
                        ld(W.w1n[lanes, h, :], A["L1_gnn_W1n"])
                        ld(W.l2w[lanes, h, :], A["L2_gnn_W"])
                        ld(W.l3b[lanes, h, :], A["l3_wt"][C:2 * C, :])
                        ld(l3a[lanes], A["l3_wt"][0:C, :])
                        for n, name in (("ln_gamma", "L0_gnn_ln_gamma"), ("ln_beta", "L0_gnn_ln_beta"),
                                        ("cheb_b", "L0_gnn_cheb_b"), ("gat_b", "L0_gnn_gat_b"),
                                        ("b2n", "L1_gnn_b2n"), ("b1e", "L1_gnn_b1e"), ("b2e", "L1_gnn_b2e"),
                                        ("l2b", "L2_gnn_b"), ("l3b", "L3_gnn_b"),
                                        ("bn_gamma", "L3_gnn_gamma"), ("bn_beta", "L3_gnn_beta")):
                            ld(col[n][lanes], A[name].rearrange("(c a) -> c a", a=1))
                    ld(col["b1n"], A["L1_gnn_b1n"].rearrange("(c a) -> c a", a=1))
                    ld(col["dp"], A["L1_gnn_dp_scale"].rearrange("(c a) -> c a", a=1).to_broadcast([P, 1]))
                    ld(col["res"], A["L1_gnn_res_w"].rearrange("(c a) -> c a", a=1).to_broadcast([P, 1]))
                    ld(W.w1[:], A["L0_gnn_cheb_w"][1])
                    ld(W.w2x2[:], A["L0_gnn_cheb_w"][2])
                    for q in (0, 1):
                        ld(W.gatw[C * q:C * q + C], A["L0_gnn_gat_w"].rearrange("k (a b f) -> b k a f", a=2, b=2)[q])
                    for q, name in enumerate(("L0_gnn_att_src", "L0_gnn_att_dst")):
                        ld(attb[:, q], A[name].unsqueeze(0).to_broadcast([C, HEADS, C]))
                    ld(W.w2n[:], A["L1_gnn_W2n"])
                    for h in (0, 1):
                        ld(W.w1e[EDIM * h:EDIM * h + EDIM, C * h:C * h + C], A["L1_gnn_W1e"])
                        ld(W.w2e[C * h:C * h + C, C * h:C * h + C], A["L1_gnn_W2e"])
                    for q, name in enumerate(("L0_gnn_ln_gamma", "L0_gnn_ln_beta", "L1_gnn_gamma", "L1_gnn_beta")):
                        ld(W.rows[:, q], A[name].unsqueeze(0).to_broadcast([P, C]))
                    ld(srcE[:], A["src_rows"].rearrange("g p s -> p g s"))
                    ld(dstE[:], A["dst_rows"].rearrange("g p s -> p g s"))
                    ld(dnE[:], A["next_rows"].rearrange("g p s -> p g s"))
                    ld(ewE[:], A["ew_rows"].rearrange("g p s -> p g s"))

                    def load(i, r, g):
                        sp.wait_ge(masks_used, g + 1)
                        for q in (0, 1):
                            at = g * G_ROWS + (1 - q)
                            sp.dma_start(pairrow[:, r, q], linear[:, bass.ds(at, G_ROWS)].to_broadcast([C, G_ROWS])
                                         ).then_inc(masks_in[r], 16)
                    ring_loop(sp, GROUPS, [load])
                    sp.wait_ge(stepped, PREP_STEPS)
                    sp.dma_start(D.final_idx.rearrange("g p s -> p g s"), W.finE[:]).then_inc(fin_st, 16)
                    sp.wait_ge(fin_st, 16)

                @block.gpsimd
                def _(pool):
                    for x in (W.w02, W.w1e, W.w2e, W.gmean, W.w1n, W.l2w, W.l3b, W.l3ab, W.att_half, W.vecs):
                        last = nc.gpsimd.memset(x[:], 0.0)
                    last.then_inc(consts, 1)
                    nc.gpsimd.memset(W.ident[:], 0.0).then_inc(consts, 1)
                    pool.wait_ge(consts, 2)
                    nc.gpsimd.affine_select(out=W.ident[:], in_=W.ident[:], compare_op=ALU.not_equal, fill=1.0,
                                            base=0, pattern=[[-1, P]], channel_multiplier=1).then_inc(consts, 1)

                @block.vector
                def _(dve):
                    dve.sem_inc(masks_used, RING)
                    n = [0]

                    def done(ins):
                        n[0] += 1
                        ins.then_inc(stepped, 1)

                    def wait():
                        dve.wait_ge(stepped, n[0])
                    dve.wait_ge(loaded, 16 * n_loads[0])
                    dve.wait_ge(consts, 1)
                    for h in (0, 1):
                        lanes, out_cols = slice(C * h, C * h + C), slice(C * h, C * h + C)
                        done(nc.vector.tensor_tensor(W.w02[lanes, out_cols], chw[lanes, 0], chw[lanes, 2], ALU.subtract))
                        done(nc.vector.tensor_tensor(W.l3ab[lanes, h], l3a[lanes], W.l3b[lanes, h], ALU.subtract))
                        done(nc.vector.reduce_sum(W.gmean[lanes, out_cols], gw2[lanes].rearrange("k h f -> k f h"), AX_X))
                    for at, slope in ((0, 0.01), (2, 0.1)):
                        for k, f in enumerate((slope, 1.0 - slope)):
                            done(nc.vector.tensor_scalar(W.slanted[:, k, at:at + 2], W.vecs[:, at:at + 2], f, None, ALU.mult))
                    wait()
                    done(nc.vector.tensor_scalar(W.gmean[:], W.gmean[:], 1.0 / HEADS, None, ALU.mult))
                    done(nc.vector.tensor_scalar(W.gatw[:], W.gatw[:], 1.0 / HEADS, None, ALU.mult))
                    done(nc.vector.tensor_scalar(W.w2x2[:], W.w2x2[:], 2.0, None, ALU.mult))
                    for q in (0, 1):
                        done(nc.vector.tensor_tensor(prod[:, q], gw2[0:C], attb[:, q], ALU.mult))
                    wait()
                    for q in (0, 1):
                        done(nc.vector.reduce_sum(W.att[:, q], prod[:, q], AX_X))
                    wait()
                    done(nc.vector.tensor_copy(W.att_half[0:C, 0], W.att[:, 0]))
                    done(nc.vector.tensor_copy(W.att_half[C:P, 1], W.att[:, 0]))
                    done(nc.vector.tensor_tensor(lastE[:], dstE[:], dnE[:], ALU.not_equal))
                    wait()
                    done(nc.vector.tensor_scalar(idx0[:], lastE[:], -NOWHERE, NOWHERE, ALU.mult, ALU.add))
                    wait()
                    done(nc.vector.tensor_tensor(W.finE[:], idx0[:], dstE[:], ALU.add))
                    wait()
                    assert n[0] == PREP_STEPS, n[0]
                    nc.vector.memset(same[:, EP:EP + 1], 0)

                    def mask(i, r, g):
                        dve.wait_ge(masks_in[r], i * 32 + 32)
                        nc.vector.tensor_tensor(same[:, bass.ds(g * G_ROWS, G_ROWS)], pairrow[:, r, 0],
                                                pairrow[:, r, 1], ALU.is_equal).then_inc(masks_used, 1)
                    ring_loop(dve, GROUPS, [mask])
        def phase(part, *args):
            own = []

            def new(name):
                own.append(nc.alloc_semaphore(name=name))
                return own[-1]
            HELD[0] = new("held_" + part.__name__)
            part(nc, A, new, *args)
            nc.clear_and_free_semaphores(own)
            nc.all_engine_barrier()

        W.col, W.ewE, W.wE, W.same = col, ewE, wE, same
        W.cm, W.w02c, W.cm0, W.cm1, W.gamma1 = (sb(n, [P, P]) for n in ("cm", "w02c", "cm0", "cm1", "gamma1"))
        W.b2e_dp = sb("b2e_dp", [P, 1])
        W.base_b, W.base_slanted = sb("base_b", [P, 1]), sb("base_slanted", [P, 2])
        W.ones_row, W.beta_rows = sb("ones_row", [1, P]), sb("beta_rows", [1, 2, P // C * 4, C])
        phase(fold_norms, W, D, bank)
        phase(degrees, W, D, bank, srcE, ewE)
        phase(lone_states, W, D, bank, out)
        phase(first_propagation, W, D, bank)
        phase(second_propagation, W, D, bank)
        phase(attention_sources, W, D, bank)
        phase(attention_weights, W, D, bank)
        phase(attention_sums, W, D, bank)
        phase(gated_messages, W, D, bank)
        phase(relu_messages, W, D, bank)
        stats = sb("bn_stats", [C, 2 * GROUPS * 6])
        phase(edge_convolution, W, D, bank, stats)
        phase(finish_rows, W, D, bank, out, stats)


def degrees(nc, A, sem, W, D, bank, srcE, ewE):
    ctx = ExitStack()
    with ctx:
        t = lambda n, sh, dt=F32: ctx.enter_context(nc.sbuf_tensor(n, sh, dt))
        hiS, loS, rem = (t(n, [P, GROUPS, S]) for n in ("hiS", "loS", "rem"))
        tmpI = t("tmpI", [P, GROUPS, S], I32)
        part = t("part", [P, GROUPS, S])
        vals = t("vals", [P, GROUPS, S, PARTS], BF16)
        iota_i = t("iota_i", [P, LO], I32)
        iota_hi = t("iota_hi", [P, P], BF16)
        iota_lo = t("iota_lo", [P, LO], F16)
        hot_w = t("hot_w", [P, RING, PARTS, P], BF16)
        hot_lo = t("hot_lo", [P, RING, LO], BF16)
        zero = t("zero_bf", [P, P], BF16)
        deg = t("deg", [P, LO])
        msk = t("degmask", [P, LO])
        tab = t("tab", [P, LO, 2])
        root = t("root", [P, LO])
        rows = t("gathered", [P, RING, S, C])
        near = t("near", [P, RING, S], I32)
        (pool_ready, dstep, guarded, hots, products, rooted, table_st) = map(sem, (
            "iotas", "degree_step", "degree_guarded", "onehots_built", "products_done", "degree_rooted", "table_stored"))
        id_in, gin, st = ([sem(f"{n}{r}") for r in range(RING)] for n in
                          ("indices_loaded", "rows_gathered", "rows_stored"))
        N_STEPS = []
        with nc.Block() as block:
            @block.gpsimd
            def _(pool):
                nc.gpsimd.iota(W.posE[:], pattern=[[G_ROWS, GROUPS], [1, S]], base=0, channel_multiplier=S)
                nc.gpsimd.iota(iota_i[:], pattern=[[1, LO]], base=0, channel_multiplier=0)
                nc.gpsimd.memset(zero[:], 0.0).then_inc(pool_ready, 1)

                def gather(i, r, g):
                    hold(pool, id_in[r], i * 16 + 16)
                    hold(pool, st[r], i * 16 + 16)
                    gather_rows(nc, pool, A["x"], near[:, r], rows[:, r], gin[r], NP_ - 1)
                ring_loop(pool, GROUPS, [gather])

            @block.vector
            def _(dve):
                n = [0]

                def done(ins):
                    n[0] += 1
                    ins.then_inc(dstep, 1)

                def wait():
                    dve.wait_ge(dstep, n[0])
                dve.wait_ge(pool_ready, 1)
                done(nc.vector.tensor_copy(iota_hi[:], iota_i[:, 0:P]))
                done(nc.vector.tensor_copy(iota_lo[:], iota_i[:]))
                done(nc.vector.memset(tab[:, :, 1].bitcast(I32), int(NOWHERE)))
                done(nc.vector.tensor_scalar(tmpI[:], srcE, LO_BITS, None, ALU.logical_shift_right))
                wait()
                done(nc.vector.tensor_copy(hiS[:], tmpI[:]))
                wait()
                done(nc.vector.tensor_scalar(tmpI[:], srcE, LO - 1, None, ALU.bitwise_and))
                wait()
                done(nc.vector.tensor_copy(loS[:], tmpI[:]))
                wait()
                done(nc.vector.tensor_copy(rem[:], ewE[:]))
                for k in range(3):
                    wait()
                    done(nc.vector.tensor_copy(vals[:, :, :, k], rem[:]))
                    wait()
                    if k < 2:
                        done(nc.vector.tensor_copy(part[:], vals[:, :, :, k]))
                        wait()
                        done(nc.vector.tensor_tensor(rem[:], rem[:], part[:], ALU.subtract))
                wait()
                hs, ls = (x[:].rearrange("p g s -> p (g s)") for x in (hiS, loS))
                v = vals[:].rearrange("p g s k -> p (g s) k")
                wide = lambda x, k: x.unsqueeze(1).to_broadcast([P, k, P])
                dve.sem_inc(products, RING)

                def hot(i, r, tile):
                    dve.wait_ge(products, tile + 1)
                    one = bass.ds(tile, 1)
                    vt = v[:, one, :].rearrange("p a k -> p (a k)")
                    nc.vector.scalar_tensor_tensor(
                        out=hot_w[:, r], in0=wide(iota_hi[:], 3), scalar=hs[:, one],
                        in1=vt.unsqueeze(2).to_broadcast([P, 3, P]), op0=ALU.is_equal, op1=ALU.mult)
                    nc.vector.tensor_scalar(hot_lo[:, r], iota_lo[:], ls[:, one], None, ALU.is_equal
                                            ).then_inc(hots, 1)
                ring_loop(dve, TILES, [hot])
                dve.wait_ge(products, TILES + RING + 1)
                done(nc.vector.tensor_scalar(msk[:], bank(0, 2), 0.0, None, ALU.is_gt))
                done(nc.vector.tensor_scalar(deg[:], bank(0, 2), 0.0, None, ALU.is_le))
                wait()
                done(nc.vector.tensor_tensor(tab[:, :, 0], msk[:], bank(0, 2), ALU.mult))
                wait()
                nc.vector.tensor_tensor(deg[:], deg[:], tab[:, :, 0], ALU.add).then_inc(guarded, 1)
                dve.wait_ge(rooted, 1)
                done(nc.vector.reciprocal(deg[:], root[:]))
                wait()
                done(nc.vector.tensor_tensor(tab[:, :, 0], deg[:], msk[:], ALU.mult))
                N_STEPS.append(n[0])

            @block.tensor
            def _(pe):
                pe.wait_ge(pool_ready, 1)
                for b in range(2):
                    nc.tensor.matmul(bank(b), zero[0:1, :], zero[0:1, 0:1].to_broadcast([1, 512]), start=True, stop=False)

                def product(i, r, tile):
                    hold(pe, hots, tile + 1)
                    for k in range(3):
                        for h in (0, 1):
                            last = nc.tensor.matmul(bank(h), hot_w[:, r, k], hot_lo[:, r, 512 * h:512 * h + 512],
                                                    start=False, stop=False)
                    last.then_inc(products, 1)
                ring_loop(pe, TILES, [product])
                for b in range(2):
                    last = nc.tensor.matmul(bank(b), zero[0:1, :], zero[0:1, 0:1].to_broadcast([1, 512]), start=False, stop=True)
                last.then_inc(products, 1)

            @block.scalar
            def _(act):
                act.wait_ge(guarded, 1)
                nc.scalar.activation(root[:], deg[:], ACT.Sqrt).then_inc(rooted, 1)

            @block.sync
            def _(sp):
                for r in range(RING):
                    sp.sem_inc(st[r], 16)

                def load(i, r, g):
                    sp.wait_ge(st[r], i * 16 + 16)
                    sp.dma_start(near[:, r], A["src_rows"][g]).then_inc(id_in[r], 16)

                def store(i, r, g):
                    sp.wait_ge(gin[r], (i * 16 + 16) * S)
                    sp.dma_start(group_rows(D.xs)[g], rows[:, r]).then_inc(st[r], 16)
                ring_loop(sp, GROUPS, [load], [], [store])
                for r in range(RING):
                    sp.wait_ge(st[r], 16 * (of_slot(r, GROUPS) + 1))
                sp.wait_ge(dstep, N_STEPS[0])
                sp.dma_start(D.table.rearrange("(h l) c -> h l c", l=LO), tab[0:HI]).then_inc(table_st, 16)
                sp.wait_ge(table_st, 16)


def fold_norms(nc, A, sem, W, D, bank):
    ctx = ExitStack()
    with ctx:
        t = lambda n, sh, dt=F32: ctx.enter_context(nc.sbuf_tensor(n, sh, dt))
        scaled = t("fold_scaled", [P, P])
        step, ready, product, loaded = (sem("fold_" + n) for n in ("step", "ready", "product", "loaded"))
        with nc.Block() as block:
            @block.sync
            def _(sp):
                for q, name in enumerate(("L0_gnn_ln_beta", "L1_gnn_beta")):
                    sp.dma_start(W.beta_rows[:, q], A[name].unsqueeze(0).unsqueeze(1).to_broadcast([1, S, C])
                                 ).then_inc(loaded, 16)
                sp.wait_ge(loaded, 32)

            @block.vector
            def _(dve):
                nc.vector.memset(W.ones_row[:], 1.0)
                nc.vector.memset(W.cm[:], 0.0).then_inc(step, 1)
                dve.wait_ge(step, 1)
                nc.vector.memset(W.cm[0:C, 0:C], -1.0 / C)
                nc.vector.memset(W.cm[C:P, C:P], -1.0 / C).then_inc(step, 1)
                nc.vector.tensor_scalar(scaled[:], W.w02[:], W.col["ln_gamma"], None, ALU.mult).then_inc(step, 1)
                dve.wait_ge(step, 3)
                nc.vector.tensor_tensor(W.cm[:], W.cm[:], W.ident[:], ALU.add).then_inc(step, 1)
                dve.wait_ge(step, 4)
                for q, out, mat in ((0, W.cm0, W.cm), (2, W.cm1, W.cm), (2, W.gamma1, W.ident)):
                    nc.vector.tensor_tensor(out[:].rearrange("p (h c) -> p h c", h=2),
                                            mat[:].rearrange("p (h c) -> p h c", h=2),
                                            W.rows[:, q].unsqueeze(1).to_broadcast([P, 2, C]), ALU.mult)
                nc.vector.tensor_tensor(W.b2e_dp[:], W.col["b2e"], W.col["dp"], ALU.mult)
                dve.sem_inc(ready, 1)
                dve.wait_ge(product, 1)
                nc.vector.tensor_copy(W.w02c[:], bank(0)[:, 0:P])
                nc.vector.tensor_tensor(W.base_b[:], bank(1)[:, 0:1], W.col["cheb_b"], ALU.add).then_inc(step, 1)
                dve.wait_ge(step, 5)
                for k, f in enumerate((0.01, 0.99)):
                    nc.vector.tensor_scalar(W.base_slanted[:, k:k + 1], W.base_b[:], f, None, ALU.mult)

            @block.tensor
            def _(pe):
                pe.wait_ge(ready, 1)
                nc.tensor.matmul(bank(0)[:, 0:P], W.cm[:], scaled[:], start=True, stop=True)
                nc.tensor.matmul(bank(1)[:, 0:1], W.w02[:], W.col["ln_beta"], start=True, stop=True).then_inc(product, 1)


def rows_by(nc, out, paired, weights, beta, W):
    nc.tensor.matmul(out, W.ones_row[:], beta.rearrange("a s c -> a (s c)"), start=True, stop=False)
    for q in range(S // 2):
        last = nc.tensor.matmul(out[:, P * q:P * q + P], paired[:, P * q:P * q + P], weights[:], start=False,
                                stop=q == S // 2 - 1)
    return last


def lone_states(nc, A, sem, W, D, bank, out):
    for name, count, source, dests in (("lone_sources", GROUPS, D.xs, True),
                                       ("lone_nodes", NODE_GROUPS, A["x"], False)):
        lone_run(nc, sem, W, D, bank, out, name, count, source, dests)


def lone_run(nc, sem, W, D, bank, out, name, count, source, dests):
    ctx = ExitStack()
    with ctx:
        t = lambda n, sh, dt=F32: ctx.enter_context(nc.sbuf_tensor(name + n, sh, dt))
        col = W.col
        x, x1, x2 = (t(n, [P, RING, S, C]) for n in ("x", "x1", "x2"))
        if dests:
            tr, hb = (t(n, [P, RING, S, C]) for n in ("tr", "hb"))
        ya, yb = (t(n, [P, S, C]) for n in ("ya", "yb"))
        yaf, ybf = (t(n, [P, HALF]) for n in ("yaf", "ybf"))
        hf, uf = ([t(f"{n}{k}", [P, HALF])[:] for k in (0, 1)] for n in ("hf", "uf"))
        norm_a, norm_b = NormTwice(sem, t, name + "a"), NormTwice(sem, t, name + "b")
        names = ("ya_done", "ya_t", "yaf_done", "base_done", "h_done", "mean_done", "u_done", "u_rows", "x1_done",
                 "yb_done", "yb_t", "ybf_done", "residual", "x2_done", "t_rows", "t_done", "h_rows", "hb_done")
        m = {n: sem(name + n) for n in names}
        x_in, stored = ([sem(f"{name}{n}{r}") for r in range(RING)] for n in ("x_in", "stored"))
        n_st = 4 if dests else 1
        assert dests or count == 2 * GROUPS
        near, tab = t("near", [P, RING, S], I32), t("tab", [P, RING, S, 2])
        ids_done = sem(name + "ids_done")
        landed = [sem(f"{name}tab{r}") for r in range(RING)]
        if not dests:
            tabs, ls = t("tabs", [P, 2 * GROUPS, S, 2]), t("ls", [P, GROUPS, S], I32)
            taken, w_step, ls_stored = (sem(name + n) for n in ("taken", "w_step", "ls_stored"))
        with nc.Block() as block:
            @block.gpsimd
            def _(pool):
                def scatter(i, r, g):
                    hold(pool, ids_done, g + 1)
                    for q in range(S):
                        nc.gpsimd.indirect_dma_start(
                            out=D.table.rearrange("n (c a) -> (n c) a", a=1), out_offset=bass.IndirectOffsetOnAxis(ap=near[:, r, q:q + 1], axis=0),
                            in_=tab[:, r, q, 0:1], in_offset=None, bounds_check=2 * NP_ - 1, oob_is_err=False
                        ).then_inc(landed[r], 16)

                def gather(i, r, g):
                    hold(pool, ids_done, g + 1)
                    gather_rows(nc, pool, D.table, near[:, r], tab[:, r], landed[r], NP_ - 1)
                ring_loop(pool, count, [scatter if dests else gather])
                for r in range(RING):
                    pool.wait_ge(landed[r], 128 * of_slot(r, count))

            @block.sync
            def _(sp):
                for r in range(RING):
                    sp.sem_inc(stored[r], 16 * n_st)

                def load(i, r, g):
                    sp.wait_ge(m["x1_done"], g + 1)
                    sp.dma_start(x[:, r], group_rows(source)[g]).then_inc(x_in[r], 16)

                def store(i, r, g):
                    sp.wait_ge(m["x2_done"], g + 1)
                    if dests:
                        sp.dma_start(group_rows(D.x1_lone)[g], x1[:, r]).then_inc(stored[r], 16)
                        sp.dma_start(group_rows(D.x2_lone)[g], x2[:, r]).then_inc(stored[r], 16)
                        sp.wait_ge(m["t_done"], g + 1)
                        sp.wait_ge(m["hb_done"], g + 1)
                        sp.dma_start(group_rows(D.t0s)[g], tr[:, r]).then_inc(stored[r], 16)
                        sp.dma_start(group_rows(D.h_lone)[g], hb[:, r]).then_inc(stored[r], 16)
                    else:
                        sp.dma_start(group_rows(out)[g], x2[:, r]).then_inc(stored[r], 16)
                ring_loop(sp, count, [load], [], [], [], [], [], [store])
                for r in range(RING):
                    sp.wait_ge(stored[r], 16 * n_st * (of_slot(r, count) + 1))
                if not dests:
                    sp.wait_ge(w_step, 2)
                    sp.dma_start(D.ls.rearrange("g p s -> p g s"), ls[:]).then_inc(ls_stored, 16)
                    sp.wait_ge(ls_stored, 16)

            @block.vector
            def _(dve):
                dve.sem_inc(m["x1_done"], RING)

                def indices(i, r, g):
                    if dests:
                        after(dve, landed[r], i * 128)
                        nc.vector.tensor_scalar(near[:, r], of_group(W.finE, g), 2, 1, ALU.mult, ALU.add)
                        nc.vector.tensor_copy(tab[:, r, :, 0].bitcast(I32), of_group(W.posE, g)).then_inc(ids_done, 1)
                    else:
                        nc.vector.tensor_copy(near[:, r], of_group(W.idsE, g)).then_inc(ids_done, 1)

                def take(i, r, g):
                    dve.wait_ge(landed[r], i * 128 + 128)
                    nc.vector.tensor_copy(tabs[:, bass.ds(g, 1)], tab[:, r].unsqueeze(1)).then_inc(taken, 1)

                def a(i, r, g):
                    dve.wait_ge(x_in[r], i * 16 + 16)
                    yield from norm_a.centre(nc, dve, g, x[:, r], (0, 1))
                    yield from norm_a.scale(nc, dve, g, (8, 9, 10, 11, 13, 14))
                    if not (isinstance(g, int) and g == 0):
                        dve.wait_ge(m["ya_t"], g)
                    nc.vector.tensor_tensor(ya[:], norm_a.y, spread(norm_a.gain), ALU.mult).then_inc(m["ya_done"], 1)

                def b(i, r, g):
                    yield 4
                    dve.wait_ge(stored[r], 16 * n_st * (i + 1))
                    dve.wait_ge(m["u_rows"], g + 1)
                    nc.vector.tensor_tensor(x1[:, r], x[:, r], as_rows(bank(1)), ALU.add).then_inc(m["x1_done"], 1)
                    yield 7
                    dve.wait_ge(m["x1_done"], g + RING + 1)
                    yield from norm_b.centre(nc, dve, g, x1[:, r], (7, 10))

                def scale_b(i, r, g):
                    yield from norm_b.scale(nc, dve, g, (2, 3, 5, 6, 8, 9))
                    after(dve, m["yb_t"], g)
                    nc.vector.tensor_tensor(yb[:], norm_b.y, spread(norm_b.gain), ALU.mult).then_inc(m["yb_done"], 1)

                def c(i, r, g):
                    yield 12
                    dve.wait_ge(m["residual"], g + 1)
                    nc.vector.tensor_tensor(x2[:, r], x1[:, r], as_rows(bank(5)), ALU.add).then_inc(m["x2_done"], 1)
                if dests:
                    ring_loop(dve, count, [a, indices], [], [], [b], [scale_b], [c])
                else:
                    ring_loop(dve, count, [a, indices], [], [], [b, take], [scale_b], [c])
                    dve.wait_ge(taken, count)
                    nc.vector.scalar_tensor_tensor(out=W.wE[:], in0=tabs[:, 0:GROUPS, :, 0], scalar=-1.0,
                                                   in1=tabs[:, GROUPS:, :, 0],
                                                   op0=ALU.mult, op1=ALU.mult).then_inc(w_step, 1)
                    nc.vector.tensor_copy(ls[:], tabs[:, 0:GROUPS, :, 1].bitcast(I32)).then_inc(w_step, 1)
                    dve.wait_ge(w_step, 2)
                    nc.vector.tensor_tensor(W.wE[:], W.wE[:], W.ewE[:], ALU.mult)

            @block.tensor
            def _(pe):
                def base(i, r, g):
                    yield 0
                    hold(pe, m["ya_done"], g + 1)
                    transpose_pairs(nc, bank(0), ya[:], W).then_inc(m["ya_t"], 1)
                    yield 2
                    hold(pe, m["yaf_done"], g + 1)
                    hold(pe, m["h_done"], g)
                    nc.tensor.matmul(bank(2), W.w02c[:], yaf[:], start=True, stop=True).then_inc(m["base_done"], 1)
                    if dests:
                        yield 11
                        hold(pe, m["t_done"], g)
                        rows_by(nc, bank(6), yaf[:], W.cm0, W.beta_rows[:, 0], W).then_inc(m["t_rows"], 1)

                def mean(i, r, g):
                    yield 1
                    hold(pe, m["h_done"], g + 1)
                    for k in (0, 1):
                        last = nc.tensor.matmul(bank(3), W.gmean[:], hf[k], start=k == 0, stop=k == 1)
                    last.then_inc(m["mean_done"], 1)
                    if dests:
                        yield 3
                        hold(pe, m["hb_done"], g)
                        sum_transposed(nc, bank(7), hf, W, S // 2).then_inc(m["h_rows"], 1)
                    yield 8
                    hold(pe, m["u_done"], g + 1)
                    hold(pe, m["x1_done"], g + RING)
                    sum_transposed(nc, bank(1), uf, W, S // 2).then_inc(m["u_rows"], 1)

                def transposed(i, r, g):
                    yield 10
                    hold(pe, m["yb_done"], g + 1)
                    transpose_pairs(nc, bank(4), yb[:], W).then_inc(m["yb_t"], 1)

                def residual(i, r, g):
                    yield 2
                    hold(pe, m["ybf_done"], g + 1)
                    hold(pe, m["x2_done"], g)
                    rows_by(nc, bank(5), ybf[:], W.cm1, W.beta_rows[:, 1], W).then_inc(m["residual"], 1)
                ring_loop(pe, count, [], [base], [mean], [], [transposed], [residual])

            @block.scalar
            def _(act):
                def a(i, r, g):
                    yield from norm_a.square(nc, act, g, (2, 2))
                    yield from norm_a.root(nc, act, g, 12)

                def base(i, r, g):
                    yield 1
                    act.wait_ge(m["ya_t"], g + 1)
                    nc.scalar.activation(yaf[:], bank(0), ACT.Copy).then_inc(m["yaf_done"], 1)
                    yield 8
                    act.wait_ge(m["base_done"], g + 1)
                    if dests:
                        after(act, m["h_rows"], g)
                    leaky_parts(nc, hf, bank(2), 0.01, W.base_slanted[:, 0:1], W.base_slanted[:, 1:2]
                                ).then_inc(m["h_done"], 1)
                    if dests:
                        yield 15
                        act.wait_ge(stored[r], 16 * n_st * (i + 1))
                        act.wait_ge(m["t_rows"], g + 1)
                        nc.scalar.activation(tr[:, r], as_rows(bank(6)), ACT.Copy).then_inc(m["t_done"], 1)

                def mean(i, r, g):
                    yield 7
                    act.wait_ge(m["mean_done"], g + 1)
                    leaky_parts(nc, uf, bank(3), 0.01, col["gat_b_slope"], col["gat_b_rest"]).then_inc(m["u_done"], 1)
                    if dests:
                        yield 9
                        act.wait_ge(m["h_rows"], g + 1)
                        nc.scalar.activation(hb[:, r], as_rows(bank(7)), ACT.Copy).then_inc(m["hb_done"], 1)

                def b(i, r, g):
                    yield from norm_b.square(nc, act, g, (13, 13))

                def residual(i, r, g):
                    yield from norm_b.root(nc, act, g, 7)
                    yield 14
                    act.wait_ge(m["yb_t"], g + 1)
                    nc.scalar.activation(ybf[:], bank(4), ACT.Copy).then_inc(m["ybf_done"], 1)
                ring_loop(act, count, [a], [base], [mean], [b], [residual])


def gather_rows(nc, pool, source, ids, out, landed, limit):
    for q in range(S):
        nc.gpsimd.indirect_dma_start(
            out=out[:, q], out_offset=None, in_=source,
            in_offset=bass.IndirectOffsetOnAxis(ap=ids[:, q:q + 1], axis=0),
            bounds_check=limit, oob_is_err=False).then_inc(landed, 16)


def first_propagation(nc, A, sem, W, D, bank):
    ctx = ExitStack()
    with ctx:
        t = lambda n, sh, dt=F32: ctx.enter_context(nc.sbuf_tensor(n, sh, dt))
        ts, xd, g1 = (t("p1_" + n, [P, RING, S, C]) for n in ("ts", "xd", "g1"))
        near = t("p1_near", [P, RING, S], I32)
        msg, yd = t("p1_msg", [P, S, C]), t("p1_yd", [P, S, C])
        yf = t("p1_yf", [P, 2, HALF])
        sums = t("p1_sums", [C, 2, G_ROWS])
        pd = t("p1_pd", [C, RING, G_ROWS])
        norm = NormTwice(sem, t, "p1_n")
        names = ("msg_done", "yd_done", "msg_t", "yd_t", "yf_done", "pd_mm", "back", "evacuated", "carry")
        m = {n: sem("p1_" + n) for n in names}
        inn, landed, st = ([sem(f"p1_{n}{r}") for r in range(RING)] for n in ("in", "got", "st"))
        with nc.Block() as block:
            @block.sync
            def _(sp):
                for r in range(RING):
                    sp.sem_inc(st[r], 32)

                def load(i, r, g):
                    sp.wait_ge(m["yd_done"], g + 1)
                    sp.dma_start(ts[:, r], group_rows(D.t0s)[g]).then_inc(inn[r], 16)
                    sp.dma_start(near[:, r], A["dst_rows"][g]).then_inc(inn[r], 16)

                def store(i, r, g):
                    sp.wait_ge(m["evacuated"], g * 2 + 2)
                    sp.dma_start(group_cols(D.pd)[g], pd[:, r]).then_inc(st[r], 16)
                    sp.dma_start(group_rows(D.tx1)[g], g1[:, r]).then_inc(st[r], 16)
                ring_loop(sp, GROUPS, [load], [], [], [], [store])
                for r in range(RING):
                    sp.wait_ge(st[r], 32 * (of_slot(r, GROUPS) + 1))

            @block.gpsimd
            def _(pool):
                def gather(i, r, g):
                    hold(pool, inn[r], i * 32 + 32)
                    gather_rows(nc, pool, A["x"], near[:, r], xd[:, r], landed[r], NP_ - 1)
                ring_loop(pool, GROUPS, [gather])

            @block.vector
            def _(dve):
                dve.sem_inc(m["yd_done"], RING)
                nc.vector.memset(sums[:, 1, G_ROWS - 1:G_ROWS], 0.0).then_inc(m["carry"], 1)

                def a(i, r, g):
                    dve.wait_ge(inn[r], i * 32 + 32)
                    dve.wait_ge(landed[r], i * 128 + 128)
                    yield from norm.centre(nc, dve, g, xd[:, r])
                    yield from norm.scale(nc, dve, g)
                    if not (isinstance(g, int) and g == 0):
                        dve.wait_ge(m["yd_t"], g)
                    nc.vector.tensor_tensor(yd[:], norm.y, spread(norm.gain), ALU.mult).then_inc(m["yd_done"], 1)

                def messages(i, r, g):
                    yield 3
                    w = W.wE[:, bass.ds(g, 1)].rearrange("p a s -> p (a s)")
                    if not (isinstance(g, int) and g == 0):
                        dve.wait_ge(m["msg_t"], g)
                    nc.vector.tensor_tensor(msg[:], ts[:, r], spread(w), ALU.mult).then_inc(m["msg_done"], 1)

                def scan(i, r, g):
                    yield 4
                    dve.wait_ge(m["msg_t"], g + 1)
                    if not (isinstance(g, int) and g < 2):
                        dve.wait_ge(m["back"], g - 1)
                    dve.wait_ge(m["carry"], g + 1)
                    run_sums(nc, W, g, r % 2, bank(4, 2)[0:C], sums, m)
                ring_loop(dve, GROUPS, [a, messages], [scan])

            @block.tensor
            def _(pe):
                def b(i, r, g):
                    yield 1
                    hold(pe, m["msg_done"], g + 1)
                    hold(pe, m["carry"], g + 1)
                    transpose_rows(nc, bank(4, 2), msg[:], W).then_inc(m["msg_t"], 1)
                    yield 2
                    hold(pe, m["yd_done"], g + RING + 1)
                    hold(pe, m["yf_done"], g)
                    transpose_pairs(nc, bank(0), yd[:], W).then_inc(m["yd_t"], 1)

                def c(i, r, g):
                    yield 3
                    hold(pe, m["yf_done"], g + 1)
                    hold(pe, m["carry"], g + 2)
                    hold(pe, m["evacuated"], g * 2)
                    for h in (0, 1):
                        part = slice(HALF * h, HALF * h + HALF)
                        nc.tensor.matmul(bank(2, 2)[0:C, part], W.w02c[:, C * h:C * h + C], yf[:, r % 2], start=True,
                                         stop=False)
                        last = nc.tensor.matmul(bank(2, 2)[0:C, part], W.w1[:], sums[:, r % 2, part], start=False,
                                                stop=True)
                    last.then_inc(m["pd_mm"], 1)
                    transpose_back(nc, bank(1), sums[:, r % 2], W).then_inc(m["back"], 1)
                ring_loop(pe, GROUPS, [], [b], [c])

            @block.scalar
            def _(act):
                def a(i, r, g):
                    yield from norm.square(nc, act, g)
                    yield from norm.root(nc, act, g)

                def b(i, r, g):
                    yield 5
                    act.wait_ge(m["yd_t"], g + 1)
                    nc.scalar.activation(yf[:, r % 2], bank(0), ACT.Copy).then_inc(m["yf_done"], 1)

                def c(i, r, g):
                    yield 11
                    act.wait_ge(st[r], i * 32 + 32)
                    act.wait_ge(m["pd_mm"], g + 1)
                    nc.scalar.activation(pd[:, r], bank(2, 2)[0:C], ACT.Identity, bias=W.base_b[0:C]
                                         ).then_inc(m["evacuated"], 1)
                    yield 11
                    act.wait_ge(m["back"], g + 1)
                    nc.scalar.activation(g1[:, r], as_rows(bank(1)), ACT.Copy).then_inc(m["evacuated"], 1)
                ring_loop(act, GROUPS, [a], [b], [c])


def run_sums(nc, W, g, par, messages, sums, m):
    return nc.vector.tensor_tensor_scan(
        sums[:, par], W.same[:, bass.ds(g * G_ROWS, G_ROWS)], messages, sums[:, 1 - par, G_ROWS - 1:G_ROWS],
        ALU.mult, ALU.add).then_inc(m["carry"], 1)


def second_propagation(nc, A, sem, W, D, bank):
    ctx = ExitStack()
    with ctx:
        t = lambda n, sh, dt=F32: ctx.enter_context(nc.sbuf_tensor(n, sh, dt))
        near = t("p2_near", [P, RING, S], I32)
        got, hr = (t("p2_" + n, [P, RING, S, C]) for n in ("got", "hr"))
        msg = t("p2_msg", [P, 2, S, C])
        sums, hf = t("p2_sums", [C, 2, G_ROWS]), t("p2_hf", [C, 2, G_ROWS])
        pd, pre = t("p2_pd", [C, 2, G_ROWS]), t("p2_pre", [C, G_ROWS])
        att = t("p2_att", [2 * HEADS, RING, G_ROWS])
        names = ("msg_done", "zeroed", "msg_t", "carry", "mm", "pre_done", "h_done", "back", "att_mm", "evacuated",
                 "pd_in0", "pd_in1")
        m = {n: sem("p2_" + n) for n in names}
        pd_in = (m["pd_in0"], m["pd_in1"])
        inn, landed, st = ([sem(f"p2_{n}{r}") for r in range(RING)] for n in ("in", "got", "st"))
        with nc.Block() as block:
            @block.sync
            def _(sp):
                for r in range(RING):
                    sp.sem_inc(st[r], 32)

                def load(i, r, g):
                    sp.wait_ge(m["msg_done"], g + 1)
                    sp.dma_start(near[:, r], D.ls[g]).then_inc(inn[r], 16)

                def load_later(i, r, g):
                    sp.wait_ge(m["pre_done"], g + 1)
                    sp.dma_start(pd[:, r % 2], group_cols(D.pd)[g]).then_inc(pd_in[r % 2], 16)

                def store(i, r, g):
                    sp.wait_ge(m["evacuated"], g * 2 + 2)
                    sp.dma_start(group_rows(D.hd)[g], hr[:, r]).then_inc(st[r], 16)
                    sp.dma_start(group_cols(D.att_d)[g], att[:, r]).then_inc(st[r], 16)
                ring_loop(sp, GROUPS, [load], [], [load_later], [], [], [store])
                for r in range(RING):
                    sp.wait_ge(st[r], 32 * (of_slot(r, GROUPS) + 1))

            @block.gpsimd
            def _(pool):
                def gather(i, r, g):
                    hold(pool, inn[r], i * 16 + 16)
                    hold(pool, m["zeroed"], g + 1)
                    gather_rows(nc, pool, D.tx1, near[:, r], got[:, r], landed[r], EP - 1)
                ring_loop(pool, GROUPS, [gather])

            @block.vector
            def _(dve):
                dve.sem_inc(m["msg_done"], RING)
                dve.sem_inc(m["pre_done"], 2)
                for r in range(RING):
                    nc.vector.memset(got[:, r], 0.0).then_inc(m["zeroed"], 1)
                nc.vector.memset(sums[:, 1, G_ROWS - 1:G_ROWS], 0.0).then_inc(m["carry"], 1)

                def messages(i, r, g):
                    yield 4
                    dve.wait_ge(landed[r], i * 128 + 128)
                    if not (isinstance(g, int) and g < 2):
                        dve.wait_ge(m["msg_t"], g - 1)
                    w = W.wE[:, bass.ds(g, 1)].rearrange("p a s -> p (a s)")
                    nc.vector.tensor_tensor(msg[:, r % 2], got[:, r], spread(w), ALU.mult).then_inc(m["msg_done"], 1)
                    yield 5
                    dve.wait_ge(m["msg_done"], g + RING + 1)
                    nc.vector.memset(got[:, r], 0.0).then_inc(m["zeroed"], 1)

                def scan(i, r, g):
                    yield 1
                    dve.wait_ge(m["msg_t"], g + 1)
                    if not (isinstance(g, int) and g < 2):
                        dve.wait_ge(m["mm"], g - 1)
                    dve.wait_ge(m["carry"], g + 1)
                    run_sums(nc, W, g, r % 2, bank(4, 2)[0:C], sums, m)

                def h(i, r, g):
                    yield 2
                    dve.wait_ge(m["mm"], g + 1)
                    after(dve, m["h_done"], g)
                    dve.wait_ge(pd_in[r % 2], half_turns(i, r) * 16 + 16)
                    nc.vector.tensor_tensor(pre[:], bank(2, 2)[0:C], pd[:, r % 2], ALU.add).then_inc(m["pre_done"], 1)
                    yield 3
                    dve.wait_ge(m["pre_done"], g + 3)
                    if not (isinstance(g, int) and g < 2):
                        dve.wait_ge(m["att_mm"], g - 1)
                    nc.vector.scalar_tensor_tensor(out=hf[:, r % 2], in0=pre[:], scalar=0.01, in1=pre[:], op0=ALU.mult,
                                                   op1=ALU.max).then_inc(m["h_done"], 1)
                ring_loop(dve, GROUPS, [messages], [scan], [h])

            @block.tensor
            def _(pe):
                def b(i, r, g):
                    yield 0
                    hold(pe, m["msg_done"], g + RING + 1)
                    hold(pe, m["carry"], g + 1)
                    transpose_rows(nc, bank(4, 2), msg[:, r % 2], W).then_inc(m["msg_t"], 1)

                def c(i, r, g):
                    yield 1
                    hold(pe, m["carry"], g + 2)
                    hold(pe, m["pre_done"], g + 2)
                    for h in (0, 1):
                        part = slice(HALF * h, HALF * h + HALF)
                        last = nc.tensor.matmul(bank(2, 2)[0:C, part], W.w2x2[:], sums[:, r % 2, part], start=True,
                                                stop=True)
                    last.then_inc(m["mm"], 1)

                def d(i, r, g):
                    yield 2
                    hold(pe, m["h_done"], g + 1)
                    hold(pe, m["evacuated"], g * 2)
                    transpose_back(nc, bank(1), hf[:, r % 2], W).then_inc(m["back"], 1)
                    for h in (0, 1):
                        part = slice(HALF * h, HALF * h + HALF)
                        last = nc.tensor.matmul(bank(6, 2)[0:2 * HEADS, part], W.att[:].rearrange("k q h -> k (q h)"),
                                                hf[:, r % 2, part], start=True, stop=True)
                    last.then_inc(m["att_mm"], 1)
                ring_loop(pe, GROUPS, [], [b], [c], [d])

            @block.scalar
            def _(act):
                def d(i, r, g):
                    act.wait_ge(st[r], i * 32 + 32)
                    act.wait_ge(m["back"], g + 1)
                    nc.scalar.activation(hr[:, r], as_rows(bank(1)), ACT.Copy).then_inc(m["evacuated"], 1)
                    act.wait_ge(m["att_mm"], g + 1)
                    nc.scalar.activation(att[:, r], bank(6, 2)[0:2 * HEADS], ACT.Copy).then_inc(m["evacuated"], 1)
                ring_loop(act, GROUPS, [], [], [], [d])


def attention_sources(nc, A, sem, W, D, bank):
    ctx = ExitStack()
    with ctx:
        t = lambda n, sh, dt=F32: ctx.enter_context(nc.sbuf_tensor(n, sh, dt))
        near = t("p3_near", [P, RING, S], I32)
        got = t("p3_got", [P, RING, S, C])
        hf = t("p3_hf", [P, 2, HALF])
        att = t("p3_att", [HEADS, RING, G_ROWS])
        ea = t("et_ea", [2 * EDIM, RING, HALF])
        hid = t("et_hid", [P, 2, HALF])
        et = t("et_out", [P, RING, HALF])
        col = W.col
        m = {n: sem("p3_" + n) for n in ("got_t", "hf_done", "mm", "att_done", "et_mm1", "et_pre", "et_hid", "et_mm2",
                                         "et_done")}
        inn, ea_in, landed, st, et_st = ([sem(f"p3_{n}{r}") for r in range(RING)] for n in
                                         ("in", "ea_in", "got", "st", "et_st"))
        with nc.Block() as block:
            @block.sync
            def _(sp):
                for r in range(RING):
                    sp.sem_inc(st[r], 32)
                    sp.sem_inc(et_st[r], 32)

                def load(i, r, g):
                    sp.wait_ge(m["att_done"], g + 1)
                    sp.wait_ge(st[r], i * 32 + 32)
                    sp.dma_start(near[:, r], D.ls[g]).then_inc(inn[r], 16)
                    sp.dma_start(got[:, r], group_rows(D.h_lone)[g]).then_inc(inn[r], 16)
                    sp.wait_ge(m["et_done"], g + 1)
                    sp.dma_start(ea[:, r], pairs(A["ea_pairs"])[g]).then_inc(ea_in[r], 16)

                def store(i, r, g):
                    sp.wait_ge(landed[r], i * 128 + 128)
                    sp.dma_start(group_rows(D.hs)[g], got[:, r]).then_inc(st[r], 16)
                    sp.wait_ge(m["att_done"], g + RING + 1)
                    sp.dma_start(group_cols(D.att_s)[g], att[:, r]).then_inc(st[r], 16)

                def store_factors(i, r, g):
                    sp.wait_ge(m["et_done"], g + RING + 1)
                    for h in (0, 1):
                        sp.dma_start(group_cols(D.et)[g, :, HALF * h:HALF * h + HALF], et[C * h:C * h + C, r]
                                     ).then_inc(et_st[r], 16)
                ring_loop(sp, GROUPS, [load], [], [store], [], [store_factors])
                for r in range(RING):
                    sp.wait_ge(st[r], 32 * (of_slot(r, GROUPS) + 1))
                    sp.wait_ge(et_st[r], 32 * (of_slot(r, GROUPS) + 1))

            @block.gpsimd
            def _(pool):
                def gather(i, r, g):
                    hold(pool, inn[r], i * 32 + 32)
                    gather_rows(nc, pool, D.hd, near[:, r], got[:, r], landed[r], EP - 1)
                ring_loop(pool, GROUPS, [gather])

            @block.tensor
            def _(pe):
                def work(i, r, g):
                    yield 5
                    hold(pe, landed[r], i * 128 + 128)
                    if not (isinstance(g, int) and g == 0):
                        hold(pe, m["hf_done"], g)
                    transpose_pairs(nc, bank(0), got[:, r], W).then_inc(m["got_t"], 1)
                    hold(pe, m["hf_done"], g + 1)
                    hold(pe, m["att_done"], g + RING)
                    halves(nc, bank(2, 2)[0:HEADS], W.att_half, hf[:, r % 2]).then_inc(m["mm"], 1)

                def hidden(i, r, g):
                    hold(pe, ea_in[r], i * 16 + 16)
                    hold(pe, m["et_pre"], g)
                    nc.tensor.matmul(bank(4), W.w1e[:], ea[:, r], start=True, stop=True).then_inc(m["et_mm1"], 1)

                def factors(i, r, g):
                    hold(pe, m["et_hid"], g + 1)
                    hold(pe, m["et_done"], g + RING)
                    nc.tensor.matmul(bank(5), W.w2e[:], hid[:, r % 2], start=True, stop=True).then_inc(m["et_mm2"], 1)
                ring_loop(pe, GROUPS, [work, hidden], [], [factors])

            @block.vector
            def _(dve):
                def leaky(i, r, g):
                    dve.wait_ge(m["et_pre"], g + 1)
                    h = hid[:, r % 2]
                    nc.vector.scalar_tensor_tensor(out=h, in0=h, scalar=0.1, in1=h, op0=ALU.mult, op1=ALU.max
                                                   ).then_inc(m["et_hid"], 1)
                ring_loop(dve, GROUPS, [leaky])

            @block.scalar
            def _(act):
                act.sem_inc(m["att_done"], RING)
                act.sem_inc(m["et_done"], RING)

                def work(i, r, g):
                    yield 5
                    act.wait_ge(m["got_t"], g + 1)
                    nc.scalar.activation(hf[:, r % 2], bank(0), ACT.Copy).then_inc(m["hf_done"], 1)
                    act.wait_ge(st[r], i * 32 + 32)
                    act.wait_ge(m["mm"], g + 1)
                    nc.scalar.activation(att[:, r], bank(2, 2)[0:HEADS], ACT.Copy).then_inc(m["att_done"], 1)

                def hidden(i, r, g):
                    act.wait_ge(m["et_mm1"], g + 1)
                    after(act, m["et_mm2"], g - 1)
                    nc.scalar.activation(hid[:, r % 2], bank(4), ACT.Identity, bias=col["b1e"]).then_inc(m["et_pre"], 1)

                def factors(i, r, g):
                    act.wait_ge(et_st[r], i * 32 + 32)
                    act.wait_ge(m["et_mm2"], g + 1)
                    nc.scalar.activation(et[:, r], bank(5), ACT.Identity, bias=W.b2e_dp[:], scale=col["dp"]
                                         ).then_inc(m["et_done"], 1)
                ring_loop(act, GROUPS, [work], [hidden], [factors])


def attention_weights(nc, A, sem, W, D, bank):
    ctx = ExitStack()
    with ctx:
        t = lambda n, sh, dt=F32: ctx.enter_context(nc.sbuf_tensor(n, sh, dt))
        ids = t("sm_ids", [P, 3, CHUNK], I32)
        as_, ex = (t("sm_" + n, [P, HEADS, CHUNK]) for n in ("as", "ex"))
        sums = t("sm_sums", [P, HEADS + 1, CHUNK])
        big = sums[:, 0:HEADS]
        ad, back = (t("sm_" + n, [P, 2 * HEADS, CHUNK]) for n in ("ad", "back"))
        prev, nxt, last, fm, rm, gate, zero, ones = (t("sm_" + n, [P, CHUNK]) for n in
                                                     ("prev", "next", "last", "fm", "rm", "gate", "zero", "ones"))
        ends = t("sm_ends", [P, 2, 2 * HEADS])
        rows = t("sm_rows", [2 * HEADS, 2, P + 2])
        carry = t("sm_carry", [P, 2 * HEADS])
        m = {n: sem("sm_" + n) for n in ("in", "step", "ends_t", "carry_t", "ex_ready", "ex_done", "exs_ready", "exs_done", "ready", "stored")}
        rev = lambda a: a[:, ::-1]
        ADD, MAX, MUL = ALU.add, ALU.max, ALU.mult
        PLAN = []
        with nc.Block() as block:
            @block.sync
            def _(sp):
                line = A["dst_line"]
                for k, off in enumerate((0, 1, 2)):
                    sp.dma_start(ids[:, k], line[:, off:off + EP].rearrange("a (p e) -> (a p) e", p=P)).then_inc(m["in"], 16)
                sp.dma_start(as_[:], D.att_s.rearrange("h (p e) -> p h e", p=P)).then_inc(m["in"], 16)
                sp.dma_start(ad[:], D.att_d.rearrange("h (p e) -> p h e", p=P)).then_inc(m["in"], 16)
                sp.wait_ge(m["ready"], 1)
                out = D.alpha.rearrange("h (p e) -> p h e", p=P)
                sp.dma_start(out[:, 0:HEADS], ex[:]).then_inc(m["stored"], 16)
                sp.dma_start(out[:, HEADS:2 * HEADS], as_[:]).then_inc(m["stored"], 16)
                sp.dma_start(out[:, 2 * HEADS:], sums[:, HEADS:]).then_inc(m["stored"], 16)
                sp.wait_ge(m["stored"], 48)

            @block.tensor
            def _(pe):
                for n, k in enumerate(EXCHANGES):
                    pe.wait_ge(m["ex_ready"], 2 * n + 1)
                    for q in (0, 1):
                        last = nc.tensor.transpose(bank(q)[0:k, 0:P], ends[:, q, 0:k], W.ident[:])
                    last.then_inc(m["ends_t"], 1)
                    pe.wait_ge(m["ex_ready"], 2 * n + 2)
                    nc.tensor.transpose(bank(2)[:, 0:k], rows[0:k, 1, 1:P + 1], W.ident[0:k, 0:k]).then_inc(m["carry_t"], 1)

            @block.scalar
            def _(act):
                act.wait_ge(m["exs_ready"], 1)
                nc.scalar.activation(ex[:], ex[:], ACT.Exp)
                nc.scalar.activation(ad[:, 0:HEADS], ad[:, 0:HEADS], ACT.Exp).then_inc(m["exs_done"], 1)

            @block.vector
            def _(dve):
                n, x = [0], [0]

                def done(ins):
                    n[0] += 1
                    ins.then_inc(m["step"], 1)

                def wait():
                    dve.wait_ge(m["step"], n[0])

                def exchange(k, values, flag, combine, start, backward):
                    for h in range(k):
                        done(nc.vector.tensor_copy(ends[:, 1, h:h + 1], flag))
                        done(nc.vector.tensor_copy(ends[:, 0, h:h + 1], values(h)))
                    wait()
                    dve.sem_inc(m["ex_ready"], 1)
                    x[0] += 1
                    dve.wait_ge(m["ends_t"], x[0])
                    if combine == MAX:
                        done(nc.vector.tensor_scalar(rows[0:k, 0, 0:P], bank(1)[0:k, 0:P], -1.0, FAR, ADD, MUL))
                    else:
                        done(nc.vector.tensor_copy(rows[0:k, 0, 0:P], bank(1)[0:k, 0:P]))
                    at = slice(0, P) if backward else slice(2, P + 2)
                    done(nc.vector.memset(rows[0:k, 1], start))
                    wait()
                    order = rev if backward else (lambda a: a)
                    done(nc.vector.tensor_tensor_scan(order(rows[0:k, 1, at]), order(rows[0:k, 0, 0:P]),
                                                      order(bank(0)[0:k, 0:P]), start,
                                                      ADD if combine == MAX else MUL, combine))
                    wait()
                    dve.sem_inc(m["ex_ready"], 1)
                    dve.wait_ge(m["carry_t"], x[0])
                    done(nc.vector.tensor_copy(carry[:, 0:k], bank(2)[:, 0:k]))
                    wait()

                def spread_back(k, values):
                    done(nc.vector.tensor_tensor(back[:, 0:k], values, last[:].unsqueeze(1).to_broadcast([P, k, CHUNK]), MUL))
                    wait()
                    for h in range(k):
                        done(nc.vector.tensor_tensor_scan(rev(back[:, h]), rev(nxt[:]), rev(back[:, h]), 0.0, MUL, ADD))
                    wait()
                    exchange(k, lambda h: back[:, h, 0:1], rm[:, 0:1], ADD, 0.0, True)
                    for h in range(k):
                        done(nc.vector.scalar_tensor_tensor(out=back[:, h], in0=rm[:], scalar=carry[:, h:h + 1],
                                                            in1=back[:, h], op0=MUL, op1=ADD))
                    wait()

                dve.wait_ge(m["in"], 80)
                done(nc.vector.tensor_tensor(prev[:], ids[:, 0], ids[:, 1], ALU.is_equal))
                done(nc.vector.tensor_tensor(nxt[:], ids[:, 1], ids[:, 2], ALU.is_equal))
                done(nc.vector.tensor_tensor(last[:], ids[:, 1], ids[:, 2], ALU.not_equal))
                done(nc.vector.memset(zero[:], 0.0))
                done(nc.vector.memset(ones[:], 1.0))
                wait()
                done(nc.vector.tensor_tensor_scan(fm[:], prev[:], zero[:], 1.0, MUL, ADD))
                done(nc.vector.tensor_tensor_scan(rev(rm[:]), rev(nxt[:]), zero[:], 1.0, MUL, ADD))
                done(nc.vector.tensor_scalar(gate[:], prev[:], -1.0, FAR, ADD, MUL))
                wait()
                for h in range(HEADS):
                    done(nc.vector.tensor_tensor_scan(big[:, h], gate[:], as_[:, h], -FAR, ADD, MAX))
                wait()
                exchange(HEADS, lambda h: big[:, h, CHUNK - 1:CHUNK], fm[:, CHUNK - 1:CHUNK], MAX, -FAR, False)
                done(nc.vector.tensor_scalar(gate[:], fm[:], -1.0, FAR, ADD, MUL))
                wait()
                for h in range(HEADS):
                    done(nc.vector.scalar_tensor_tensor(out=big[:, h], in0=gate[:], scalar=carry[:, h:h + 1],
                                                        in1=big[:, h], op0=ADD, op1=MAX))
                wait()
                done(nc.vector.tensor_tensor(big, big, ad[:, 0:HEADS], MAX))
                wait()
                done(nc.vector.tensor_tensor(big, big, ad[:, HEADS:], ADD))
                done(nc.vector.tensor_tensor(ad[:, 0:HEADS], ad[:, 0:HEADS], ad[:, HEADS:], ADD))
                wait()
                done(nc.vector.scalar_tensor_tensor(out=big, in0=big, scalar=0.2, in1=big, op0=MUL, op1=MAX))
                done(nc.vector.scalar_tensor_tensor(out=ad[:, 0:HEADS], in0=ad[:, 0:HEADS], scalar=0.2,
                                                    in1=ad[:, 0:HEADS], op0=MUL, op1=MAX))
                wait()
                done(nc.vector.tensor_tensor(ad[:, 0:HEADS], ad[:, 0:HEADS], big, ALU.subtract))
                spread_back(HEADS, ad[:, HEADS:])
                done(nc.vector.tensor_tensor(ex[:], as_[:], back[:, 0:HEADS], ADD))
                wait()
                done(nc.vector.scalar_tensor_tensor(out=ex[:], in0=ex[:], scalar=0.2, in1=ex[:], op0=MUL, op1=MAX))
                wait()
                spread_back(HEADS, big)
                done(nc.vector.tensor_tensor(ex[:], ex[:], back[:, 0:HEADS], ALU.subtract))
                done(nc.vector.tensor_scalar(ad[:, 0:HEADS], ad[:, 0:HEADS], 0.0, None, ALU.min))
                wait()
                dve.sem_inc(m["exs_ready"], 1)
                dve.wait_ge(m["exs_done"], 1)
                for h in range(HEADS):
                    done(nc.vector.tensor_tensor_scan(sums[:, h], prev[:], ex[:, h], 0.0, MUL, ADD))
                done(nc.vector.tensor_tensor_scan(sums[:, HEADS], prev[:], ones[:], 0.0, MUL, ADD))
                wait()
                exchange(HEADS + 1, lambda h: sums[:, h, CHUNK - 1:CHUNK], fm[:, CHUNK - 1:CHUNK], ADD, 0.0, False)
                for h in range(HEADS + 1):
                    done(nc.vector.scalar_tensor_tensor(out=sums[:, h], in0=fm[:], scalar=carry[:, h:h + 1],
                                                        in1=sums[:, h], op0=MUL, op1=ADD))
                wait()
                done(nc.vector.scalar_tensor_tensor(out=big, in0=big, scalar=1e-16, in1=ad[:, 0:HEADS], op0=ADD, op1=ADD))
                wait()
                done(nc.vector.reciprocal(big, big))
                wait()
                done(nc.vector.tensor_tensor(as_[:], ad[:, 0:HEADS], big, MUL))
                spread_back(HEADS, big)
                done(nc.vector.tensor_tensor(ex[:], ex[:], back[:, 0:HEADS], MUL))
                done(nc.vector.tensor_tensor(as_[:], as_[:], last[:].unsqueeze(1).to_broadcast([P, HEADS, CHUNK]), MUL))
                wait()
                dve.sem_inc(m["ready"], 1)
                assert x[0] == len(EXCHANGES)


def attention_sums(nc, A, sem, W, D, bank):
    ctx = ExitStack()
    with ctx:
        t = lambda n, sh, dt=F32: ctx.enter_context(nc.sbuf_tensor(n, sh, dt))
        col = W.col
        hs, hd = (t("at_" + n, [P, 2, S, C]) for n in ("hs", "hd"))
        xd, x1 = t("at_xd", [P, RING, S, C]), t("at_x1", [P, 2, S, C])
        near = t("at_near", [P, RING, S], I32)
        alpha = t("at_alpha", [ALPHAS, 2, G_ROWS])
        al = t("at_al", [P, 2, S, ALPHAS])
        wide, own = t("at_wide", [P, 2, S, HEADS, C]), t("at_own", [P, S, HEADS, C])
        pf = t("at_pf", [P, 2, 2, HALF])
        sums = t("at_sums", [C, 2, G_ROWS])
        parts = [t(f"at_u{k}", [C, G_ROWS])[:] for k in (0, 1)]
        names = ("al_t", "al_done", "wide_step", "wide_t", "pf_done", "mm", "carry", "u_done", "back", "x1_done")
        m = {n: sem("at_" + n) for n in names}
        inn, st = ([sem(f"at_{n}{k}") for k in (0, 1)] for n in ("in", "st"))
        near_in, landed = ([sem(f"at_{n}{r}") for r in range(RING)] for n in ("near_in", "got"))
        with nc.Block() as block:
            @block.sync
            def _(sp):
                for k in (0, 1):
                    sp.sem_inc(st[k], 16)

                def load(i, r, g):
                    sp.wait_ge(m["wide_step"], g * 3 + 2)
                    for b, d in ((hs, D.hs), (hd, D.hd)):
                        sp.dma_start(b[:, r % 2], group_rows(d)[g]).then_inc(inn[r % 2], 16)
                    sp.dma_start(alpha[:, r % 2], group_cols(D.alpha)[g]).then_inc(inn[r % 2], 16)

                def load_x(i, r, g):
                    sp.wait_ge(m["x1_done"], g + 1)
                    sp.dma_start(near[:, r], A["dst_rows"][g]).then_inc(near_in[r], 16)

                def store(i, r, g):
                    sp.wait_ge(m["x1_done"], g + RING + 1)
                    sp.dma_start(group_rows(D.x1d)[g], x1[:, r % 2]).then_inc(st[r % 2], 16)
                ring_loop(sp, GROUPS, [load], [], [load_x], [], [], [], [store])
                for k in (0, 1):
                    sp.wait_ge(st[k], ODD_EVEN[k] + 16)

            @block.gpsimd
            def _(pool):
                def gather(i, r, g):
                    hold(pool, near_in[r], i * 16 + 16)
                    gather_rows(nc, pool, A["x"], near[:, r], xd[:, r], landed[r], NP_ - 1)
                ring_loop(pool, GROUPS, [gather])

            @block.vector
            def _(dve):
                dve.sem_inc(m["wide_step"], 6)
                dve.sem_inc(m["x1_done"], RING)
                nc.vector.memset(sums[:, 1, G_ROWS - 1:G_ROWS], 0.0).then_inc(m["carry"], 1)

                def a(i, r, g):
                    yield 1
                    dve.wait_ge(inn[r % 2], half_turns(i, r) * 48 + 48)
                    dve.wait_ge(m["al_done"], g + 1)
                    after(dve, m["wide_t"], g * 2 - 2)
                    by = lambda x: x.unsqueeze(2).to_broadcast([P, S, HEADS, C])
                    wt = lambda k: al[:, r % 2, :, HEADS * k:HEADS * k + HEADS].unsqueeze(3).to_broadcast([P, S, HEADS, C])
                    nc.vector.tensor_copy(W.countE[:, bass.ds(g, 1)], al[:, r % 2, :, 2 * HEADS].unsqueeze(1))
                    nc.vector.tensor_tensor(wide[:, r % 2], by(hs[:, r % 2]), wt(0), ALU.mult).then_inc(m["wide_step"], 1)
                    yield 3
                    dve.wait_ge(m["wide_step"], g * 3 + 6)
                    nc.vector.tensor_tensor(own[:], by(hd[:, r % 2]), wt(1), ALU.mult).then_inc(m["wide_step"], 1)
                    yield 7
                    dve.wait_ge(m["wide_step"], g * 3 + 8)
                    nc.vector.tensor_tensor(wide[:, r % 2], wide[:, r % 2], own[:], ALU.add).then_inc(m["wide_step"], 1)

                def scan(i, r, g):
                    yield 2
                    dve.wait_ge(m["mm"], g + 1)
                    dve.wait_ge(m["carry"], g + 1)
                    after(dve, m["u_done"], g - 1)
                    run_sums(nc, W, g, r % 2, bank(4, 2)[0:C], sums, m)

                def x(i, r, g):
                    yield 4
                    dve.wait_ge(landed[r], i * 128 + 128)
                    dve.wait_ge(st[r % 2], half_turns(i, r) * 16 + 16)
                    dve.wait_ge(m["back"], g + 1)
                    nc.vector.tensor_tensor(x1[:, r % 2], xd[:, r], as_rows(bank(1)), ALU.add).then_inc(m["x1_done"], 1)
                ring_loop(dve, GROUPS, [], [a], [], [scan], [x])

            @block.tensor
            def _(pe):
                def a(i, r, g):
                    yield 1
                    hold(pe, inn[r % 2], half_turns(i, r) * 48 + 48)
                    hold(pe, m["al_done"], g)
                    for n in range(S):
                        last = nc.tensor.transpose(bank(0)[:, ALPHAS * n:ALPHAS * (n + 1)],
                                                   alpha[:, r % 2, slot_cols(n)], W.ident[0:ALPHAS, 0:ALPHAS])
                    last.then_inc(m["al_t"], 1)

                def b(i, r, g):
                    yield 0
                    hold(pe, m["wide_step"], g * 3 + 9)
                    hold(pe, m["pf_done"], g * 2)
                    for h in (0, 1):
                        for j in range(S // 2):
                            for q in (0, 1):
                                last = nc.tensor.transpose(bank((2, 6)[h] + q)[:, P * j:P * j + P],
                                                           wide[:, r % 2, 2 * j + h, 2 * q:2 * q + 2].rearrange("p h c -> p (h c)"),
                                                           W.ident[:])
                        last.then_inc(m["wide_t"], 1)
                    yield 3
                    hold(pe, m["carry"], g + 1)
                    for h in (0, 1):
                        hold(pe, m["pf_done"], g * 2 + h + 1)
                        for q in (0, 1):
                            last = nc.tensor.matmul(bank(4, 2)[0:C, HALF * h:HALF * h + HALF], W.gatw[:, q],
                                                    pf[:, h, q], start=q == 0, stop=q == 1)
                    last.then_inc(m["mm"], 1)

                def d(i, r, g):
                    yield 2
                    hold(pe, m["u_done"], g + 1)
                    hold(pe, m["x1_done"], g + RING)
                    sum_transposed(nc, bank(1), parts, W, S).then_inc(m["back"], 1)
                ring_loop(pe, GROUPS, [a], [], [b], [], [d])

            @block.scalar
            def _(act):
                def a(i, r, g):
                    yield 4
                    after(act, m["wide_step"], g * 3 + 2)
                    act.wait_ge(m["al_t"], g + 1)
                    nc.scalar.activation(al[:, r % 2], bank(0)[:, 0:ALPHAS * S].rearrange("p (s h) -> p s h", s=S),
                                         ACT.Copy).then_inc(m["al_done"], 1)

                def b(i, r, g):
                    for h in (0, 1):
                        yield 1
                        act.wait_ge(m["wide_t"], g * 2 + h + 1)
                        after(act, m["mm"], g)
                        nc.scalar.activation(pf[:, h], bank((2, 6)[h], 2).rearrange("p (q n) -> p q n", q=2), ACT.Copy
                                             ).then_inc(m["pf_done"], 1)

                def c(i, r, g):
                    yield 5
                    act.wait_ge(m["carry"], g + 2)
                    after(act, m["back"], g)
                    leaky_parts(nc, parts, sums[:, r % 2], 0.01, col["gat_b_slope"][0:C], col["gat_b_rest"][0:C]
                                ).then_inc(m["u_done"], 1)
                ring_loop(act, GROUPS, [a], [], [b], [c])


def gated_messages(nc, A, sem, W, D, bank):
    ctx = ExitStack()
    with ctx:
        t = lambda n, sh, dt=F32: ctx.enter_context(nc.sbuf_tensor(n, sh, dt))
        col = W.col
        near = t("l1_near", [P, RING, S], I32)
        got, xd = (t("l1_" + n, [P, RING, S, C]) for n in ("got", "xd"))
        x2 = t("l1_x2", [P, 2, S, C])
        hn, hd, o1, xn = (t("l1_" + n, [P, S, C]) for n in ("hn", "hd", "o1", "xn"))
        et, sums = t("l1_et", [C, 2, G_ROWS]), t("l1_sums", [C, 2, G_ROWS])
        msg = t("l1_msg", [C, G_ROWS])
        hf, xf = t("l1_hf", [P, HALF]), t("l1_xf", [P, HALF])
        hid = [t(f"l1_hid{k}", [P, G_ROWS])[:] for k in (0, 1)]
        norm_s, norm_d, norm_o = (Norm(sem, t, "l1_" + n) for n in ("s", "d", "o"))
        names = ("hn_done", "hn_t", "hf_done", "mm1", "hid_done", "mm2", "msg_done", "carry", "back", "hd_done",
                 "o1_done", "xn_done", "xn_t", "xf_done", "residual", "x2_done")
        m = {n: sem("l1_" + n) for n in names}
        inn, landed, x_in = ([sem(f"l1_{n}{r}") for r in range(RING)] for n in ("in", "got", "x_in"))
        et_in, st = ([sem(f"l1_{n}{k}") for k in (0, 1)] for n in ("et_in", "st"))
        with nc.Block() as block:
            @block.sync
            def _(sp):
                for k in (0, 1):
                    sp.sem_inc(st[k], 16)

                def load(i, r, g):
                    sp.wait_ge(m["hn_done"], g + 1)
                    sp.dma_start(near[:, r], D.ls[g]).then_inc(inn[r], 16)
                    sp.dma_start(got[:, r], group_rows(D.x1_lone)[g]).then_inc(inn[r], 16)

                def load_et(i, r, g):
                    sp.wait_ge(m["msg_done"], g + 1)
                    sp.dma_start(et[:, r % 2], group_cols(D.et)[g]).then_inc(et_in[r % 2], 16)

                def load_x(i, r, g):
                    sp.wait_ge(m["x2_done"], g + 1)
                    sp.dma_start(xd[:, r], group_rows(D.x1d)[g]).then_inc(x_in[r], 16)

                def store(i, r, g):
                    sp.wait_ge(m["x2_done"], g + RING + 1)
                    sp.dma_start(group_rows(D.x2d)[g], x2[:, r % 2]).then_inc(st[r % 2], 16)
                ring_loop(sp, GROUPS, [load], [], [], [load_et], [load_x], [], [], [], [store])
                for k in (0, 1):
                    sp.wait_ge(st[k], ODD_EVEN[k] + 16)

            @block.gpsimd
            def _(pool):
                def gather(i, r, g):
                    hold(pool, inn[r], i * 32 + 32)
                    gather_rows(nc, pool, D.x1d, near[:, r], got[:, r], landed[r], EP - 1)
                ring_loop(pool, GROUPS, [gather])

            @block.vector
            def _(dve):
                dve.sem_inc(m["hn_done"], RING)
                dve.sem_inc(m["msg_done"], 2)
                dve.sem_inc(m["x2_done"], RING)
                nc.vector.memset(sums[:, 1, G_ROWS - 1:G_ROWS], 0.0).then_inc(m["carry"], 1)

                def sources(i, r, g):
                    dve.wait_ge(landed[r], i * 128 + 128)
                    yield from norm_s.dve(nc, dve, g, 0, got[:, r])
                    after(dve, m["hn_t"], g)
                    nc.vector.scalar_tensor_tensor(out=hn[:], in0=norm_s.xc, scalar=0.0, in1=spread(norm_s.rstd),
                                                   op0=ALU.max, op1=ALU.mult).then_inc(m["hn_done"], 1)

                def sums_of(i, r, g):
                    yield 3
                    dve.wait_ge(et_in[r % 2], half_turns(i, r) * 16 + 16)
                    dve.wait_ge(m["mm2"], g + 1)
                    nc.vector.scalar_tensor_tensor(out=msg[:], in0=bank(4, 2)[0:C], scalar=col["b2n"][0:C],
                                                   in1=et[:, r % 2], op0=ALU.add, op1=ALU.mult).then_inc(m["msg_done"], 1)
                    yield 6
                    dve.wait_ge(m["msg_done"], g + 3)
                    dve.wait_ge(m["carry"], g + 1)
                    after(dve, m["back"], g - 1)
                    run_sums(nc, W, g, r % 2, msg[:], sums, m)

                def dests(i, r, g):
                    dve.wait_ge(x_in[r], i * 16 + 16)
                    yield from norm_d.dve(nc, dve, g, 0, xd[:, r])
                    nc.vector.scalar_tensor_tensor(out=hd[:], in0=norm_d.xc, scalar=0.0, in1=spread(norm_d.rstd),
                                                   op0=ALU.max, op1=ALU.mult).then_inc(m["hd_done"], 1)
                    yield 9
                    dve.wait_ge(m["hd_done"], g + 1)
                    dve.wait_ge(m["back"], g + 1)
                    nc.vector.scalar_tensor_tensor(out=o1[:], in0=as_rows(bank(1)), scalar=col["res"], in1=hd[:],
                                                   op0=ALU.mult, op1=ALU.add).then_inc(m["o1_done"], 1)

                def normed(i, r, g):
                    yield 0
                    dve.wait_ge(m["o1_done"], g + 1)
                    yield from norm_o.dve(nc, dve, g, 0, o1[:])
                    after(dve, m["xn_t"], g)
                    nc.vector.tensor_tensor(xn[:], norm_o.xc, spread(norm_o.rstd), ALU.mult).then_inc(m["xn_done"], 1)

                def result(i, r, g):
                    yield 10
                    dve.wait_ge(st[r % 2], half_turns(i, r) * 16 + 16)
                    dve.wait_ge(m["residual"], g + 1)
                    nc.vector.tensor_tensor(x2[:, r % 2], xd[:, r], as_rows(bank(6)), ALU.add
                                            ).then_inc(m["x2_done"], 1)
                ring_loop(dve, GROUPS, [sources], [], [sums_of], [dests], [normed], [result])

            @block.tensor
            def _(pe):
                def b(i, r, g):
                    yield 0
                    hold(pe, m["hn_done"], g + RING + 1)
                    transpose_pairs(nc, bank(0), hn[:], W).then_inc(m["hn_t"], 1)
                    yield 2
                    hold(pe, m["hf_done"], g + 1)
                    hold(pe, m["hid_done"], g)
                    halves(nc, bank(2, 2), W.w1n, hf[:]).then_inc(m["mm1"], 1)
                    yield 6
                    hold(pe, m["hid_done"], g + 1)
                    hold(pe, m["msg_done"], g + 2)
                    for h in (0, 1):
                        part = slice(HALF * h, HALF * h + HALF)
                        for k in (0, 1):
                            last = nc.tensor.matmul(bank(4, 2)[0:C, part], W.w2n[:], hid[k][:, part],
                                                    start=k == 0, stop=k == 1)
                    last.then_inc(m["mm2"], 1)

                def back(i, r, g):
                    yield 1
                    hold(pe, m["carry"], g + 2)
                    hold(pe, m["o1_done"], g)
                    transpose_back(nc, bank(1), sums[:, r % 2], W).then_inc(m["back"], 1)

                def residual(i, r, g):
                    yield 1
                    hold(pe, m["xn_done"], g + 1)
                    transpose_pairs(nc, bank(7), xn[:], W).then_inc(m["xn_t"], 1)
                    yield 4
                    hold(pe, m["xf_done"], g + 1)
                    hold(pe, m["x2_done"], g + RING)
                    rows_by(nc, bank(6), xf[:], W.gamma1, W.beta_rows[:, 1], W).then_inc(m["residual"], 1)
                ring_loop(pe, GROUPS, [], [b], [], [back], [], [residual])

            @block.scalar
            def _(act):
                def sources(i, r, g):
                    yield from norm_s.act(nc, act, g, 0)

                def b(i, r, g):
                    yield 1
                    act.wait_ge(m["hn_t"], g + 1)
                    nc.scalar.activation(hf[:], bank(0), ACT.Copy).then_inc(m["hf_done"], 1)
                    yield 5
                    act.wait_ge(m["mm1"], g + 1)
                    leaky_parts(nc, hid, bank(2, 2), 0.1, col["b1n_slope"], col["b1n_rest"]).then_inc(m["hid_done"], 1)

                def dests(i, r, g):
                    yield from norm_d.act(nc, act, g, 0)

                def normed(i, r, g):
                    yield from norm_o.act(nc, act, g, 0)

                def residual(i, r, g):
                    yield 2
                    act.wait_ge(m["xn_t"], g + 1)
                    nc.scalar.activation(xf[:], bank(7), ACT.Copy).then_inc(m["xf_done"], 1)
                ring_loop(act, GROUPS, [sources], [b], [], [dests], [normed], [residual])


def relu_messages(nc, A, sem, W, D, bank):
    ctx = ExitStack()
    with ctx:
        t = lambda n, sh, dt=F32: ctx.enter_context(nc.sbuf_tensor(n, sh, dt))
        col = W.col
        near = t("l2_near", [P, RING, S], I32)
        got = t("l2_got", [P, RING, S, C])
        xd, x3 = (t("l2_" + n, [P, 2, S, C]) for n in ("xd", "x3"))
        hn = t("l2_hn", [P, S, C])
        msg, sums = t("l2_msg", [C, 2, G_ROWS]), t("l2_sums", [C, 2, G_ROWS])
        hf = t("l2_hf", [P, HALF])
        norm = Norm(sem, t, "l2_n")
        names = ("hn_done", "hn_t", "hf_done", "mm", "msg_done", "carry", "back", "x3_done")
        m = {n: sem("l2_" + n) for n in names}
        inn, landed = ([sem(f"l2_{n}{r}") for r in range(RING)] for n in ("in", "got"))
        x_in, st = ([sem(f"l2_{n}{k}") for k in (0, 1)] for n in ("x_in", "st"))
        with nc.Block() as block:
            @block.sync
            def _(sp):
                for k in (0, 1):
                    sp.sem_inc(st[k], 16)

                def load(i, r, g):
                    sp.wait_ge(m["hn_done"], g + 1)
                    sp.dma_start(near[:, r], D.ls[g]).then_inc(inn[r], 16)
                    sp.dma_start(got[:, r], group_rows(D.x2_lone)[g]).then_inc(inn[r], 16)

                def load_x(i, r, g):
                    sp.wait_ge(m["x3_done"], g + 1)
                    sp.dma_start(xd[:, r % 2], group_rows(D.x2d)[g]).then_inc(x_in[r % 2], 16)

                def store(i, r, g):
                    sp.wait_ge(m["x3_done"], g + 3)
                    sp.dma_start(group_rows(D.x3d)[g], x3[:, r % 2]).then_inc(st[r % 2], 16)
                ring_loop(sp, GROUPS, [load], [], [], [], [load_x], [], [store])
                for k in (0, 1):
                    sp.wait_ge(st[k], ODD_EVEN[k] + 16)

            @block.gpsimd
            def _(pool):
                def gather(i, r, g):
                    hold(pool, inn[r], i * 32 + 32)
                    gather_rows(nc, pool, D.x2d, near[:, r], got[:, r], landed[r], EP - 1)
                ring_loop(pool, GROUPS, [gather])

            @block.vector
            def _(dve):
                dve.sem_inc(m["hn_done"], RING)
                dve.sem_inc(m["x3_done"], 2)
                nc.vector.memset(sums[:, 1, G_ROWS - 1:G_ROWS], 0.0).then_inc(m["carry"], 1)

                def sources(i, r, g):
                    dve.wait_ge(landed[r], i * 128 + 128)
                    yield from norm.dve(nc, dve, g, 0, got[:, r])
                    after(dve, m["hn_t"], g)
                    nc.vector.scalar_tensor_tensor(out=hn[:], in0=norm.xc, scalar=0.0, in1=spread(norm.rstd),
                                                   op0=ALU.max, op1=ALU.mult).then_inc(m["hn_done"], 1)

                def scan(i, r, g):
                    yield 3
                    dve.wait_ge(m["msg_done"], g + 1)
                    dve.wait_ge(m["carry"], g + 1)
                    after(dve, m["back"], g - 1)
                    run_sums(nc, W, g, r % 2, msg[:, r % 2], sums, m)

                def result(i, r, g):
                    yield 6
                    dve.wait_ge(x_in[r % 2], half_turns(i, r) * 16 + 16)
                    dve.wait_ge(st[r % 2], half_turns(i, r) * 16 + 16)
                    dve.wait_ge(m["back"], g + 1)
                    nc.vector.tensor_tensor(x3[:, r % 2], xd[:, r % 2], as_rows(bank(1)), ALU.add).then_inc(m["x3_done"], 1)
                ring_loop(dve, GROUPS, [sources], [], [scan], [result])

            @block.tensor
            def _(pe):
                def b(i, r, g):
                    yield 0
                    hold(pe, m["hn_done"], g + RING + 1)
                    transpose_pairs(nc, bank(0), hn[:], W).then_inc(m["hn_t"], 1)
                    yield 2
                    hold(pe, m["hf_done"], g + 1)
                    hold(pe, m["msg_done"], g)
                    halves(nc, bank(2, 2)[0:C], W.l2w, hf[:]).then_inc(m["mm"], 1)

                def back(i, r, g):
                    yield 3
                    hold(pe, m["carry"], g + 2)
                    hold(pe, m["x3_done"], g + 2)
                    transpose_back(nc, bank(1), sums[:, r % 2], W).then_inc(m["back"], 1)
                ring_loop(pe, GROUPS, [], [b], [], [back])

            @block.scalar
            def _(act):
                def sources(i, r, g):
                    yield from norm.act(nc, act, g, 0)

                def b(i, r, g):
                    yield 1
                    act.wait_ge(m["hn_t"], g + 1)
                    nc.scalar.activation(hf[:], bank(0), ACT.Copy).then_inc(m["hf_done"], 1)
                    yield 5
                    after(act, m["carry"], g)
                    act.wait_ge(m["mm"], g + 1)
                    nc.scalar.activation(msg[:, r % 2], bank(2, 2)[0:C], ACT.Relu, bias=col["l2b"][0:C]
                                         ).then_inc(m["msg_done"], 1)
                ring_loop(act, GROUPS, [sources], [b])


def edge_convolution(nc, A, sem, W, D, bank, stats):
    ctx = ExitStack()
    with ctx:
        t = lambda n, sh, dt=F32: ctx.enter_context(nc.sbuf_tensor(n, sh, dt))
        col = W.col
        near = t("l3_near", [P, RING, S], I32)
        got, xd = (t("l3_" + n, [P, RING, S, C]) for n in ("got", "xd"))
        hn, dn = (t("l3_" + n, [P, S, C]) for n in ("hn", "dn"))
        neg, hh = (t("l3_" + n, [C, 2, G_ROWS]) for n in ("neg", "hh"))
        ended = t("l3_ended", [C, 2, G_ROWS])
        nxt = t("l3_nxt", [C, 2, G_ROWS], U8)
        hf, df = (t("l3_" + n, [P, 2, HALF]) for n in ("hf", "df"))
        norm_s, norm_d = Norm(sem, t, "l3_s"), Norm(sem, t, "l3_d")
        names = ("hn_done", "hn_t", "hf_done", "mm", "ended", "carry", "hh_done", "stats", "nxt_done")
        m = {n: sem("l3_" + n) for n in names}
        inn, landed = ([sem(f"l3_{n}{r}") for r in range(RING)] for n in ("in", "got"))
        st = [sem(f"l3_st{k}") for k in (0, 1)]
        back = lambda g: g * -1 + (GROUPS - 1)
        with nc.Block() as block:
            @block.sync
            def _(sp):
                for k in (0, 1):
                    sp.sem_inc(st[k], 16)

                def load(i, r, g):
                    sp.wait_ge(m["hn_done"], g + 1)
                    sp.dma_start(near[:, r], D.ls[back(g)]).then_inc(inn[r], 16)
                    sp.dma_start(got[:, r], group_rows(D.x2_lone)[back(g)]).then_inc(inn[r], 16)
                    sp.dma_start(xd[:, r], group_rows(D.x3d)[back(g)]).then_inc(inn[r], 16)

                def store(i, r, g):
                    sp.wait_ge(m["hh_done"], g + 1)
                    sp.dma_start(group_cols(D.hh)[back(g)], hh[:, r % 2]).then_inc(st[r % 2], 16)
                ring_loop(sp, GROUPS, [load], [], [], [], [], [store])
                for k in (0, 1):
                    sp.wait_ge(st[k], ODD_EVEN[k] + 16)

            @block.gpsimd
            def _(pool):
                def gather(i, r, g):
                    hold(pool, inn[r], i * 48 + 48)
                    gather_rows(nc, pool, D.x3d, near[:, r], got[:, r], landed[r], EP - 1)
                ring_loop(pool, GROUPS, [gather])

            @block.vector
            def _(dve):
                dve.sem_inc(m["hn_done"], RING)
                nc.vector.memset(neg[:, 1, 0:1], 0.0).then_inc(m["carry"], 1)

                def dests(i, r, g):
                    dve.wait_ge(inn[r], i * 48 + 48)
                    yield from norm_d.dve(nc, dve, g, 0, xd[:, r])
                    after(dve, m["hn_t"], g)
                    nc.vector.scalar_tensor_tensor(out=dn[:], in0=norm_d.xc, scalar=0.0, in1=spread(norm_d.rstd),
                                                   op0=ALU.max, op1=ALU.mult)

                def sources(i, r, g):
                    dve.wait_ge(landed[r], i * 128 + 128)
                    yield from norm_s.dve(nc, dve, g, 0, got[:, r])
                    after(dve, m["hn_t"], g)
                    nc.vector.scalar_tensor_tensor(out=hn[:], in0=norm_s.xc, scalar=0.0, in1=spread(norm_s.rstd),
                                                   op0=ALU.max, op1=ALU.mult).then_inc(m["hn_done"], 1)

                def c(i, r, g):
                    yield 1
                    dve.wait_ge(m["nxt_done"], g + 1)
                    dve.wait_ge(m["mm"], g + 1)
                    nc.vector.scalar_tensor_tensor(out=ended[:, r % 2], in0=nxt[:, r % 2], scalar=-1.0,
                                                   in1=bank(2, 2)[0:C], op0=ALU.add, op1=ALU.mult).then_inc(m["ended"], 1)

                def scan(i, r, g):
                    yield 3
                    dve.wait_ge(m["ended"], g + 1)
                    dve.wait_ge(m["carry"], g + 1)
                    nc.vector.tensor_tensor_scan(neg[:, r % 2, ::-1], nxt[:, r % 2, ::-1], ended[:, r % 2, ::-1],
                                                 neg[:, 1 - r % 2, 0:1], ALU.mult, ALU.add).then_inc(m["carry"], 1)
                    yield 6
                    dve.wait_ge(m["carry"], g + 2)
                    dve.wait_ge(st[r % 2], half_turns(i, r) * 16 + 16)
                    nc.vector.scalar_tensor_tensor(out=hh[:, r % 2], in0=bank(4 + 2 * (r % 2), 2)[0:C],
                                                   scalar=col["l3b"][0:C], in1=neg[:, r % 2], op0=ALU.add,
                                                   op1=ALU.subtract).then_inc(m["hh_done"], 1)
                    yield 8
                    dve.wait_ge(m["hh_done"], g + 1)
                    for h in (0, 1):
                        at = bass.ds(back(g) * 12 + 6 * h, 6)
                        nc.vector.bn_stats(stats[:, at], hh[:, r % 2, HALF * h:HALF * h + HALF]).then_inc(m["stats"], 1)
                ring_loop(dve, GROUPS, [dests, sources], [], [], [c, scan])
                dve.wait_ge(m["stats"], 2 * GROUPS)

            @block.tensor
            def _(pe):
                def b(i, r, g):
                    yield 0
                    hold(pe, m["hn_done"], g + RING + 1)
                    hold(pe, m["hf_done"], g)
                    transpose_pairs(nc, bank(1), dn[:], W)
                    transpose_pairs(nc, bank(0), hn[:], W).then_inc(m["hn_t"], 1)

                def c(i, r, g):
                    yield 1
                    hold(pe, m["hf_done"], g + 1)
                    hold(pe, m["ended"], g)
                    hold(pe, m["hh_done"], g - 1)
                    halves(nc, bank(2, 2)[0:C], W.l3ab, df[:, r % 2])
                    halves(nc, bank(4 + 2 * (r % 2), 2)[0:C], W.l3b, hf[:, r % 2]).then_inc(m["mm"], 1)
                ring_loop(pe, GROUPS, [], [b], [c])

            @block.scalar
            def _(act):
                def norms(i, r, g):
                    yield from norm_d.act(nc, act, g, 0)

                def norms_s(i, r, g):
                    yield from norm_s.act(nc, act, g, 0)

                def b(i, r, g):
                    yield 2
                    act.wait_ge(m["hn_t"], g + 1)
                    after(act, m["mm"], g - 1)
                    nc.scalar.activation(df[:, r % 2], bank(1), ACT.Copy)
                    nc.scalar.activation(hf[:, r % 2], bank(0), ACT.Copy).then_inc(m["hf_done"], 1)
                    yield 5
                    after(act, m["carry"], g)
                    nc.scalar.activation(nxt[:, r % 2], W.same[:, bass.ds(back(g) * G_ROWS + 1, G_ROWS)], ACT.Copy
                                         ).then_inc(m["nxt_done"], 1)
                ring_loop(act, GROUPS, [norms, norms_s], [b])


def finish_rows(nc, A, sem, W, D, bank, out, stats):
    ctx = ExitStack()
    with ctx:
        t = lambda n, sh, dt=F32: ctx.enter_context(nc.sbuf_tensor(n, sh, dt))
        col = W.col
        near = t("fi_near", [P, RING, S], I32)
        res = t("fi_res", [P, RING, S, C])
        xd = t("fi_xd", [P, 2, S, C])
        avg = t("fi_avg", [P, S, C])
        hh, z, sums = (t("fi_" + n, [C, 2, G_ROWS]) for n in ("hh", "z", "sums"))
        msg = t("fi_msg", [C, G_ROWS])
        inv = t("fi_inv", [P, GROUPS, S])
        tail_n = EDGES % HALF
        tail = t("fi_tail", [C, tail_n])
        mv, sc = t("fi_mv", [C, 2]), t("fi_sc", [C, 4])
        names = ("tail", "bn_step", "root", "z_done", "msg_done", "carry", "avg_done", "back", "res_done", "freed")
        m = {n: sem("fi_" + n) for n in names}
        ids_in, st = ([sem(f"fi_{n}{r}") for r in range(RING)] for n in ("ids", "st"))
        hh_in, x_in = ([sem(f"fi_{n}{k}") for k in (0, 1)] for n in ("hh_in", "x_in"))
        with nc.Block() as block:
            @block.sync
            def _(sp):
                sp.dma_start(tail[:], D.hh[:, EDGES - tail_n:EDGES]).then_inc(m["tail"], 16)

                def load(i, r, g):
                    sp.wait_ge(m["z_done"], g + 1)
                    sp.dma_start(hh[:, r % 2], group_cols(D.hh)[g]).then_inc(hh_in[r % 2], 16)

                def load_x(i, r, g):
                    sp.wait_ge(m["res_done"], g + 1)
                    sp.dma_start(xd[:, r % 2], group_rows(D.x3d)[g]).then_inc(x_in[r % 2], 16)
                    sp.wait_ge(m["freed"], g + 1)
                    sp.dma_start(near[:, r], D.final_idx[g]).then_inc(ids_in[r], 16)
                ring_loop(sp, GROUPS, [load], [], [load_x])

            @block.gpsimd
            def _(pool):
                pool.sem_inc(m["freed"], RING)

                def scatter(i, r, g):
                    hold(pool, ids_in[r], i * 16 + 16)
                    hold(pool, m["res_done"], g + 3)
                    for q in range(S):
                        nc.gpsimd.indirect_dma_start(
                            out=out, out_offset=bass.IndirectOffsetOnAxis(ap=near[:, r, q:q + 1], axis=0),
                            in_=res[:, r, q], in_offset=None, bounds_check=NP_ - 1, oob_is_err=False
                        ).then_inc(st[r], 16)

                def free(i, r, g):
                    hold(pool, st[r], i * 128 + 128)
                    pool.sem_inc(m["freed"], 1)
                ring_loop(pool, GROUPS, [scatter], [free])

            @block.vector
            def _(dve):
                n = [0]

                def done(ins):
                    n[0] += 1
                    ins.then_inc(m["bn_step"], 1)

                def wait():
                    dve.wait_ge(m["bn_step"], n[0])
                dve.sem_inc(m["res_done"], 2)
                done(nc.vector.reciprocal(inv[:], W.countE[:]))
                done(nc.vector.memset(sums[:, 1, G_ROWS - 1:G_ROWS], 0.0))
                dve.wait_ge(m["tail"], 16)
                at = 6 * ((EDGES - tail_n) // HALF)
                done(nc.vector.bn_stats(stats[:, at:at + 6], tail[:]))
                wait()
                done(nc.vector.bn_aggr(mv[:], stats[:, 0:at + 6]))
                wait()
                done(nc.vector.tensor_scalar(sc[:, 0:1], mv[:, 1:2], EPS, None, ALU.add))
                dve.wait_ge(m["root"], 1)
                done(nc.vector.reciprocal(sc[:, 0:1], sc[:, 1:2]))
                wait()
                done(nc.vector.tensor_tensor(sc[:, 2:3], sc[:, 0:1], col["bn_gamma"][0:C], ALU.mult))
                wait()
                done(nc.vector.tensor_tensor(sc[:, 3:4], mv[:, 0:1], sc[:, 2:3], ALU.mult))
                wait()
                done(nc.vector.tensor_tensor(sc[:, 3:4], col["bn_beta"][0:C], sc[:, 3:4], ALU.subtract))
                wait()
                dve.sem_inc(m["carry"], 1)
                assert n[0] == BN_STEPS

                def a(i, r, g):
                    dve.wait_ge(m["z_done"], g + 3)
                    after(dve, m["carry"], g + 1)
                    nc.vector.scalar_tensor_tensor(out=msg[:], in0=z[:, r % 2], scalar=0.3, in1=z[:, r % 2], op0=ALU.mult,
                                                   op1=ALU.max).then_inc(m["msg_done"], 1)
                    yield 2
                    dve.wait_ge(m["msg_done"], g + 1)
                    dve.wait_ge(m["carry"], g + 1)
                    after(dve, m["back"], g - 1)
                    run_sums(nc, W, g, r % 2, msg[:], sums, m)

                def b(i, r, g):
                    yield 1
                    dve.wait_ge(m["back"], g + 1)
                    dve.wait_ge(m["res_done"], g + 2)
                    nc.vector.tensor_tensor(avg[:], as_rows(bank(1)),
                                            spread(inv[:, bass.ds(g, 1)].rearrange("p a s -> p (a s)")), ALU.mult
                                            ).then_inc(m["avg_done"], 1)
                    yield 3
                    dve.wait_ge(x_in[r % 2], half_turns(i, r) * 16 + 16)
                    dve.wait_ge(m["freed"], g + 1)
                    dve.wait_ge(m["avg_done"], g + 1)
                    nc.vector.tensor_tensor(res[:, r], xd[:, r % 2], avg[:], ALU.add).then_inc(m["res_done"], 1)
                ring_loop(dve, GROUPS, [a], [b])

            @block.tensor
            def _(pe):
                def work(i, r, g):
                    hold(pe, m["carry"], g + 2)
                    hold(pe, m["avg_done"], g)
                    transpose_back(nc, bank(1), sums[:, r % 2], W).then_inc(m["back"], 1)
                ring_loop(pe, GROUPS, [work])

            @block.scalar
            def _(act):
                act.wait_ge(m["bn_step"], 5)
                nc.scalar.activation(sc[:, 1:2], sc[:, 0:1], ACT.Sqrt).then_inc(m["root"], 1)
                act.wait_ge(m["bn_step"], BN_STEPS)
                act.sem_inc(m["z_done"], 2)

                def work(i, r, g):
                    act.wait_ge(hh_in[r % 2], half_turns(i, r) * 16 + 16)
                    after(act, m["msg_done"], g - 1)
                    nc.scalar.activation(z[:, r % 2], hh[:, r % 2], ACT.Identity, bias=sc[:, 3:4], scale=sc[:, 2:3]
                                         ).then_inc(m["z_done"], 1)
                ring_loop(act, GROUPS, [work])


def lay_out(inputs):
    import numpy as np
    a = {k: np.ascontiguousarray(v) for k, v in inputs.items()}
    src, dst = a.pop("src").astype(np.int32), a.pop("dst").astype(np.int32)
    ew, ea, x = a.pop("edge_weight"), a.pop("edge_attr_32"), a.pop("x")

    def padded(v, fill):
        return np.concatenate([v, np.full((EP - EDGES,) + v.shape[1:], fill, v.dtype)])

    def rows(v):
        return np.ascontiguousarray(v.reshape(GROUPS, 2, S // 2, P).transpose(0, 3, 2, 1).reshape(GROUPS, P, S))

    end = np.array([-2], np.int32)
    dp = padded(dst, NODES)
    a["src_rows"], a["dst_rows"] = rows(padded(src, 0)), rows(dp)
    a["next_rows"] = rows(np.concatenate([dp[1:], end]))
    a["ew_rows"] = rows(padded(ew, 0))
    a["dst_line"] = np.concatenate([end, dp, end])[None]
    a["ea_pairs"] = np.ascontiguousarray(padded(ea, 0).reshape(GROUPS, 2, HALF, EDIM).transpose(1, 3, 0, 2)
                                         .reshape(2 * EDIM, EP // 2))
    a["x"] = np.concatenate([x, np.zeros((NP_ - NODES, C), x.dtype)])
    a["l3_wt"] = np.ascontiguousarray(a.pop("L3_gnn_W").T)
    return a


def kernel(**inputs):
    import concourse.bacc as bacc
    from concourse.bass_utils import run_bass_kernel_spmd
    arrays = lay_out(inputs)
    nc = bacc.Bacc("TRN2", target_bir_lowering=False, num_devices=1)
    args = {n: nc.dram_tensor("in_" + n, v.shape, mybir.dt.from_np(v.dtype), kind="ExternalInput").ap()
            for n, v in arrays.items()}
    out = nc.dram_tensor("out_0", (NP_, C), F32, kind="ExternalOutput").ap()
    build(nc, args, out)
    r = run_bass_kernel_spmd(nc, [{"in_" + n: v for n, v in arrays.items()}], core_ids=[0])
    return r.results[0]["out_0"][:NODES]
```
